# Optimizing a Trainium2 kernel written in Bass

```python
import numpy as np
import jax
import jax.numpy as jnp

def _softmax(x, axis=-1):
    return jax.nn.softmax(x, axis=axis)

def _gelu(x):
    return jax.nn.gelu(x, approximate=True)

def _silu(x):
    return jax.nn.silu(x)

def _sigmoid(x):
    return jax.nn.sigmoid(x)

def _layernorm(x, axis=-1, eps=1e-05):
    m = jnp.mean(x, axis=axis, keepdims=True)
    v = jnp.var(x, axis=axis, keepdims=True)
    return (x - m) / jnp.sqrt(v + eps)

def _scatter_add(tgt, idx, src, axis=0):
    return tgt.at[idx].add(src)

def _segment_sum(src, seg, n):
    return jax.ops.segment_sum(src, seg, n)
kernel_name = 'mk_decoder_preln_d2_seqx_r8_ba5279'

def setup_inputs(seed: int=0):
    np.random.seed(seed)
    _w = jnp.asarray

    def _rec_inputs():
        import jax
        import jax.numpy as jnp
        _rk = jax.random.key(seed)
        x = 7.22e-05 + 1 * jax.random.normal(jax.random.fold_in(_rk, 1), (64, 64, 256), jnp.float32)
        _lenS = 64 - jax.random.randint(jax.random.fold_in(_rk, 7), (64,), 0, max(1, 64 // 4) + 1, jnp.int32)
        _lenS2 = 64 - jax.random.randint(jax.random.fold_in(_rk, 8), (64,), 0, max(1, 64 // 4) + 1, jnp.int32)
        _ctx_2048P = jax.random.normal(jax.random.fold_in(_rk, 11), (64, 16, 256), jnp.float32)
        _ctx_2048c = jax.random.dirichlet(jax.random.fold_in(_rk, 511), 0.3 * jnp.ones((16,), jnp.float32), (64, 64))
        _ctx_2048t = jnp.einsum('bsk,bkd->bsd', _ctx_2048c, _ctx_2048P)
        _ctx_2048t = _ctx_2048t * jax.lax.rsqrt(jnp.mean(jnp.square(_ctx_2048t)) + 1e-12) * 0.953939
        ctx_2048 = 4.13588e-05 + 0.999923 * (_ctx_2048t + 0.3 * jax.random.normal(jax.random.fold_in(_rk, 611), (64, 64, 256), jnp.float32))
        return (x, ctx_2048)
    x, ctx_2048 = _rec_inputs()

    def _L0_attn_setup():
        import jax, jax.numpy as jnp
        import numpy as np
        B, S, HID = (2, 256, 256)
        H, HKV, D = (16, 4, 128)
        ROPE_BASE = 1000000.0
        EPS = 1e-05

        def _layernorm(x, g, b):
            mu = jnp.mean(x, axis=-1, keepdims=True)
            var = jnp.mean(jnp.square(x - mu), axis=-1, keepdims=True)
            return (x - mu) * jax.lax.rsqrt(var + EPS) * g + b

        def _rope_tables(seq_len, dim, base):
            inv_freq = 1.0 / base ** (jnp.arange(0, dim, 2, dtype=jnp.float32) / dim)
            t = jnp.arange(seq_len, dtype=jnp.float32)
            freqs = jnp.outer(t, inv_freq)
            cos = jnp.concatenate([jnp.cos(freqs), jnp.cos(freqs)], axis=-1)
            sin = jnp.concatenate([jnp.sin(freqs), jnp.sin(freqs)], axis=-1)
            return (cos, sin)

        def _rotate_half(x):
            x1, x2 = jnp.split(x, 2, axis=-1)
            return jnp.concatenate([-x2, x1], axis=-1)
        key = jax.random.key(seed)
        k1, k2, k3 = jax.random.split(key, 3)
        return {'x': jax.random.normal(k1, (B, S, HID), dtype=jnp.float32), 'w_qkv': jax.random.normal(k2, ((H + 2 * HKV) * D, HID), dtype=jnp.float32) * 0.02, 'w_o': jax.random.normal(k3, (HID, H * D), dtype=jnp.float32) * 0.02, 'qn_g': jnp.ones((D,), jnp.float32), 'qn_b': jnp.zeros((D,), jnp.float32), 'kn_g': jnp.ones((D,), jnp.float32), 'kn_b': jnp.zeros((D,), jnp.float32)}
    _L0_attn_all = _L0_attn_setup()
    _L0_attn_in = {k: v for k, v in _L0_attn_all.items() if k in ('w_qkv', 'w_o', 'qn_g', 'qn_b', 'kn_g', 'kn_b')}
    del _L0_attn_all

    def _L0_xattn_setup():
        import jax, jax.numpy as jnp
        import numpy as np
        N_HEAD = 8
        key = jax.random.key(seed)
        k1, k2, k3 = jax.random.split(key, 3)
        b, d, m = (4, 128, 256)
        c, n = (128, 256)
        q = jax.random.normal(k1, (b, d, m), dtype=jnp.float32)
        k = jax.random.normal(k2, (d // d * b, d, n), dtype=jnp.float32).reshape(b, d, n)
        v = jax.random.normal(k3, (b, c, n), dtype=jnp.float32)
        return {'q': q, 'k': k, 'v': v}
    _L0_xattn_all = _L0_xattn_setup()
    _L0_xattn_in = {k: v for k, v in _L0_xattn_all.items() if k in ()}
    del _L0_xattn_all

    def _L0_ffn_setup():
        import jax, jax.numpy as jnp
        import numpy as np
        B_, S, D = (4, 512, 256)
        OUT = 256
        E, R = (8, 16)
        ALPHA = 32.0
        SCALING = ALPHA / R
        key = jax.random.key(seed)
        ks = jax.random.split(key, 6)
        x = jax.random.normal(ks[0], (B_, S, D), dtype=jnp.float32)
        W_base = jax.random.normal(ks[1], (OUT, D), dtype=jnp.float32) * D ** (-0.5)
        b_base = jax.random.normal(ks[2], (OUT,), dtype=jnp.float32) * 0.01
        router_W = jax.random.normal(ks[3], (E, D), dtype=jnp.float32) * D ** (-0.5)
        A = jax.random.normal(ks[4], (E, R, D), dtype=jnp.float32) * D ** (-0.5)
        Bw = jax.random.normal(ks[5], (E, OUT, R), dtype=jnp.float32) * 0.02
        return {'x': x, 'W_base': W_base, 'b_base': b_base, 'router_W': router_W, 'A': A, 'Bw': Bw}
    _L0_ffn_all = _L0_ffn_setup()
    _L0_ffn_in = {k: v for k, v in _L0_ffn_all.items() if k in ('W_base', 'b_base', 'router_W', 'A', 'Bw')}
    del _L0_ffn_all

    def _L1_attn_setup():
        import jax, jax.numpy as jnp
        import numpy as np
        D_MODEL = 256
        HEADS = 16
        HEAD_DIM = D_MODEL // HEADS
        key = jax.random.key(seed)
        k1, k2, k3 = jax.random.split(key, 3)
        B, S = (1, 256)
        x = jax.random.normal(k1, (B, S, D_MODEL), dtype=jnp.float32)
        Wqkv_w = jax.random.normal(k2, (D_MODEL + 2 * HEAD_DIM, D_MODEL), dtype=jnp.float32) * D_MODEL ** (-0.5)
        Wqkv_b = jnp.zeros((D_MODEL + 2 * HEAD_DIM,), dtype=jnp.float32)
        out_w = jax.random.normal(k3, (D_MODEL, D_MODEL), dtype=jnp.float32) * D_MODEL ** (-0.5)
        out_b = jnp.zeros((D_MODEL,), dtype=jnp.float32)
        return {'x': x, 'Wqkv_w': Wqkv_w, 'Wqkv_b': Wqkv_b, 'out_w': out_w, 'out_b': out_b}
    _L1_attn_all = _L1_attn_setup()
    _L1_attn_in = {k: v for k, v in _L1_attn_all.items() if k in ('Wqkv_w', 'Wqkv_b', 'out_w', 'out_b')}
    del _L1_attn_all

    def _L1_xattn_setup():
        import jax, jax.numpy as jnp
        import numpy as np
        DIM = 256
        H = 16
        D = 128
        INNER = H * D
        N_IMG = 257
        EPS = 1e-06

        def rms_norm(x, scale, eps=EPS):
            ms = jnp.mean(jnp.square(x), axis=-1, keepdims=True)
            return x * jax.lax.rsqrt(ms + eps) * scale

        def sdpa(q, k, v):
            scale = 1.0 / jnp.sqrt(jnp.asarray(D, q.dtype))
            scores = jnp.einsum('bshd,blhd->bhsl', q, k) * scale
            attn = jax.nn.softmax(scores, axis=-1)
            return jnp.einsum('bhsl,blhd->bshd', attn, v)
        key = jax.random.key(seed)
        ks = jax.random.split(key, 16)
        std = 1.0 / np.sqrt(DIM)
        inp = {'x': jax.random.normal(ks[0], (2, 512, DIM), jnp.float32), 'context': jax.random.normal(ks[1], (2, 769, DIM), jnp.float32), 'q_w': jax.random.normal(ks[2], (DIM, INNER), jnp.float32) * std, 'q_b': jnp.zeros((INNER,), jnp.float32), 'k_w': jax.random.normal(ks[3], (DIM, INNER), jnp.float32) * std, 'k_b': jnp.zeros((INNER,), jnp.float32), 'v_w': jax.random.normal(ks[4], (DIM, INNER), jnp.float32) * std, 'v_b': jnp.zeros((INNER,), jnp.float32), 'ki_w': jax.random.normal(ks[5], (DIM, INNER), jnp.float32) * std, 'ki_b': jnp.zeros((INNER,), jnp.float32), 'vi_w': jax.random.normal(ks[6], (DIM, INNER), jnp.float32) * std, 'vi_b': jnp.zeros((INNER,), jnp.float32), 'o_w': jax.random.normal(ks[7], (INNER, DIM), jnp.float32) * std, 'o_b': jnp.zeros((DIM,), jnp.float32), 'nq_s': jnp.ones((INNER,), jnp.float32), 'nkt_s': jnp.ones((INNER,), jnp.float32), 'nki_s': jnp.ones((INNER,), jnp.float32)}
        return inp
    _L1_xattn_all = _L1_xattn_setup()
    _L1_xattn_in = {k: v for k, v in _L1_xattn_all.items() if k in ('q_w', 'q_b', 'k_w', 'k_b', 'v_w', 'v_b', 'ki_w', 'ki_b', 'vi_w', 'vi_b', 'o_w', 'o_b', 'nq_s', 'nkt_s', 'nki_s')}
    del _L1_xattn_all

    def _L1_ffn_setup():
        import jax, jax.numpy as jnp
        import numpy as np
        QMAX = 127.0
        EPS = 1e-08

        def _quant_dequant(v, axis):
            scale = jnp.max(jnp.abs(v), axis=axis, keepdims=True) / QMAX
            scale = jnp.maximum(scale, EPS)
            q = jnp.clip(jnp.round(v / scale), -QMAX, QMAX)
            return q * scale

        def _ste(v, axis):
            return v + jax.lax.stop_gradient(_quant_dequant(v, axis) - v)
        key = jax.random.key(seed)
        k1, k2, k3 = jax.random.split(key, 3)
        H, I = (256, 704)
        x = jax.random.normal(k1, (4, 256, H), dtype=jnp.float32)
        w_gate_up = jax.random.normal(k2, (2 * I, H), dtype=jnp.float32) * H ** (-0.5)
        w_down = jax.random.normal(k3, (H, I), dtype=jnp.float32) * I ** (-0.5)
        return {'x': x, 'w_gate_up': w_gate_up, 'w_down': w_down}
    _L1_ffn_all = _L1_ffn_setup()
    _L1_ffn_in = {k: v for k, v in _L1_ffn_all.items() if k in ('w_gate_up', 'w_down')}
    del _L1_ffn_all
    return {'x': x, 'ctx_2048': ctx_2048, 'L0_attn_w_qkv': _L0_attn_in['w_qkv'], 'L0_attn_w_o': _L0_attn_in['w_o'], 'L0_attn_qn_g': _L0_attn_in['qn_g'], 'L0_attn_qn_b': _L0_attn_in['qn_b'], 'L0_attn_kn_g': _L0_attn_in['kn_g'], 'L0_attn_kn_b': _L0_attn_in['kn_b'], 'L0_ffn_W_base': _L0_ffn_in['W_base'], 'L0_ffn_b_base': _L0_ffn_in['b_base'], 'L0_ffn_router_W': _L0_ffn_in['router_W'], 'L0_ffn_A': _L0_ffn_in['A'], 'L0_ffn_Bw': _L0_ffn_in['Bw'], 'L1_attn_Wqkv_w': _L1_attn_in['Wqkv_w'], 'L1_attn_Wqkv_b': _L1_attn_in['Wqkv_b'], 'L1_attn_out_w': _L1_attn_in['out_w'], 'L1_attn_out_b': _L1_attn_in['out_b'], 'L1_xattn_q_w': _L1_xattn_in['q_w'], 'L1_xattn_q_b': _L1_xattn_in['q_b'], 'L1_xattn_k_w': _L1_xattn_in['k_w'], 'L1_xattn_k_b': _L1_xattn_in['k_b'], 'L1_xattn_v_w': _L1_xattn_in['v_w'], 'L1_xattn_v_b': _L1_xattn_in['v_b'], 'L1_xattn_ki_w': _L1_xattn_in['ki_w'], 'L1_xattn_ki_b': _L1_xattn_in['ki_b'], 'L1_xattn_vi_w': _L1_xattn_in['vi_w'], 'L1_xattn_vi_b': _L1_xattn_in['vi_b'], 'L1_xattn_o_w': _L1_xattn_in['o_w'], 'L1_xattn_o_b': _L1_xattn_in['o_b'], 'L1_xattn_nq_s': _L1_xattn_in['nq_s'], 'L1_xattn_nkt_s': _L1_xattn_in['nkt_s'], 'L1_xattn_nki_s': _L1_xattn_in['nki_s'], 'L1_ffn_w_gate_up': _L1_ffn_in['w_gate_up'], 'L1_ffn_w_down': _L1_ffn_in['w_down']}

def reference(x, ctx_2048, L0_attn_w_qkv, L0_attn_w_o, L0_attn_qn_g, L0_attn_qn_b, L0_attn_kn_g, L0_attn_kn_b, L0_ffn_W_base, L0_ffn_b_base, L0_ffn_router_W, L0_ffn_A, L0_ffn_Bw, L1_attn_Wqkv_w, L1_attn_Wqkv_b, L1_attn_out_w, L1_attn_out_b, L1_xattn_q_w, L1_xattn_q_b, L1_xattn_k_w, L1_xattn_k_b, L1_xattn_v_w, L1_xattn_v_b, L1_xattn_ki_w, L1_xattn_ki_b, L1_xattn_vi_w, L1_xattn_vi_b, L1_xattn_o_w, L1_xattn_o_b, L1_xattn_nq_s, L1_xattn_nkt_s, L1_xattn_nki_s, L1_ffn_w_gate_up, L1_ffn_w_down):
    import jax
    import jax.numpy as jnp

    def _L0_attn_ref(x, w_qkv, w_o, qn_g, qn_b, kn_g, kn_b):
        import jax, jax.numpy as jnp
        import numpy as np
        B, S, HID = (2, 256, 256)
        H, HKV, D = (16, 4, 128)
        ROPE_BASE = 1000000.0
        EPS = 1e-05

        def _layernorm(x, g, b):
            mu = jnp.mean(x, axis=-1, keepdims=True)
            var = jnp.mean(jnp.square(x - mu), axis=-1, keepdims=True)
            return (x - mu) * jax.lax.rsqrt(var + EPS) * g + b

        def _rope_tables(seq_len, dim, base):
            inv_freq = 1.0 / base ** (jnp.arange(0, dim, 2, dtype=jnp.float32) / dim)
            t = jnp.arange(seq_len, dtype=jnp.float32)
            freqs = jnp.outer(t, inv_freq)
            cos = jnp.concatenate([jnp.cos(freqs), jnp.cos(freqs)], axis=-1)
            sin = jnp.concatenate([jnp.sin(freqs), jnp.sin(freqs)], axis=-1)
            return (cos, sin)

        def _rotate_half(x):
            x1, x2 = jnp.split(x, 2, axis=-1)
            return jnp.concatenate([-x2, x1], axis=-1)
        b, s, _ = x.shape
        qkv = jnp.einsum('bsh,oh->bso', x, w_qkv)
        q, k, v = jnp.split(qkv, [H * D, (H + HKV) * D], axis=-1)
        q = q.reshape(b, s, H, D).transpose(0, 2, 1, 3)
        k = k.reshape(b, s, HKV, D).transpose(0, 2, 1, 3)
        v = v.reshape(b, s, HKV, D).transpose(0, 2, 1, 3)
        q = _layernorm(q, qn_g, qn_b)
        k = _layernorm(k, kn_g, kn_b)
        cos, sin = _rope_tables(s, D, ROPE_BASE)
        q = q * cos + _rotate_half(q) * sin
        k = k * cos + _rotate_half(k) * sin
        rep = H // HKV
        k = jnp.repeat(k, rep, axis=1)
        v = jnp.repeat(v, rep, axis=1)
        scores = jnp.einsum('bhqd,bhkd->bhqk', q, k) / jnp.sqrt(jnp.float32(D))
        causal = jnp.triu(jnp.ones((s, s), dtype=bool), k=1)
        scores = jnp.where(causal, -jnp.inf, scores)
        weights = jax.nn.softmax(scores, axis=-1)
        attn = jnp.einsum('bhqk,bhkd->bhqd', weights, v)
        attn = attn.transpose(0, 2, 1, 3).reshape(b, s, H * D)
        return jnp.einsum('bsd,od->bso', attn, w_o)

    def _L0_xattn_ref(q, k, v):
        import jax, jax.numpy as jnp
        import numpy as np
        N_HEAD = 8
        b, d, m = q.shape
        c = v.shape[1]
        h = N_HEAD
        qh = q.reshape(b * h, d // h, m)
        kh = k.reshape(b * h, d // h, -1)
        vh = v.reshape(b * h, c // h, -1)
        scale = 1.0 / jnp.sqrt(jnp.asarray(d // h, dtype=q.dtype))
        qk = jnp.einsum('bdm,bdn->bmn', qh, kh) * scale
        sm = jax.nn.softmax(qk, axis=-1)
        ret = jnp.einsum('bmn,bcn->bcm', sm, vh)
        return ret.reshape(b, c, m)

    def _L0_ffn_ref(x, W_base, b_base, router_W, A, Bw):
        import jax, jax.numpy as jnp
        import numpy as np
        B_, S, D = (4, 512, 256)
        OUT = 256
        E, R = (8, 16)
        ALPHA = 32.0
        SCALING = ALPHA / R
        base_out = jnp.einsum('bsd,od->bso', x, W_base) + b_base
        logits = jnp.einsum('bsd,ed->bse', jax.lax.stop_gradient(x), router_W)
        routing_probs = jax.nn.softmax(logits, axis=-1)
        expert_idx = jnp.argmax(routing_probs, axis=-1)
        onehot = jax.nn.one_hot(expert_idx, E, dtype=x.dtype)
        h = jnp.einsum('bsd,erd->bser', x, A)
        h = h * onehot[..., None]
        delta = jnp.einsum('bser,eor->bso', h, Bw)
        return base_out + delta * SCALING

    def _L1_attn_ref(x, Wqkv_w, Wqkv_b, out_w, out_b):
        import jax, jax.numpy as jnp
        import numpy as np
        D_MODEL = 256
        HEADS = 16
        HEAD_DIM = D_MODEL // HEADS
        B, S, _ = x.shape
        qkv = jnp.einsum('bsd,ed->bse', x, Wqkv_w) + Wqkv_b
        q = qkv[..., :D_MODEL]
        k = qkv[..., D_MODEL:D_MODEL + HEAD_DIM]
        v = qkv[..., D_MODEL + HEAD_DIM:]
        q = q.reshape(B, S, HEADS, HEAD_DIM)
        scale = 1.0 / np.sqrt(HEAD_DIM)
        scores = jnp.einsum('bqhd,bkd->bhqk', q, k) * scale
        min_val = jnp.finfo(scores.dtype).min
        causal = jnp.tril(jnp.ones((S, S), dtype=bool))
        scores = jnp.where(causal[None, None], scores, min_val)
        attn = jax.nn.softmax(scores, axis=-1)
        ctx = jnp.einsum('bhqk,bkd->bqhd', attn, v)
        ctx = ctx.reshape(B, S, D_MODEL)
        out = jnp.einsum('bsd,ed->bse', ctx, out_w) + out_b
        return out

    def _L1_xattn_ref(x, context, q_w, q_b, k_w, k_b, v_w, v_b, ki_w, ki_b, vi_w, vi_b, o_w, o_b, nq_s, nkt_s, nki_s):
        import jax, jax.numpy as jnp
        import numpy as np
        DIM = 256
        H = 16
        D = 128
        INNER = H * D
        N_IMG = 257
        EPS = 1e-06

        def rms_norm(x, scale, eps=EPS):
            ms = jnp.mean(jnp.square(x), axis=-1, keepdims=True)
            return x * jax.lax.rsqrt(ms + eps) * scale

        def sdpa(q, k, v):
            scale = 1.0 / jnp.sqrt(jnp.asarray(D, q.dtype))
            scores = jnp.einsum('bshd,blhd->bhsl', q, k) * scale
            attn = jax.nn.softmax(scores, axis=-1)
            return jnp.einsum('bhsl,blhd->bshd', attn, v)
        B, S, _ = x.shape
        img_ctx = context[:, :N_IMG]
        txt_ctx = context[:, N_IMG:]
        q = rms_norm(x @ q_w + q_b, nq_s).reshape(B, S, H, D)
        k_txt = rms_norm(txt_ctx @ k_w + k_b, nkt_s).reshape(B, -1, H, D)
        v_txt = (txt_ctx @ v_w + v_b).reshape(B, -1, H, D)
        out_txt = sdpa(q, k_txt, v_txt)
        k_img = rms_norm(img_ctx @ ki_w + ki_b, nki_s).reshape(B, -1, H, D)
        v_img = (img_ctx @ vi_w + vi_b).reshape(B, -1, H, D)
        out_img = sdpa(q, k_img, v_img)
        out = (out_txt + out_img).reshape(B, S, INNER)
        return out @ o_w + o_b

    def _L1_ffn_ref(x, w_gate_up, w_down):
        import jax, jax.numpy as jnp
        import numpy as np
        QMAX = 127.0
        EPS = 1e-08

        def _quant_dequant(v, axis):
            scale = jnp.max(jnp.abs(v), axis=axis, keepdims=True) / QMAX
            scale = jnp.maximum(scale, EPS)
            q = jnp.clip(jnp.round(v / scale), -QMAX, QMAX)
            return q * scale

        def _ste(v, axis):
            return v + jax.lax.stop_gradient(_quant_dequant(v, axis) - v)
        I = w_down.shape[1]
        xq = _ste(x, axis=-1)
        w1q = _ste(w_gate_up, axis=-1)
        gate_up = jnp.einsum('bsh,oh->bso', xq, w1q)
        gate, up = (gate_up[..., :I], gate_up[..., I:])
        h = jax.nn.silu(gate) * up
        hq = _ste(h, axis=-1)
        w2q = _ste(w_down, axis=-1)
        return jnp.einsum('bsi,oi->bso', hq, w2q)
    x = x + _L0_attn_ref(_layernorm(x, axis=-1), L0_attn_w_qkv, L0_attn_w_o, L0_attn_qn_g, L0_attn_qn_b, L0_attn_kn_g, L0_attn_kn_b)
    x = x + _L0_xattn_ref(_layernorm(x, axis=-1), ctx_2048, ctx_2048)
    x = x + _L0_ffn_ref(_layernorm(x, axis=-1), L0_ffn_W_base, L0_ffn_b_base, L0_ffn_router_W, L0_ffn_A, L0_ffn_Bw)
    x = x + _L1_attn_ref(_layernorm(x, axis=-1), L1_attn_Wqkv_w, L1_attn_Wqkv_b, L1_attn_out_w, L1_attn_out_b)
    x = x + _L1_xattn_ref(_layernorm(x, axis=-1), ctx_2048, L1_xattn_q_w, L1_xattn_q_b, L1_xattn_k_w, L1_xattn_k_b, L1_xattn_v_w, L1_xattn_v_b, L1_xattn_ki_w, L1_xattn_ki_b, L1_xattn_vi_w, L1_xattn_vi_b, L1_xattn_o_w, L1_xattn_o_b, L1_xattn_nq_s, L1_xattn_nkt_s, L1_xattn_nki_s)
    x = x + _L1_ffn_ref(_layernorm(x, axis=-1), L1_ffn_w_gate_up, L1_ffn_w_down)
    return x

_drawn_inputs = setup_inputs


def setup_inputs(seed=0):
    import zlib

    import numpy as np

    out = dict(_drawn_inputs(seed))
    spreads = {'L0_attn_qn_g': (1.0, 0.6),
     'L0_attn_qn_b': (0.0, 0.596),
     'L0_attn_kn_g': (1.0, 0.6),
     'L0_attn_kn_b': (0.0, 0.8),
     'L1_attn_Wqkv_b': (0.0, 0.1),
     'L1_attn_out_b': (0.0, 0.1),
     'L1_xattn_q_b': (0.0, 0.291),
     'L1_xattn_k_b': (0.0, 0.1),
     'L1_xattn_v_b': (0.0, 0.1),
     'L1_xattn_ki_b': (0.0, 0.8),
     'L1_xattn_vi_b': (0.0, 0.1),
     'L1_xattn_o_b': (0.0, 0.1),
     'L1_xattn_nq_s': (1.0, 0.2),
     'L1_xattn_nkt_s': (1.0, 0.2),
     'L1_xattn_nki_s': (1.0, 0.2)}
    factors = {'L0_ffn_b_base': 6.865}
    for name, (base, spread) in spreads.items():
        noise = np.random.default_rng([zlib.crc32(name.encode()), seed]).standard_normal(out[name].shape)
        drawn = base * np.exp(spread * noise) if base else spread * noise
        out[name] = jnp.asarray(drawn.astype(out[name].dtype))
    for name, factor in factors.items():
        out[name] = (out[name] * factor).astype(out[name].dtype)
    return out
```

```python
from contextlib import ExitStack

import numpy as np
import concourse.bass as bass
from concourse import mybir
from concourse.alu_op_type import AluOpType as ALU

F32 = mybir.dt.float32
F16 = mybir.dt.float16
BF16 = mybir.dt.bfloat16
ACT = mybir.ActivationFunctionType
AX = mybir.AxisListType.X

P = 128
TILES = 32
SEQ = 64
DM = 256
KC = DM // P
WS = 64.0
LN_EPS = 1e-5
NEG = -1.0e30
PHASES = (0, 1, 2, 3, 4, 5)


def over_tiles(eng, head, step):
    head()
    step(0, 0, True)
    step(1, 1, TILES > 2)
    if TILES > 4:
        with eng.Fori(1, TILES // 2 - 1) as i:
            step(2 * i, 0, True)
            step(2 * i + 1, 1, True)
    if TILES > 2:
        step(TILES - 2, 0, True)
        step(TILES - 1, 1, False)


def wait_used(eng, sem, t, buffers, per_tile=1, last=0):
    if isinstance(t, int) and t < buffers:
        return
    eng.wait_ge(sem, (t - buffers) * per_tile + (last or per_tile))


class Semaphores:

    def __init__(self, nc, tag):
        self.nc, self.tag, self.stack, self.all = nc, tag, ExitStack(), []

    def __enter__(self):
        return self

    def __call__(self, name):
        self.all.append(self.stack.enter_context(self.nc.semaphore(self.tag + name)))
        return self.all[-1]

    def __exit__(self, *error):
        if error[0] is None:
            with self.nc.Block() as block:
                @block.sync
                def _(sp):
                    for s in self.all:
                        sp.sem_clear(s)
        self.stack.close()


class Chain:

    def __init__(self, eng, sem, head, each):
        self.eng, self.sem, self.head, self.each, self.k, self.base = eng, sem, head, each, 0, 0

    def tile(self, t):
        self.base, self.k = self.head + t * self.each, 0

    def link(self, ins):
        ins.then_inc(self.sem, 1)
        self.k += 1
        self.eng.wait_ge(self.sem, self.base + self.k)


def mm3(pe, out, a, b, start, stop):
    pe.matmul(out, a[0], b[0], start=start, stop=False)
    pe.matmul(out, a[0], b[1], start=False, stop=False)
    return pe.matmul(out, a[1], b[0], start=False, stop=stop)


class Machine:

    def __init__(self, nc, ctx, d):
        self.nc, self.d = nc, d
        self.x_all = ctx.enter_context(nc.sbuf_tensor("x_all", [P, TILES, DM], F32))
        self.ident = ctx.enter_context(nc.sbuf_tensor("ident", [P, P], F32))
        self.identb = ctx.enter_context(nc.sbuf_tensor("identb", [P, P], BF16))
        self.ones = ctx.enter_context(nc.sbuf_tensor("ones", [P, P], F32))
        self.ones2 = ctx.enter_context(nc.sbuf_tensor("ones2", [P, DM], F32))
        self.onesh = ctx.enter_context(nc.sbuf_tensor("onesh", [P, P], F16))
        self.mhalf = ctx.enter_context(nc.sbuf_tensor("mhalf", [P, 32], F32))


def load_resident(m):
    nc = m.nc
    with ExitStack() as ctx:
        sem = ctx.enter_context(Semaphores(nc, "in_"))
        x_in, id_in = sem("x_in"), sem("id_in")
        block = ctx.enter_context(nc.Block())

        @block.sync
        def _(sp):
            sp.dma_start(m.ident[:, :], m.d["ident"]).then_inc(id_in, 16)
            for s in range(0, TILES, 4 if TILES >= 4 else TILES):
                n = min(4, TILES)
                sp.dma_start(m.x_all[:, s:s + n, :],
                             m.d["x"][s * P:(s + n) * P, :].rearrange("(t p) d -> p t d", p=P)).then_inc(x_in, 16)
            sp.wait_ge(x_in, 16 * (TILES // min(4, TILES)))

        @block.vector
        def _(dve):
            dve.memset(m.ones[:, :], 1.0)
            dve.memset(m.onesh[:, :], 1.0)
            dve.memset(m.ones2[:, :], 1.0)
            dve.memset(m.mhalf[:, :], -0.5)
            dve.wait_ge(id_in, 16)
            dve.tensor_copy(m.identb[:, :], m.ident[:, :])


def store_result(m):
    nc = m.nc
    with ExitStack() as ctx:
        sem = ctx.enter_context(Semaphores(nc, "out_"))
        x_out = sem("x_out")
        block = ctx.enter_context(nc.Block())

        @block.sync
        def _(sp):
            n = min(4, TILES)
            for s in range(0, TILES, n):
                sp.dma_start(m.d["out"][s * P:(s + n) * P, :].rearrange("(t p) d -> p t d", p=P),
                             m.x_all[:, s:s + n, :]).then_inc(x_out, 16)
            sp.wait_ge(x_out, 16 * (TILES // n))


STAGE = 2048


def split_weights(m, jobs, tag):
    nc = m.nc
    with ExitStack() as ctx:
        stage = [ctx.enter_context(nc.sbuf_tensor(f"stage{tag}{i}", [P, STAGE], F32)) for i in range(3)]
        mean = ctx.enter_context(nc.sbuf_tensor(f"mean{tag}", [P, STAGE // P], F32))
        sem = ctx.enter_context(Semaphores(nc, tag))
        loaded = [sem(f"w_loaded{i}") for i in range(3)]
        centred, high_done, low_done = sem("w_centred"), sem("w_high"), sem("w_low")
        pieces = []
        for src, hi, lo, centre in jobs:
            p, n = src.shape
            for c in range(0, n, STAGE):
                e = min(n, c + STAGE)
                pieces.append((p, e - c, src[:, c:e], hi[:, c:e], lo[:, c:e], centre))
        centres = [sum(x[5] for x in pieces[:i + 1]) for i in range(len(pieces))]
        block = ctx.enter_context(nc.Block())

        @block.sync
        def _(sp):
            for i, (p, n, src, hi, lo, centre) in enumerate(pieces):
                if i >= 3:
                    sp.wait_ge(low_done, i - 2)
                sp.dma_start(stage[i % 3][0:p, 0:n], src).then_inc(loaded[i % 3], 16)

        @block.scalar
        def _(act):
            for i, (p, n, src, hi, lo, centre) in enumerate(pieces):
                act.wait_ge(loaded[i % 3], 16 * (i // 3 + 1))
                if centre:
                    act.wait_ge(centred, 3 * centres[i])
                act.activation(hi, stage[i % 3][0:p, 0:n], ACT.Copy, scale=WS).then_inc(high_done, 1)

        @block.vector
        def _(dve):
            def take_means(i):
                if i >= len(pieces) or not pieces[i][5]:
                    return
                w = stage[i % 3][:, 0:pieces[i][1]].rearrange("p (h d) -> p h d", d=P)
                heads = pieces[i][1] // P
                dve.wait_ge(loaded[i % 3], 16 * (i // 3 + 1))
                dve.reduce_sum(mean[:, 0:heads], w, AX).then_inc(centred, 1)
                dve.wait_ge(centred, 3 * centres[i] - 2)
                dve.tensor_scalar(mean[:, 0:heads], mean[:, 0:heads], 1.0 / P, None, ALU.mult).then_inc(centred, 1)
                dve.wait_ge(centred, 3 * centres[i] - 1)
                dve.tensor_tensor(w, w, spread(mean[:, 0:heads], P), ALU.subtract).then_inc(centred, 1)
                dve.wait_ge(centred, 3 * centres[i])

            take_means(0)
            for i, (p, n, src, hi, lo, centre) in enumerate(pieces):
                take_means(i + 1)
                dve.wait_ge(high_done, i + 1)
                dve.scalar_tensor_tensor(lo, stage[i % 3][0:p, 0:n], WS, hi, ALU.mult, ALU.subtract).then_inc(low_done, 1)


def spread(a, n):
    return a.rearrange("p (k o) -> p k o", o=1).to_broadcast([a.shape[0], a.shape[1], n])


def repeat(a, n):
    return a.rearrange("p (o k) -> p o k", o=1).to_broadcast([a.shape[0], n, a.shape[1]])


class LayerNorm:

    def __init__(self, m, ctx, sem, tag, tp):
        nc, self.m, self.tp = m.nc, m, tp
        sb = lambda n, s, t: ctx.enter_context(nc.sbuf_tensor(n + tag, s, t))
        self.st = sb("ln_st", [P, 6], F32)
        self.mv = sb("ln_mv", [P, 2, 2], F32)
        self.ve = sb("ln_ve", [P, 2, 1], F32)
        self.rstd = sb("ln_rstd", [P, 2, 1], F32)
        self.turn = sb("ln_turn", [P, 1], F32)
        self.eps = sb("ln_eps", [P, 1], F32)
        self.xn = sb("ln_xn", [P, 2, DM], F32)
        self.xh = sb("ln_xh", [P, 2, KC, P], F16)
        self.xl = sb("ln_xl", [P, 2, KC, P], F16)
        self.eps_set = sem("eps_set")
        self.mv_ready = sem("mv_ready")
        self.pool_chain = sem("ln_pool")
        self.rstd_ready = sem("rstd_ready")
        self.xn_ready = sem("xn_ready")
        self.tp_ready = sem("tp_ready")
        self.xh_ready = sem("xh_ready")
        self.xl_ready = sem("xl_ready")

    def pool(self, pool):
        pool.memset(self.eps[:, :], LN_EPS).then_inc(self.eps_set, 1)
        pool.wait_ge(self.eps_set, 1)
        self.pool_step(pool, 0, 0)

    def pool_step(self, pool, t, p):
        pool.wait_ge(self.mv_ready, t + 1)
        pool.tensor_tensor(self.ve[:, p], self.mv[:, p, 1:2], self.eps[:, :], ALU.add).then_inc(self.pool_chain, 1)
        pool.wait_ge(self.pool_chain, t + 1)
        pool.tensor_tensor(self.rstd[:, p], self.ve[:, p], self.m.mhalf[:, 0:1], ALU.pow).then_inc(self.rstd_ready, 1)

    def stats(self, dve, ch, t, p):
        ch.link(dve.bn_stats(self.st[:, :], self.m.x_all[:, at(t), :]))
        dve.memset(self.turn[:, :], 0.0)
        dve.bn_aggr(self.mv[:, p], self.st[:, :]).then_inc(self.mv_ready, 1)

    def normalise(self, dve, t, p):
        dve.wait_ge(self.rstd_ready, t + 1)
        dve.wait_ge(self.mv_ready, t + 1)
        dve.tensor_scalar(self.xn[:, p], self.m.x_all[:, at(t), :], self.mv[:, p, 0:1], self.rstd[:, p],
                          ALU.subtract, ALU.mult).then_inc(self.xn_ready, 1)

    def transpose(self, pe, t, p):
        pe.wait_ge(self.xn_ready, t + 1)
        if not (isinstance(t, int) and t < 1):
            pe.wait_ge(self.xl_ready, t)
        for c in range(KC):
            last = pe.transpose(self.tp[:, c * P:(c + 1) * P], self.xn[:, p, c * P:(c + 1) * P], self.m.ident[:, :])
        last.then_inc(self.tp_ready, 1)

    def high(self, act, t, p, used, per_tile=1):
        act.wait_ge(self.tp_ready, t + 1)
        wait_used(act, used, t, 2, per_tile)
        act.copy(self.xh[:, p], self.tp[:, 0:DM]).then_inc(self.xh_ready, 1)

    def low(self, dve, t, p):
        dve.wait_ge(self.xh_ready, t + 1)
        dve.tensor_tensor(self.xl[:, p], self.tp[:, 0:DM], self.xh[:, p], ALU.subtract).then_inc(self.xl_ready, 1)

    def operand(self, p, c, lo=0, n=P):
        return self.xh[:, p, c, lo:lo + n], self.xl[:, p, c, lo:lo + n]


def dram_tile(a, t):
    return a[t, :, :] if isinstance(t, int) else a[bass.ds(t, 1), :, :].rearrange("a p n -> p (a n)")


def at(t):
    return t if isinstance(t, int) else bass.ds(t, 1)

HEADS, HD = 16, 128
KV = 4
REP = HEADS // KV
PAIRS = HEADS // 2


class Attend:

    def __init__(self, m, ctx, sem, tag, ps, w_out, v_cols):
        nc, self.m, self.ps, self.w_out, self.v_cols = m.nc, m, ps, w_out, v_cols
        sb = lambda n, s, t=F32: ctx.enter_context(nc.sbuf_tensor(tag + n, s, t))
        self.pv_count = 2
        self.s = sb("s", [P, HEADS, SEQ])
        self.e = sb("e", [P, HEADS, SEQ])
        self.mx = sb("mx", [P, HEADS])
        self.den = sb("den", [P, HEADS])
        self.rden = sb("rden", [P, HEADS])
        self.pt = sb("pt", [P, PAIRS, P])
        self.v = sb("v", [P, 2, v_cols])
        self.vsw = sb("vsw", [P, 2, v_cols])
        self.oh = sb("oh", [P, 2, PAIRS, P], F16)
        self.ol = sb("ol", [P, 2, PAIRS, P], F16)
        self.sc_ready = sem("sc_ready")
        self.s_ready = sem("s_ready")
        self.e_ready = sem("e_ready")
        self.p_ready = sem("p_ready")
        self.ptr_ready = sem("ptr_ready")
        self.pt_ready = sem("pt_ready")
        self.v_ready = sem("v_ready")
        self.vsw_ready = sem("vsw_ready")
        self.pv_ready = sem("pv_ready")
        self.oh_ready = sem("oh_ready")
        self.ol_ready = sem("ol_ready")
        self.y_ready = sem("y_ready")
        self.x_done = sem("x_done")
        self.sc = ps[:, 4:6, :].rearrange("p k (h s) -> p (k h) s", s=SEQ)
        self.ptp = ps[:, 4:6, :].rearrange("p k (h s) -> p (k h) s", s=P)
        self.o = ps[:, 6:8, :].rearrange("p k (h s) -> p (k h) s", s=P)
        self.y = ps[:, 4, 0:DM]

    def swap_values(self, sp, t, p):
        sp.wait_ge(self.v_ready, self.v_count * (t + 1))
        wait_used(sp, self.vsw_ready, t, 1, 32)
        wait_used(sp, self.pv_ready, t, 2, 2)
        for a in range(2):
            b = 1 - a
            sp.dma_start(self.vsw[a * SEQ:(a + 1) * SEQ, p, :],
                         self.v[b * SEQ:(b + 1) * SEQ, p, :]).then_inc(self.vsw_ready, 16)

    def take_max(self, dve, ch):
        ch.link(dve.reduce_max(self.mx[:, :], self.s[:, :, :], AX))
        dve.tensor_tensor(self.s[:, :, :], self.s[:, :, :], spread(self.mx[:, :], SEQ),
                          ALU.subtract).then_inc(self.s_ready, 1)

    def exponential(self, act, t, scale=1.0):
        act.wait_ge(self.s_ready, t + 1)
        wait_used(act, self.p_ready, t, 1)
        wait_used(act, self.ptr_ready, t, 1)
        act.activation(self.e[:, :, :], self.s[:, :, :], ACT.Exp, scale=scale).then_inc(self.e_ready, 1)

    def normalise(self, dve, ch, t):
        dve.wait_ge(self.e_ready, t + 1)
        ch.link(dve.reduce_sum(self.den[:, :], self.e[:, :, :], AX))
        ch.link(dve.reciprocal(self.rden[:, :], self.den[:, :]))
        dve.tensor_tensor(self.e[:, :, :], self.e[:, :, :], spread(self.rden[:, :], SEQ),
                          ALU.mult).then_inc(self.p_ready, 1)

    def transpose(self, pe, t):
        pe.wait_ge(self.p_ready, t + 1)
        for k in range(PAIRS):
            pair = self.e[:, 2 * k:2 * k + 2, :].rearrange("p h s -> p (h s)")
            last = pe.transpose(self.ptp[:, k, :], pair, self.m.ident[:, :])
        last.then_inc(self.ptr_ready, 1)

    def copy_transposed(self, act, t):
        act.wait_ge(self.ptr_ready, t + 1)
        wait_used(act, self.pv_ready, t, 1, self.pv_count)
        act.copy(self.pt[:, :, :], self.ptp).then_inc(self.pt_ready, 1)

    def values(self, pe, t, p, parity):
        if parity == 0:
            pe.wait_ge(self.pt_ready, t + 1)
            pe.wait_ge(self.vsw_ready, 32 * (t + 1))
            pe.wait_ge(self.v_ready, self.v_count * (t + 1))
            wait_used(pe, self.ol_ready, t, 1, 2)
        else:
            pe.wait_ge(self.ol_ready, 2 * t + 1)
        rows = slice(parity * SEQ, (parity + 1) * SEQ)
        per = PAIRS * P // self.v_cols if self.v_cols < HEADS * HD else 0
        for b in range(2):
            v = self.v if b == parity else self.vsw
            cols = slice(b * SEQ, (b + 1) * SEQ)
            if per:
                for g in range(PAIRS // per):
                    last = pe.matmul(self.o[:, g * per:(g + 1) * per, cols], v[rows, p, g * HD:(g + 1) * HD],
                                     self.pt[rows, g * per:(g + 1) * per, cols], start=True, stop=True)
            else:
                for k in range(PAIRS):
                    h = 2 * k + parity
                    last = pe.matmul(self.o[:, k, cols], v[rows, p, h * HD:(h + 1) * HD],
                                     self.pt[rows, k, cols], start=True, stop=True)
        last.then_inc(self.pv_ready, 1)

    def high(self, act, t, parity):
        act.wait_ge(self.pv_ready, 2 * t + 1 + parity)
        wait_used(act, self.y_ready, t, 1)
        act.copy(self.oh[:, parity], self.o).then_inc(self.oh_ready, 1)

    def low(self, dve, t, parity):
        dve.wait_ge(self.oh_ready, 2 * t + 1 + parity)
        dve.tensor_tensor(self.ol[:, parity], self.o, self.oh[:, parity], ALU.subtract).then_inc(self.ol_ready, 1)

    def project(self, pe, t, parity):
        pe.wait_ge(self.ol_ready, 2 * t + 1 + parity)
        for k in range(PAIRS):
            h = 2 * k + parity
            last = mm3(pe, self.y, (self.oh[:, parity, k], self.ol[:, parity, k]),
                       (self.w_out[0][:, h * DM:(h + 1) * DM], self.w_out[1][:, h * DM:(h + 1) * DM]),
                       parity == 0 and k == 0, parity == 1 and k == PAIRS - 1)
        if parity:
            last.then_inc(self.y_ready, 1)

    def add(self, dve, ch, t, bias=None):
        dve.wait_ge(self.y_ready, t + 1)
        x = self.m.x_all[:, at(t), :]
        upd = dve.scalar_tensor_tensor(x, self.y, 1.0 / WS, x, ALU.mult, ALU.add)
        if bias is not None:
            ch.link(upd)
            upd = dve.tensor_tensor(x, x, bias, ALU.add)
        upd.then_inc(self.x_done, 1)


def attention_gqa(m):
    nc, d = m.nc, m.d
    with ExitStack() as ctx:
        sb = lambda n, s, t=F32: ctx.enter_context(nc.sbuf_tensor("a0_" + n, s, t))
        sem = ctx.enter_context(Semaphores(nc, "a0_"))
        ps = ctx.enter_context(nc.psum_tensor("a0_ps", [P, 8, 512], F32))
        NQ, NK = HEADS * HD, KV * HD
        wq, wk, wks, wv = [[sb(f"{n}{i}", [P, KC, c], F16) for i in range(2)]
                           for n, c in (("wq", NQ), ("wk", NK), ("wks", NK), ("wv", NK))]
        wo = [sb(f"wo{i}", [P, HEADS * DM], F16) for i in range(2)]
        flat = lambda w: w[:, :, :].rearrange("p c n -> p (c n)")
        split_weights(m, [(d["a0_q"], flat(wq[0]), flat(wq[1]), 1), (d["a0_k"], flat(wk[0]), flat(wk[1]), 1),
                          (d["a0_ks"], flat(wks[0]), flat(wks[1]), 1), (d["a0_v"], flat(wv[0]), flat(wv[1]), 0),
                          (d["a0_o"], wo[0][:, :], wo[1][:, :], 0)], "a0")
        ln = LayerNorm(m, ctx, sem, "a0", ps[:, 0, :])
        at_ = Attend(m, ctx, sem, "a0", ps, wo, NK)
        at_.v_count = 1
        rope = sb("rope", [P, 3, SEQ])
        gb = sb("gb", [P, 8])
        tab = sb("tab", [P, 10, SEQ])
        QC, QS, BQ, KC_, KS, BK, KCS, KSS, BKS, TMP = range(10)
        mask = sb("mask", [P, SEQ])
        u = sb("u", [P, HEADS, P])
        w = sb("w", [P, HEADS, P])
        sq = sb("sq", [P, HEADS, P])
        sqk = sb("sqk", [P, NK])
        kt = sb("kt", [P, 2, NK])
        tmp = sb("tmp", [P, 2, NK])
        vk = sb("vk", [P, KV])
        rk = sb("rk", [P, KV])
        rkd = sb("rkd", [P, KV, P])
        vq = sb("vq", [P, HEADS])
        rq = sb("rq", [P, HEADS])
        s2m = sb("s2m", [P, KV, SEQ])
        const_in, tab_set = sem("const_in"), sem("tab_set")
        chain, pool_chain = sem("chain"), sem("pool_chain")
        k_ready, ks_ready, vp_ready, q_ready, ksum_ready = (sem(n) for n in ("k_ready", "ks_ready", "vp_ready", "q_ready", "ksum_ready"))
        sqk_ready, sq_ready, uw_ready = sem("sqk_ready"), sem("sq_ready"), sem("uw_ready")
        kraw_ready, vk_ready, rkd_ready, rkb_ready, kt_ready = (sem(n) for n in ("kraw_ready", "vk_ready", "rkd_ready", "rkb_ready", "kt_ready"))
        vq_ready, rq_ready = sem("vq_ready"), sem("rq_ready")
        QBANK = (1, 2, 3, 0)
        s2_ps = ps[:, 6, 0:KV * SEQ].rearrange("p (g s) -> p g s", s=SEQ)
        var_ps = ps[:, 6, KV * SEQ:KV * SEQ + HEADS]
        seqs = lambda a: a.rearrange("p (r s) -> p r s", s=SEQ)
        block = ctx.enter_context(nc.Block())

        @block.sync
        def _(sp):
            sp.dma_start(rope[:, :, :], d["rope"]).then_inc(const_in, 16)
            sp.dma_start(gb[:, :], d["a0_gb"]).then_inc(const_in, 16)
            sp.dma_start(mask[:, :], d["causal"]).then_inc(const_in, 16)

            def step(t, p, has_next):
                if has_next:
                    at_.swap_values(sp, t + 1, 1 - p)
            over_tiles(sp, lambda: at_.swap_values(sp, 0, 0), step)
            sp.wait_ge(at_.vsw_ready, 32 * TILES)

        @block.gpsimd
        def _(pool):
            def key_rstd(t):
                pool.wait_ge(vk_ready, t + 1)
                pool.tensor_tensor(rk[:, :], vk[:, :], m.mhalf[:, 0:KV], ALU.pow).then_inc(pool_chain, 1)
                pool.wait_ge(pool_chain, t + 1)
                wait_used(pool, rkb_ready, t, 1)
                pool.tensor_tensor(rkd[:, :, :], repeat(m.ident[:, :], KV), spread(rk[:, :], P), ALU.mult).then_inc(rkd_ready, 1)

            def head():
                ln.pool(pool)
                key_rstd(0)

            def step(t, p, has_next):
                if has_next:
                    ln.pool_step(pool, t + 1, 1 - p)
                pool.wait_ge(vq_ready, t + 1)
                pool.tensor_tensor(rq[:, :], vq[:, :], m.mhalf[:, 0:HEADS], ALU.pow).then_inc(rq_ready, 1)
                if has_next:
                    key_rstd(t + 1)
            over_tiles(pool, head, step)

        @block.scalar
        def _(act):
            def key_value(t, p):
                act.wait_ge(k_ready, t + 1)
                wait_used(act, ksum_ready, t, 1)
                act.activation(sqk[:, :], ps[:, 1, :], ACT.Square).then_inc(sqk_ready, 1)
                act.wait_ge(vp_ready, t + 1)
                wait_used(act, at_.pv_ready, t, 2, 2)
                if not (isinstance(t, int) and t < 2):
                    act.wait_ge(at_.vsw_ready, 32 * (t - 1))
                act.activation(at_.v[:, p, :], ps[:, 3, :], ACT.Copy, scale=1.0 / WS).then_inc(at_.v_ready, 1)

            def square(t, g):
                act.wait_ge(q_ready, 4 * t + g + 1)
                wait_used(act, at_.sc_ready, t, 1)
                act.activation(sq[:, 4 * g:4 * g + 4, :].rearrange("p h s -> p (h s)"), ps[:, QBANK[g], :],
                               ACT.Square).then_inc(sq_ready, 1)

            def head():
                ln.high(act, 0, 0, q_ready, 4)
                key_value(0, 0)
                for g in range(4):
                    square(0, g)

            def step(t, p, has_next):
                if has_next:
                    ln.high(act, t + 1, 1 - p, q_ready, 4)
                    key_value(t + 1, 1 - p)
                    square(t + 1, 0)
                at_.exponential(act, t)
                if has_next:
                    for g in range(1, 4):
                        square(t + 1, g)
                at_.copy_transposed(act, t)
                at_.high(act, t, 0)
                at_.high(act, t, 1)
            over_tiles(act, head, step)

        @block.vector
        def _(dve):
            ch = Chain(dve, chain, 17, 10)

            def tables():
                ts = lambda o, a, s: ch.link(dve.tensor_scalar(tab[:, o, :], a, s, None, ALU.mult))
                cos, sgn, neg = rope[:, 0, :], rope[:, 1, :], rope[:, 2, :]
                dve.wait_ge(const_in, 48)
                qg, qb, qbs, kg, kb, kgs, kbs = (gb[:, i:i + 1] for i in range(7))
                ts(QC, cos, qg)
                ts(QS, neg, qg)
                ts(KC_, cos, kg)
                ts(KS, sgn, kgs)
                ts(KCS, cos, kgs)
                ts(KSS, neg, kg)
                for out, b0, b1, sn in ((BQ, qb, qbs, sgn), (BK, kb, kbs, sgn), (BKS, kbs, kb, neg)):
                    ts(TMP, sn, b1)
                    ch.link(dve.scalar_tensor_tensor(tab[:, out, :], cos, b0, tab[:, TMP, :], ALU.mult, ALU.add))
                ch.link(dve.tensor_copy(tab[:, TMP, :], cos))

            def keys_raw(t):
                dve.wait_ge(sqk_ready, t + 1)
                dve.wait_ge(ks_ready, t + 1)
                k0, k1 = seqs(ps[:, 1, :]), seqs(ps[:, 2, :])
                bc = lambda i: repeat(tab[:, i, :], NK // SEQ)
                wait_used(dve, at_.sc_ready, t, 1)
                dve.tensor_tensor(seqs(kt[:, 0, :]), k0, bc(KC_), ALU.mult)
                dve.tensor_tensor(seqs(tmp[:, 0, :]), k1, bc(KS), ALU.mult)
                dve.tensor_tensor(seqs(kt[:, 1, :]), k1, bc(KCS), ALU.mult)
                dve.tensor_tensor(seqs(tmp[:, 1, :]), k0, bc(KSS), ALU.mult).then_inc(kraw_ready, 1)
                dve.wait_ge(ksum_ready, t + 1)
                dve.tensor_scalar(vk[:, :], ps[:, 0, 0:KV], 1.0 / HD, LN_EPS * WS * WS, ALU.mult, ALU.add).then_inc(vk_ready, 1)
                dve.wait_ge(kraw_ready, t + 1)
                both = lambda a: a[:, :, :].rearrange("p a n -> p (a n)")
                ch.link(dve.tensor_tensor(both(kt), both(kt), both(tmp), ALU.add))

            def keys_scaled(t):
                bc = lambda i: repeat(tab[:, i, :], NK // SEQ)
                dve.wait_ge(rkb_ready, t + 1)
                ch.link(dve.tensor_tensor(kt[:, :, :], kt[:, :, :], repeat(ps[:, 0, :], 2), ALU.mult))
                ch.link(dve.tensor_tensor(seqs(kt[:, 0, :]), seqs(kt[:, 0, :]), bc(BK), ALU.add))
                dve.tensor_tensor(seqs(kt[:, 1, :]), seqs(kt[:, 1, :]), bc(BKS), ALU.add).then_inc(kt_ready, 1)

            def rotate_query(t, g):
                dve.wait_ge(sq_ready, 4 * t + g + 1)
                wait_used(dve, at_.sc_ready, t, 1)
                q = seqs(ps[:, QBANK[g], :])
                heads = lambda a: seqs(a[:, 4 * g:4 * g + 4, :].rearrange("p h s -> p (h s)"))
                dve.tensor_tensor(heads(u), q, repeat(tab[:, QC, :], 512 // SEQ), ALU.mult)
                dve.tensor_tensor(heads(w), q, repeat(tab[:, QS, :], 512 // SEQ), ALU.mult).then_inc(uw_ready, 1)

            def head():
                tables()
                ln.stats(dve, ch, 0, 0)
                ln.normalise(dve, 0, 0)
                ln.low(dve, 0, 0)
                keys_raw(0)
                for g in range(3):
                    rotate_query(0, g)
                keys_scaled(0)
                rotate_query(0, 3)

            def step(t, p, has_next):
                ch.tile(t)
                if has_next:
                    ln.stats(dve, ch, t + 1, 1 - p)
                    ln.normalise(dve, t + 1, 1 - p)
                    ln.low(dve, t + 1, 1 - p)
                dve.wait_ge(at_.sc_ready, t + 1)
                dve.tensor_scalar(vq[:, :], var_ps, 1.0, HD * LN_EPS * WS * WS, ALU.mult, ALU.add).then_inc(vq_ready, 1)
                ch.link(dve.scalar_tensor_tensor(s2m[:, :, :], s2_ps, HD ** -0.5, repeat(mask[:, :], KV), ALU.mult, ALU.add))
                dve.wait_ge(rq_ready, t + 1)
                wait_used(dve, at_.e_ready, t, 1)
                ch.link(dve.tensor_tensor(at_.s[:, :, :], at_.sc, spread(rq[:, :], SEQ), ALU.mult))
                s4 = at_.s[:, :, :].rearrange("p (g r) s -> p g r s", r=REP)
                s2b = s2m[:, :, :].rearrange("p g (o s) -> p g o s", o=1).to_broadcast([P, KV, REP, SEQ])
                ch.link(dve.tensor_tensor(s4, s4, s2b, ALU.add))
                at_.take_max(dve, ch)
                if has_next:
                    keys_raw(t + 1)
                    rotate_query(t + 1, 0)
                at_.normalise(dve, ch, t)
                if has_next:
                    rotate_query(t + 1, 1)
                    rotate_query(t + 1, 2)
                    keys_scaled(t + 1)
                    rotate_query(t + 1, 3)
                at_.low(dve, t, 0)
                at_.low(dve, t, 1)
                at_.add(dve, ch, t)
            over_tiles(dve, head, step)

        @block.tensor
        def _(pe):
            def front(t, p):
                pe.wait_ge(ln.xl_ready, t + 1)
                for bank, wt, g, ready in ((1, wk, 0, k_ready), (2, wks, 1, ks_ready)):
                    wait_used(pe, uw_ready, t, 1, 4, g + 1)
                    wait_used(pe, sq_ready, t, 1, 4, g + 1)
                    for h in range(KV):
                        for c in range(KC):
                            cols = slice(h * HD, (h + 1) * HD)
                            last = mm3(pe, ps[:, bank, cols], (wt[0][:, c, cols], wt[1][:, c, cols]),
                                       ln.operand(p, c), c == 0, c == KC - 1)
                    last.then_inc(ready, 1)
                wait_used(pe, uw_ready, t, 1, 4, 3)
                wait_used(pe, sq_ready, t, 1, 4, 3)
                for c in range(KC):
                    last = mm3(pe, ps[:, 3, :], ln.operand(p, c), (wv[0][:, c, :], wv[1][:, c, :]), c == 0, c == KC - 1)
                last.then_inc(vp_ready, 1)
                pe.wait_ge(sqk_ready, t + 1)
                for h in range(KV):
                    last = pe.matmul(ps[:, 0, h:h + 1], sqk[:, h * P:(h + 1) * P], m.ones[:, 0:1], start=True, stop=True)
                last.then_inc(ksum_ready, 1)
                for g in range(4):
                    if g < 2:
                        pe.wait_ge(kraw_ready, t + 1)
                    elif g == 2:
                        pe.wait_ge(at_.v_ready, t + 1)
                    else:
                        pe.wait_ge(rkd_ready, t + 1)
                        pe.matmul(ps[:, 0, :], m.ones[:, :], rkd[:, :, :].rearrange("p h s -> p (h s)"),
                                  start=True, stop=True).then_inc(rkb_ready, 1)
                        pe.wait_ge(kt_ready, t + 1)
                    for h in range(4):
                        for c in range(KC):
                            cols = slice((4 * g + h) * HD, (4 * g + h + 1) * HD)
                            last = mm3(pe, ps[:, QBANK[g], h * P:(h + 1) * P], (wq[0][:, c, cols], wq[1][:, c, cols]),
                                       ln.operand(p, c), c == 0, c == KC - 1)
                    last.then_inc(q_ready, 1)

            def scores(t):
                pe.wait_ge(kt_ready, t + 1)
                pe.wait_ge(uw_ready, 4 * (t + 1))
                pe.wait_ge(sq_ready, 4 * (t + 1))
                wait_used(pe, at_.x_done, t, 1)
                for h in range(HEADS):
                    g = h // REP
                    for b in range(2):
                        rows, cols = slice(b * SEQ, (b + 1) * SEQ), slice(g * HD + b * SEQ, g * HD + (b + 1) * SEQ)
                        pe.matmul(at_.sc[rows, h, :], u[:, h, rows], kt[:, 0, cols], start=True, stop=False)
                        pe.matmul(at_.sc[rows, h, :], w[:, h, rows], kt[:, 1, cols], start=False, stop=True)
                wait_used(pe, at_.ol_ready, t, 1, 2)
                for g in range(KV):
                    for b in range(2):
                        rows, cols = slice(b * SEQ, (b + 1) * SEQ), slice(g * HD + b * SEQ, g * HD + (b + 1) * SEQ)
                        pe.matmul(s2_ps[rows, g, :], tab[:, BQ, :], kt[:, 0, cols], start=True, stop=True)
                for h in range(HEADS):
                    last = pe.matmul(var_ps[:, h:h + 1], sq[:, h, :], m.ones[:, 0:1], start=True, stop=True)
                last.then_inc(at_.sc_ready, 1)

            def head():
                ln.transpose(pe, 0, 0)
                front(0, 0)

            def step(t, p, has_next):
                if has_next:
                    pe.wait_ge(uw_ready, 4 * (t + 1))
                    pe.wait_ge(sq_ready, 4 * (t + 1))
                    ln.transpose(pe, t + 1, 1 - p)
                scores(t)
                if has_next:
                    front(t + 1, 1 - p)
                at_.transpose(pe, t)
                for parity in range(2):
                    at_.values(pe, t, p, parity)
                    at_.project(pe, t, parity)
            over_tiles(pe, head, step)
EXPERTS, RANK, LORA_SCALE = 8, 16, 2.0


def ffn_lora(m):
    nc, d = m.nc, m.d
    H1 = EXPERTS * RANK
    with ExitStack() as ctx:
        sb = lambda n, s, t=F32: ctx.enter_context(nc.sbuf_tensor("f0_" + n, s, t))
        sem = ctx.enter_context(Semaphores(nc, "f0_"))
        ps = ctx.enter_context(nc.psum_tensor("f0_ps", [P, 8, 512], F32))
        wb = [sb(f"wb{i}", [P, KC, DM], F16) for i in range(2)]
        wa = [sb(f"wa{i}", [P, KC, H1 + EXPERTS], F16) for i in range(2)]
        wB = [sb(f"wB{i}", [P, DM], F16) for i in range(2)]
        flat = lambda w: w[:, :, :].rearrange("p c n -> p (c n)")
        split_weights(m, [(d["ffn0_base"], flat(wb[0]), flat(wb[1]), 0), (d["ffn0_a"], flat(wa[0]), flat(wa[1]), 0),
                          (d["ffn0_b"], wB[0][:, :], wB[1][:, :], 0)], "f0")
        ln = LayerNorm(m, ctx, sem, "f0", ps[:, 0, :])
        desc = sb("desc", [P, EXPERTS])
        bias = sb("bias", [P, DM])
        top = sb("top", [P, 1])
        cand = sb("cand", [P, EXPERTS])
        first = sb("first", [P, 1])
        pick = sb("pick", [P, EXPERTS])
        hm = sb("hm", [P, 2, H1])
        hh = sb("hh", [P, 2, P], F16)
        hl = sb("hl", [P, 2, P], F16)
        y_ps = lambda p: ps[:, 1 + p, 0:DM]
        a_ps = lambda p: ps[:, 3 + p, 0:H1 + EXPERTS]
        ht_ps = lambda p: ps[:, 5 + p, 0:P]
        const_in, chain = sem("const_in"), sem("chain")
        a_ready, h_ready, ht_ready = sem("a_ready"), sem("h_ready"), sem("ht_ready")
        hh_ready, hl_ready, y_ready, x_done = sem("hh_ready"), sem("hl_ready"), sem("y_ready"), sem("x_done")
        block = ctx.enter_context(nc.Block())

        @block.sync
        def _(sp):
            sp.dma_start(desc[:, :], d["desc"]).then_inc(const_in, 16)
            sp.dma_start(bias[:, :], d["ffn0_bias"].to_broadcast([P, DM])).then_inc(const_in, 16)
            sp.wait_ge(const_in, 32)

        @block.gpsimd
        def _(pool):
            def step(t, p, has_next):
                if has_next:
                    ln.pool_step(pool, t + 1, 1 - p)
            over_tiles(pool, lambda: ln.pool(pool), step)

        @block.scalar
        def _(act):
            def step(t, p, has_next):
                if has_next:
                    ln.high(act, t + 1, 1 - p, y_ready)
                act.wait_ge(ht_ready, t + 1)
                wait_used(act, y_ready, t, 2)
                act.copy(hh[:, p], ht_ps(p)).then_inc(hh_ready, 1)
            over_tiles(act, lambda: ln.high(act, 0, 0, y_ready), step)

        @block.vector
        def _(dve):
            ch = Chain(dve, chain, 1, 6)

            def head():
                ln.stats(dve, ch, 0, 0)
                ln.normalise(dve, 0, 0)
                ln.low(dve, 0, 0)
                dve.wait_ge(const_in, 32)

            def step(t, p, has_next):
                ch.tile(t)
                if has_next:
                    ln.stats(dve, ch, t + 1, 1 - p)
                else:
                    ch.k += 0
                dve.wait_ge(a_ready, t + 1)
                logits = a_ps(p)[:, H1:]
                ch.link(dve.reduce_max(top[:, :], logits, AX))
                ch.link(dve.scalar_tensor_tensor(cand[:, :], logits, top[:, :], desc[:, :], ALU.is_ge, ALU.mult))
                ch.link(dve.reduce_max(first[:, :], cand[:, :], AX))
                ch.link(dve.tensor_scalar(pick[:, :], cand[:, :], first[:, :], LORA_SCALE / WS, ALU.is_equal, ALU.mult))
                wait_used(dve, ht_ready, t, 2)
                dve.tensor_tensor(hm[:, p].rearrange("p (e r) -> p e r", r=RANK),
                                  a_ps(p)[:, 0:H1].rearrange("p (e r) -> p e r", r=RANK),
                                  spread(pick[:, :], RANK),
                                  ALU.mult).then_inc(h_ready, 1)
                if has_next:
                    ln.normalise(dve, t + 1, 1 - p)
                    ln.low(dve, t + 1, 1 - p)
                dve.wait_ge(hh_ready, t + 1)
                dve.tensor_tensor(hl[:, p], ht_ps(p), hh[:, p], ALU.subtract).then_inc(hl_ready, 1)
                dve.wait_ge(y_ready, t + 1)
                x = m.x_all[:, at(t), :]
                ch.link(dve.scalar_tensor_tensor(x, y_ps(p), 1.0 / WS, x, ALU.mult, ALU.add))
                dve.tensor_tensor(x, x, bias[:, :], ALU.add).then_inc(x_done, 1)
            over_tiles(dve, head, step)

        @block.tensor
        def _(pe):
            def step(t, p, has_next):
                pe.wait_ge(ln.xl_ready, t + 1)
                wait_used(pe, h_ready, t, 2)
                for c in range(KC):
                    last = mm3(pe, a_ps(p), ln.operand(p, c), (wa[0][:, c], wa[1][:, c]), c == 0, c == KC - 1)
                last.then_inc(a_ready, 1)
                wait_used(pe, x_done, t, 2)
                for c in range(KC):
                    mm3(pe, y_ps(p), ln.operand(p, c), (wb[0][:, c], wb[1][:, c]), c == 0, False)
                if has_next:
                    ln.transpose(pe, t + 1, 1 - p)
                pe.wait_ge(h_ready, t + 1)
                wait_used(pe, hl_ready, t, 2)
                pe.transpose(ht_ps(p), hm[:, p], m.ident[:, :]).then_inc(ht_ready, 1)
                pe.wait_ge(hl_ready, t + 1)
                mm3(pe, y_ps(p), (hh[:, p], hl[:, p]), (wB[0][:, :], wB[1][:, :]), False, True).then_inc(y_ready, 1)
            over_tiles(pe, lambda: ln.transpose(pe, 0, 0), step)
XH = 8
XT = SEQ // XH
XU = 2 * XH
XG = 4
VC = XT + 1


def attention_features(m):
    nc, d = m.nc, m.d
    with ExitStack() as ctx:
        sb = lambda n, s, t=F32: ctx.enter_context(nc.sbuf_tensor("x0_" + n, s, t))
        sem = ctx.enter_context(Semaphores(nc, "x0_"))
        ps = ctx.enter_context(nc.psum_tensor("x0_ps", [P, 8, 512], F32))
        ln = LayerNorm(m, ctx, sem, "x0", ps[:, 0, :])
        self_ = sb("sel_f", [P, 4, XG * P])
        sel = sb("sel", [P, 4, XG, P], F16)
        one_row = sb("one_row", [P, 1])
        nident = sb("nident", [P, P], F16)
        xh = sb("xh", [P, 2, DM], F16)
        xl = sb("xl", [P, 2, DM], F16)
        cf = sb("cf", [P, 2, DM])
        chi = sb("chi", [P, DM], F16)
        clo = sb("clo", [P, DM], F16)
        vt = sb("vt", [P, 2, KC, XU, VC])
        q = sb("q", [P, 2, XG, DM], F16)
        k = sb("k", [P, 2, XG, DM], F16)
        mx = sb("mx", [P, KC, XG, P], F16)
        e = sb("e", [P, 4, KC, DM])
        rec = sb("rec", [P, KC, XU])
        o = sb("o", [P, KC, XU, XT])
        const_in, zeroed, sel_set = sem("const_in"), sem("zeroed"), sem("sel_set")
        c_in = [sem(f"c_in{i}") for i in range(2)]
        v_in = [sem(f"v_in{i}") for i in range(2)]
        chain, xs_ready, chi_ready, clo_ready = sem("chain"), sem("xs_ready"), sem("chi_ready"), sem("clo_ready")
        qsel, ksel, q1_ready, k_ready, s1_ready, mx_ready, nm_ready, q2_ready = (
            sem(n) for n in ("qsel", "ksel", "q1_ready", "k_ready", "s1_ready", "mx_ready", "nm_ready", "q2_ready"))
        s2_ready, e_ready, pv_ready, o_ready, ot_ready, x_done = (
            sem(n) for n in ("s2_ready", "e_ready", "pv_ready", "o_ready", "ot_ready", "x_done"))
        q_ps = ps[:, 0:2, :].rearrange("p b (g n) -> p (b g) n", n=DM)
        k_ps = ps[:, 2, :].rearrange("p (g n) -> p g n", n=DM)
        ot_ps = ps[:, 2, 0:DM]
        o_ps = ps[:, 3, 0:KC * XU * VC].rearrange("p (c u v) -> p c u v", c=KC, v=VC)
        s1_ps = lambda u: ps[:, 4 + u % 2, :].rearrange("p (c n) -> p c n", n=DM)
        s2_ps = lambda u: ps[:, 6 + u % 2, :]
        further = lambda t: not (isinstance(t, int) and t + 2 >= TILES)
        block = ctx.enter_context(nc.Block())

        @block.sync
        def _(sp):
            sp.dma_start(self_[:, :, :], d["x0_sel"]).then_inc(const_in, 16)
            sp.dma_start(one_row[:, :], d["x0_one"]).then_inc(const_in, 16)

            def load(t, p):
                wait_used(sp, clo_ready, t, 2)
                sp.dma_start(cf[:, p], dram_tile(d["ctx"], t)).then_inc(c_in[p], 16)
                wait_used(sp, pv_ready, t, 2, XU)
                sp.dma_start(vt[:, p].rearrange("p c u v -> p (c u v)"), dram_tile(d["ctx_v"], t)).then_inc(v_in[p], 16)

            def head():
                load(0, 0)
                load(1, 1)

            def step(t, p, has_next):
                if further(t):
                    load(t + 2, p)
            over_tiles(sp, head, step)
            for p in range(2):
                sp.wait_ge(v_in[p], 8 * TILES)

        @block.gpsimd
        def _(pool):
            def split_context(t, p):
                pool.wait_ge(c_in[p], (t - p) * 8 + 16)
                wait_used(pool, ksel, t, 1, 2)
                pool.tensor_tensor(chi[:, :], cf[:, p], m.ones2[:, :], ALU.mult).then_inc(chi_ready, 1)
                pool.wait_ge(chi_ready, t + 1)
                pool.tensor_tensor(clo[:, :], cf[:, p], chi[:, :], ALU.subtract).then_inc(clo_ready, 1)

            def head():
                ln.pool(pool)
                split_context(0, 0)
                ln.pool_step(pool, 1, 1)

            def step(t, p, has_next):
                if has_next:
                    split_context(t + 1, 1 - p)
                if further(t):
                    ln.pool_step(pool, t + 2, p)
            over_tiles(pool, head, step)

        @block.scalar
        def _(act):
            def operands(t, p):
                act.wait_ge(qsel, t + 1)
                wait_used(act, s2_ready, t, 2, XU)
                act.copy(q[:, p], q_ps).then_inc(q1_ready, 1)
                for r in range(2):
                    act.wait_ge(ksel, 2 * t + r + 1)
                    act.activation(k[:, p, 2 * r:2 * r + 2], k_ps, ACT.Identity, bias=one_row[:, :]).then_inc(k_ready, 1)

            def shifted(t, p):
                act.wait_ge(nm_ready, t + 1)
                act.copy(q[:, p], q_ps).then_inc(q2_ready, 1)

            def head():
                act.wait_ge(const_in, 32)
                operands(0, 0)
                shifted(0, 0)

            def step(t, p, has_next):
                if has_next:
                    operands(t + 1, 1 - p)
                for u in range(XU):
                    act.wait_ge(s2_ready, XU * t + u + 1)
                    if isinstance(t, int) and t == 0:
                        if u >= 4:
                            act.wait_ge(pv_ready, u - 3)
                    else:
                        act.wait_ge(pv_ready, XU * t + u - 3)
                    act.activation(e[:, u % 4].rearrange("p c n -> p (c n)"), s2_ps(u), ACT.Exp,
                                   scale=XT ** -0.5).then_inc(e_ready, 1)
                if has_next:
                    shifted(t + 1, 1 - p)
            over_tiles(act, head, step)

        @block.vector
        def _(dve):
            ch = Chain(dve, chain, 4, 3)

            def split_x(t, p):
                ln.stats(dve, ch, t, p)
                ln.normalise(dve, t, p)
                dve.wait_ge(ln.xn_ready, t + 1)
                wait_used(dve, qsel, t, 2)
                ch.link(dve.tensor_copy(xh[:, p], ln.xn[:, p]))
                dve.tensor_tensor(xl[:, p], ln.xn[:, p], xh[:, p], ALU.subtract).then_inc(xs_ready, 1)

            def maximum(t, u):
                dve.wait_ge(s1_ready, XU * t + u + 1)
                if u == 0:
                    wait_used(dve, nm_ready, t, 1)
                g, jj = divmod(u, 4)
                c = 32 * jj + 3 * XT
                dve.reduce_max(mx[:, :, g, c:c + 1].rearrange("p c o -> p (c o)"), s1_ps(u), AX).then_inc(mx_ready, 1)

            def normalise(t):
                dve.wait_ge(pv_ready, XU * (t + 1))
                wait_used(dve, ot_ready, t, 1)
                for c in range(KC):
                    last = dve.reciprocal(rec[:, c, :], o_ps[:, c, :, XT])
                ch.link(last)
                for c in range(KC):
                    last = dve.tensor_tensor(o[:, c], o_ps[:, c, :, 0:XT], spread(rec[:, c, :], XT), ALU.mult)
                last.then_inc(o_ready, 1)

            def finish(t):
                dve.wait_ge(ot_ready, t + 1)
                x = m.x_all[:, at(t), :]
                dve.tensor_tensor(x, x, ot_ps, ALU.add).then_inc(x_done, 1)

            def head():
                dve.memset(mx[:, :, :, :].rearrange("p a b c -> p (a b c)"), 0.0).then_inc(zeroed, 1)
                dve.wait_ge(const_in, 32)
                dve.tensor_scalar(nident[:, :], m.ident[:, :], -1.0, None, ALU.mult)
                dve.tensor_copy(sel[:, :, :, :].rearrange("p a g c -> p a (g c)"), self_[:, :, :]).then_inc(sel_set, 1)
                split_x(0, 0)
                split_x(1, 1)
                dve.wait_ge(zeroed, 1)
                for u in range(XU):
                    maximum(0, u)

            def step(t, p, has_next):
                ch.tile(t)
                if isinstance(t, int) and t == TILES - 1:
                    ch.base -= 2
                first = isinstance(t, int) and t == 0
                if not first:
                    normalise(t - 1)
                else:
                    ch.link(dve.memset(ln.turn[:, :], 0.0))
                for u in range(XU):
                    if has_next:
                        maximum(t + 1, u)
                    if u == 2 and not first:
                        finish(t - 1)
                    if u == 5 and further(t):
                        split_x(t + 2, p)
            over_tiles(dve, head, step)
            ch.base, ch.k = 4 + 3 * TILES - 2 * 2, 0
            normalise(TILES - 1)
            finish(TILES - 1)

        @block.tensor
        def _(pe):
            def select_q(t, p):
                pe.wait_ge(xs_ready, t + 1)
                wait_used(pe, q2_ready, t, 1)
                for g in range(XG):
                    pe.matmul(q_ps[:, g], sel[:, 0, g], xh[:, p], start=g % 2 == 0, stop=False, skip_group_check=True)
                    last = pe.matmul(q_ps[:, g], sel[:, 1, g], xl[:, p], start=False, stop=False, skip_group_check=True)
                last.then_inc(qsel, 1)

            def select_k(t):
                pe.wait_ge(clo_ready, t + 1)
                for r in range(2):
                    if r:
                        pe.wait_ge(k_ready, 2 * t + 1)
                    else:
                        wait_used(pe, x_done, t, 3)
                        wait_used(pe, k_ready, t, 1, 2)
                    for i in range(2):
                        g = 2 * r + i
                        pe.matmul(k_ps[:, i], sel[:, 2, g], chi[:, :], start=True, stop=False)
                        last = pe.matmul(k_ps[:, i], sel[:, 3, g], clo[:, :], start=False, stop=True)
                    last.then_inc(ksel, 1)

            def rows(u):
                g, jj = divmod(u, 4)
                return g, slice(32 * jj, 32 * jj + 32)

            def scores(t, p, u):
                g, r = rows(u)
                if u == 0:
                    pe.wait_ge(q1_ready, t + 1)
                if u % 8 == 0:
                    pe.wait_ge(k_ready, 2 * t + 1 + u // 8)
                if isinstance(t, int) and t == 0:
                    if u >= 2:
                        pe.wait_ge(mx_ready, u - 1)
                else:
                    pe.wait_ge(mx_ready, XU * t + u - 1)
                for c in range(KC):
                    last = pe.matmul(s1_ps(u)[:, c], q[r, p, g, c * P:(c + 1) * P], k[r, p, g], start=True, stop=True)
                last.then_inc(s1_ready, 1)

            def shifted_scores(t, p, u):
                g, r = rows(u)
                if u == 0:
                    pe.wait_ge(q2_ready, t + 1)
                if isinstance(t, int) and t == 0:
                    if u >= 2:
                        pe.wait_ge(e_ready, u - 1)
                else:
                    pe.wait_ge(e_ready, XU * t + u - 1)
                for c in range(KC):
                    last = pe.matmul(s2_ps(u)[:, c * DM:(c + 1) * DM], k[r, p, g, c * P:(c + 1) * P], q[r, p, g],
                                     start=True, stop=True)
                last.then_inc(s2_ready, 1)

            def values(t, p, u):
                pe.wait_ge(e_ready, XU * t + u + 1)
                if u == 0:
                    pe.wait_ge(v_in[p], (t - p) * 8 + 16)
                    wait_used(pe, o_ready, t, 1)
                for c in range(KC):
                    for n in range(KC):
                        last = pe.matmul(o_ps[:, c, u, :], e[:, u % 4, n, c * P:(c + 1) * P],
                                         vt[:, p, n, u, :], start=n == 0, stop=n == KC - 1)
                last.then_inc(pv_ready, 1)

            def add_maxima(t):
                pe.wait_ge(mx_ready, XU * (t + 1))
                pe.wait_ge(q1_ready, t + 1)
                for g in range(XG):
                    for c in range(KC):
                        last = pe.matmul(q_ps[:, g, c * P:(c + 1) * P], mx[:, c, g, :], nident[:, :],
                                         start=False, stop=True, skip_group_check=True)
                last.then_inc(nm_ready, 1)

            def head():
                pe.wait_ge(sel_set, 1)
                select_q(0, 0)
                select_k(0)
                for u in range(XU):
                    scores(0, 0, u)
                add_maxima(0)

            def transpose_out(t):
                pe.wait_ge(o_ready, t + 1)
                for c in range(KC):
                    last = pe.transpose(ot_ps[:, c * P:(c + 1) * P], o[:, c].rearrange("p u i -> p (u i)"), m.ident[:, :])
                last.then_inc(ot_ready, 1)

            def step(t, p, has_next):
                if has_next:
                    select_q(t + 1, 1 - p)
                    select_k(t + 1)
                for u in range(XU + 1):
                    if u < XU:
                        if has_next:
                            scores(t + 1, 1 - p, u)
                        shifted_scores(t, p, u)
                    if u == 1 and not (isinstance(t, int) and t == 0):
                        if has_next:
                            pe.wait_ge(k_ready, 2 * (t + 2))
                        transpose_out(t - 1)
                    if u:
                        values(t, p, u - 1)
                if has_next:
                    add_maxima(t + 1)
            over_tiles(pe, head, step)
            transpose_out(TILES - 1)
RMS_EPS = 1e-6
BR = 64


def bias_rows(m, jobs, tag):
    nc = m.nc
    with ExitStack() as ctx:
        n_all = sum(src.shape[1] for src, _ in jobs)
        stage = ctx.enter_context(nc.sbuf_tensor(f"bstage{tag}", [1, n_all], F32))
        sem = ctx.enter_context(Semaphores(nc, tag))
        loaded, zeroed, high_done = sem("b_loaded"), sem("b_zeroed"), sem("b_high")
        starts = [sum(src.shape[1] for src, _ in jobs[:i]) for i in range(len(jobs))]
        block = ctx.enter_context(nc.Block())

        @block.sync
        def _(sp):
            for (src, rows), s in zip(jobs, starts):
                sp.dma_start(stage[0:1, s:s + src.shape[1]], src).then_inc(loaded, 16)
            sp.wait_ge(loaded, 16 * len(jobs))

        @block.scalar
        def _(act):
            act.wait_ge(loaded, 16 * len(jobs))
            act.wait_ge(zeroed, len(jobs))
            for (src, rows), s in zip(jobs, starts):
                act.activation(rows[0:1, :], stage[0:1, s:s + src.shape[1]], ACT.Copy, scale=WS).then_inc(high_done, 1)

        @block.vector
        def _(dve):
            for _, rows in jobs:
                dve.memset(rows, 0.0).then_inc(zeroed, 1)
            for i, ((src, rows), s) in enumerate(zip(jobs, starts)):
                dve.wait_ge(high_done, i + 1)
                dve.scalar_tensor_tensor(rows[32:33, :], stage[0:1, s:s + src.shape[1]], WS, rows[0:1, :],
                                         ALU.mult, ALU.subtract)


def attention_cross(m):
    nc, d = m.nc, m.d
    NI = HEADS * HD
    with ExitStack() as ctx:
        sb = lambda n, s, t=F32: ctx.enter_context(nc.sbuf_tensor("x1_" + n, s, t))
        sem = ctx.enter_context(Semaphores(nc, "x1_"))
        ps = ctx.enter_context(nc.psum_tensor("x1_ps", [P, 8, 512], F32))
        wq, wk, wv = [[sb(f"{n}{i}", [P, KC, NI], F16) for i in range(2)] for n in ("wq", "wk", "wv")]
        wo = [sb(f"wo{i}", [P, HEADS * DM], F16) for i in range(2)]
        bq, bk, bv = (sb(n, [BR, NI], F16) for n in ("bq", "bk", "bv"))
        flat = lambda w: w[:, :, :].rearrange("p c n -> p (c n)")
        split_weights(m, [(d["x1_q"], flat(wq[0]), flat(wq[1]), 0), (d["x1_k"], flat(wk[0]), flat(wk[1]), 0),
                          (d["x1_v"], flat(wv[0]), flat(wv[1]), 0), (d["x1_o"], wo[0][:, :], wo[1][:, :], 0)], "x1")
        bias_rows(m, [(d["x1_bq"], bq[:, :]), (d["x1_bk"], bk[:, :]), (d["x1_bv"], bv[:, :])], "x1")
        ln = LayerNorm(m, ctx, sem, "x1", ps[:, 0, :])
        at_ = Attend(m, ctx, sem, "x1", ps, wo, NI)
        cf = sb("cf", [P, 2, KC, P])
        chi = sb("chi", [P, 2, KC, P], F16)
        clo = sb("clo", [P, 2, KC, P], F16)
        qs = sb("qs", [P, 2, HEADS])
        qk_scale = sb("qk_scale", [P, HEADS])
        bo = sb("bo", [P, DM])
        q = sb("q", [P, HEADS, P])
        k = sb("k", [P, HEADS, P])
        sq = sb("sq", [P, 4, 512])
        sum2 = sb("sum2", [P, 2, 512])
        sums = sb("sums", [P, 2, 512])
        var = sb("var", [P, SEQ + 1])
        rms = sb("rms", [P, SEQ + 1])
        const_in, scale_set, ctx_in = sem("const_in"), sem("scale_set"), [sem(f"ctx_in{i}") for i in range(2)]
        chain, pool_chain = sem("chain"), sem("pool_chain")
        chi_ready, clo_ready, proj_ready = sem("chi_ready"), sem("clo_ready"), sem("proj_ready")
        act_left, dve_left = sem("act_left"), sem("dve_left")
        sum2_ready, sums_ready, ss_ready, var_ready, rms_ready = (sem(n) for n in ("sum2_ready", "sums_ready", "ss_ready", "var_ready", "rms_ready"))
        at_.v_ready, at_.v_count = act_left, 12
        bank = lambda e: (e + 1) % 4
        block = ctx.enter_context(nc.Block())

        @block.sync
        def _(sp):
            sp.dma_start(qs[:, :, :], d["x1_scales"]).then_inc(const_in, 16)
            sp.dma_start(bo[:, :], d["x1_bo"].to_broadcast([P, DM])).then_inc(const_in, 16)

            def load_context(t, p):
                wait_used(sp, clo_ready, t, 2)
                sp.dma_start(cf[:, p].rearrange("p c s -> p (c s)"),
                             d["ctx_t"][at(t), :, :].rearrange("a p n -> p (a n)") if not isinstance(t, int)
                             else d["ctx_t"][t, :, :]).then_inc(ctx_in[p], 16)

            def head():
                load_context(0, 0)
                load_context(1, 1)
                at_.swap_values(sp, 0, 0)

            def step(t, p, has_next):
                if has_next:
                    if not (isinstance(t, int) and t + 2 >= TILES):
                        load_context(t + 2, p)
                    at_.swap_values(sp, t + 1, 1 - p)
            over_tiles(sp, head, step)
            sp.wait_ge(at_.vsw_ready, 32 * TILES)

        @block.gpsimd
        def _(pool):
            def split_context(t, p):
                pool.wait_ge(ctx_in[p], (t - p) * 8 + 16)
                wait_used(pool, proj_ready, t, 2, 12)
                pool.tensor_tensor(chi[:, p], cf[:, p], repeat(m.ones[:, :], KC), ALU.mult).then_inc(chi_ready, 1)
                pool.wait_ge(chi_ready, t + 1)
                pool.tensor_tensor(clo[:, p], cf[:, p], chi[:, p], ALU.subtract).then_inc(clo_ready, 1)

            def sum_squares(t, i):
                pool.wait_ge(act_left, 12 * t + 4 * i + 4)
                if not (isinstance(t, int) and t == 0 and i == 0):
                    pool.wait_ge(sums_ready, 2 * t + i)
                pool.tensor_tensor(sum2[:, :, :], sq[:, 0:2, :], sq[:, 2:4, :], ALU.add).then_inc(sum2_ready, 1)
                pool.wait_ge(sum2_ready, 2 * t + i + 1)
                wait_used(pool, ss_ready, t, 1)
                pool.tensor_tensor(sums[:, i, :], sum2[:, 0, :], sum2[:, 1, :], ALU.add).then_inc(sums_ready, 1)

            def front(t, p):
                sum_squares(t, 0)
                sum_squares(t, 1)
                pool.wait_ge(var_ready, t + 1)
                wait_used(pool, at_.e_ready, t, 1)
                pool.tensor_tensor(rms[:, :], var[:, :], m.mhalf[:, 0:1].to_broadcast([P, SEQ + 1]), ALU.pow).then_inc(rms_ready, 1)

            def head():
                ln.pool(pool)
                split_context(0, 0)
                front(0, 0)

            def step(t, p, has_next):
                if has_next:
                    ln.pool_step(pool, t + 1, 1 - p)
                    split_context(t + 1, 1 - p)
                    front(t + 1, 1 - p)
            over_tiles(pool, head, step)

        @block.scalar
        def _(act):
            def square(t, e):
                act.wait_ge(proj_ready, 12 * t + e + 1)
                if e >= 4:
                    act.wait_ge(sum2_ready, 2 * t + 1)
                else:
                    wait_used(act, sum2_ready, t, 1, 2)
                act.activation(sq[:, e % 4, :], ps[:, bank(e), :], ACT.Square).then_inc(act_left, 1)

            def value(t, p, g):
                act.wait_ge(proj_ready, 12 * t + 8 + g + 1)
                wait_used(act, at_.pv_ready, t, 2, 2)
                if not (isinstance(t, int) and t < 2):
                    act.wait_ge(at_.vsw_ready, 32 * (t - 1))
                act.activation(at_.v[:, p, g * 512:(g + 1) * 512], ps[:, bank(8 + g), :], ACT.Copy,
                               scale=1.0 / WS).then_inc(act_left, 1)

            def head():
                ln.high(act, 0, 0, proj_ready, 12)
                for e in range(8):
                    square(0, e)
                for g in range(4):
                    value(0, 0, g)

            def step(t, p, has_next):
                if has_next:
                    ln.high(act, t + 1, 1 - p, proj_ready, 12)
                    for e in range(3):
                        square(t + 1, e)
                act.wait_ge(rms_ready, t + 1)
                at_.exponential(act, t, rms[:, SEQ:SEQ + 1])
                if has_next:
                    for e in range(3, 8):
                        square(t + 1, e)
                    value(t + 1, 1 - p, 0)
                    value(t + 1, 1 - p, 1)
                at_.copy_transposed(act, t)
                if has_next:
                    value(t + 1, 1 - p, 2)
                    value(t + 1, 1 - p, 3)
                at_.high(act, t, 0)
                at_.high(act, t, 1)
            over_tiles(act, head, step)

        @block.vector
        def _(dve):
            ch = Chain(dve, chain, 1, 6)

            def leave(t, e):
                dve.wait_ge(act_left, 12 * t + e + 1)
                wait_used(dve, at_.sc_ready, t, 1)
                g = e % 4
                src = ps[:, bank(e), :].rearrange("p (h s) -> p h s", s=P)
                if e < 4:
                    ins = dve.tensor_tensor(q[:, 4 * g:4 * g + 4, :], src, spread(qk_scale[:, 4 * g:4 * g + 4], P), ALU.mult)
                else:
                    ins = dve.tensor_copy(k[:, 4 * g:4 * g + 4, :], src)
                ins.then_inc(dve_left, 1)

            def variances(t):
                dve.wait_ge(ss_ready, t + 1)
                wait_used(dve, rms_ready, t, 1)
                dve.tensor_scalar(var[:, 0:SEQ], ps[:, 1, 0:SEQ], 1.0 / NI, RMS_EPS * WS * WS, ALU.mult, ALU.add)
                dve.tensor_scalar(var[:, SEQ:], ps[:, 1, SEQ:SEQ + 1], HD / NI, HD * RMS_EPS * WS * WS,
                                  ALU.mult, ALU.add).then_inc(var_ready, 1)

            def head():
                dve.wait_ge(const_in, 32)
                dve.tensor_tensor(qk_scale[:, :], qs[:, 0, :], qs[:, 1, :], ALU.mult).then_inc(scale_set, 1)
                ln.stats(dve, ch, 0, 0)
                ln.normalise(dve, 0, 0)
                ln.low(dve, 0, 0)
                dve.wait_ge(scale_set, 1)
                for e in range(8):
                    leave(0, e)
                variances(0)

            def step(t, p, has_next):
                ch.tile(t)
                if has_next:
                    ln.stats(dve, ch, t + 1, 1 - p)
                    ln.normalise(dve, t + 1, 1 - p)
                    ln.low(dve, t + 1, 1 - p)
                dve.wait_ge(at_.sc_ready, t + 1)
                dve.wait_ge(rms_ready, t + 1)
                wait_used(dve, at_.e_ready, t, 1)
                ch.link(dve.tensor_tensor(at_.s[:, :, :], at_.sc, repeat(rms[:, 0:SEQ], HEADS), ALU.mult))
                at_.take_max(dve, ch)
                if has_next:
                    for e in range(0, 3):
                        leave(t + 1, e)
                at_.normalise(dve, ch, t)
                if has_next:
                    for e in range(3, 8):
                        leave(t + 1, e)
                at_.low(dve, t, 0)
                at_.low(dve, t, 1)
                at_.add(dve, ch, t, bo[:, :])
                if has_next:
                    variances(t + 1)
            over_tiles(dve, head, step)

        @block.tensor
        def _(pe):
            def project_heads(t, p, e, w, bias, operand):
                g = e % 4
                for h in range(4):
                    cols = slice((4 * g + h) * HD, (4 * g + h + 1) * HD)
                    out = ps[:, bank(e), h * P:(h + 1) * P]
                    for c in range(KC):
                        mm3(pe, out, (w[0][:, c, cols], w[1][:, c, cols]), operand(p, c), c == 0, False)
                    last = pe.matmul(out, bias[:, cols], m.onesh[0:BR, :], start=False, stop=True)
                last.then_inc(proj_ready, 1)

            def context(p, c):
                return chi[:, p, c, :], clo[:, p, c, :]

            def front(t, p):
                for e in range(12):
                    if e >= 4:
                        pe.wait_ge(dve_left, 8 * t + e - 3)
                    else:
                        wait_used(pe, act_left, t, 1, 12, 9 + e)
                    if e == 0:
                        wait_used(pe, var_ready, t, 1)
                    if e < 4:
                        pe.wait_ge(ln.xl_ready, t + 1)
                        project_heads(t, p, e, wq, bq, ln.operand)
                    elif e < 8:
                        pe.wait_ge(clo_ready, t + 1)
                        project_heads(t, p, e, wk, bk, context)
                    else:
                        cols = slice((e - 8) * 512, (e - 7) * 512)
                        out = ps[:, bank(e), :]
                        for c in range(KC):
                            mm3(pe, out, context(p, c), (wv[0][:, c, cols], wv[1][:, c, cols]), c == 0, False)
                        pe.matmul(out, m.onesh[0:BR, :], bv[:, cols], start=False, stop=True).then_inc(proj_ready, 1)

            def sums_of_squares(t):
                pe.wait_ge(sums_ready, 2 * (t + 1))
                pe.wait_ge(act_left, 12 * t + 9)
                for b in range(2):
                    for h in range(4):
                        cols = slice(h * P + b * SEQ, h * P + (b + 1) * SEQ)
                        pe.matmul(ps[b * SEQ:(b + 1) * SEQ, 1, 0:SEQ], m.ones[:, 0:SEQ], sums[:, 1, cols],
                                  start=h == 0, stop=h == 3)
                for h in range(4):
                    last = pe.matmul(ps[:, 1, SEQ:SEQ + 1], sums[:, 0, h * P:(h + 1) * P], m.ones[:, 0:1],
                                     start=h == 0, stop=h == 3)
                last.then_inc(ss_ready, 1)

            def scores(t):
                pe.wait_ge(dve_left, 8 * (t + 1))
                wait_used(pe, at_.x_done, t, 1)
                for h in range(HEADS):
                    for b in range(2):
                        rows = slice(b * SEQ, (b + 1) * SEQ)
                        last = pe.matmul(at_.sc[rows, h, :], q[:, h, rows], k[:, h, rows], start=True, stop=True)
                last.then_inc(at_.sc_ready, 1)

            def head():
                ln.transpose(pe, 0, 0)
                front(0, 0)
                sums_of_squares(0)

            def step(t, p, has_next):
                if has_next:
                    pe.wait_ge(act_left, 12 * (t + 1))
                    ln.transpose(pe, t + 1, 1 - p)
                scores(t)
                if has_next:
                    front(t + 1, 1 - p)
                at_.transpose(pe, t)
                for parity in range(2):
                    at_.values(pe, t, p, parity)
                    at_.project(pe, t, parity)
                if has_next:
                    sums_of_squares(t + 1)
            over_tiles(pe, head, step)
AH, AD = 16, 16
AG = P // AD


def attention_mqa(m):
    nc, d = m.nc, m.d
    with ExitStack() as ctx:
        sb = lambda n, s, t=F32: ctx.enter_context(nc.sbuf_tensor("a1_" + n, s, t))
        sem = ctx.enter_context(Semaphores(nc, "a1_"))
        ps = ctx.enter_context(nc.psum_tensor("a1_ps", [P, 8, 512], F32))
        wqk = [sb(f"wqk{i}", [P, KC, 3 * P], F16) for i in range(2)]
        wv = [sb(f"wv{i}", [P, KC, AD], F16) for i in range(2)]
        wo = [sb(f"wo{i}", [P, KC, DM], F16) for i in range(2)]
        flat = lambda w: w[:, :, :].rearrange("p c n -> p (c n)")
        split_weights(m, [(d["a1_qk"], flat(wqk[0]), flat(wqk[1]), 0), (d["a1_v"], flat(wv[0]), flat(wv[1]), 0),
                          (d["a1_o"], flat(wo[0]), flat(wo[1]), 0)], "a1")
        ln = LayerNorm(m, ctx, sem, "a1", ps[:, 0, :])
        at_ = Attend(m, ctx, sem, "a1", ps, wo, 2 * AD)
        at_.pv_count = 1
        qk_bias = sb("qk_bias", [P, 3])
        v_bias = sb("v_bias", [P, AD])
        o_bias = sb("o_bias", [P, DM])
        mask = sb("mask", [P, SEQ])
        own = sb("own", [P, AG])
        qk = sb("qk", [P, 2, 3, P])
        kd = sb("kd", [P, AG, P])
        vd = sb("vd", [P, 2, 2, 2, AD])
        o_sb = sb("o_sb", [P, DM])
        oh = sb("oh", [P, KC, P], F16)
        ol = sb("ol", [P, KC, P], F16)
        const_in, zeroed, chain = sem("const_in"), sem("zeroed"), sem("chain")
        proj_ready, qk_ready, kd_ready, vd_ready = sem("proj_ready"), sem("qk_ready"), sem("kd_ready"), sem("vd_ready")
        o_ready, ot_ready, oh_ready, ol_ready, y_ready, x_done = (
            sem(n) for n in ("o_ready", "ot_ready", "oth_ready", "otl_ready", "yp_ready", "x_added"))
        y = ps[:, 3, 0:DM]
        o_ps = ps[:, 6, 0:DM]
        ot_ps = ps[:, 7, 0:DM]
        block = ctx.enter_context(nc.Block())

        @block.sync
        def _(sp):
            sp.dma_start(qk_bias[:, :], d["a1_bqk"]).then_inc(const_in, 16)
            sp.dma_start(v_bias[:, :], d["a1_bv"].to_broadcast([P, AD])).then_inc(const_in, 16)
            sp.dma_start(o_bias[:, :], d["a1_bo"].to_broadcast([P, DM])).then_inc(const_in, 16)
            sp.dma_start(mask[:, :], d["causal"]).then_inc(const_in, 16)
            sp.dma_start(own[:, :], d["a1_own"]).then_inc(const_in, 16)
            sp.wait_ge(const_in, 80)

        @block.gpsimd
        def _(pool):
            def diagonal_keys(t, p):
                pool.wait_ge(qk_ready, t + 1)
                wait_used(pool, at_.sc_ready, t, 1)
                pool.tensor_tensor(kd[:, :, :], repeat(qk[:, p, 2, :], AG), spread(own[:, :], P), ALU.mult).then_inc(kd_ready, 1)

            def head():
                ln.pool(pool)
                pool.wait_ge(const_in, 80)
                diagonal_keys(0, 0)

            def step(t, p, has_next):
                if has_next:
                    ln.pool_step(pool, t + 1, 1 - p)
                    diagonal_keys(t + 1, 1 - p)
            over_tiles(pool, head, step)

        @block.scalar
        def _(act):
            def query_key(t, p):
                act.wait_ge(proj_ready, t + 1)
                wait_used(act, at_.sc_ready, t, 2)
                for c in range(3):
                    last = act.activation(qk[:, p, c, :], ps[:, 1 + p, c * P:(c + 1) * P], ACT.Identity,
                                          scale=1.0 / WS, bias=qk_bias[:, c:c + 1])
                last.then_inc(qk_ready, 1)

            def head():
                act.wait_ge(const_in, 80)
                ln.high(act, 0, 0, proj_ready)
                query_key(0, 0)

            def step(t, p, has_next):
                if has_next:
                    ln.high(act, t + 1, 1 - p, proj_ready)
                    query_key(t + 1, 1 - p)
                at_.exponential(act, t, AD ** -0.5)
                at_.copy_transposed(act, t)
                act.wait_ge(at_.pv_ready, t + 1)
                wait_used(act, ot_ready, t, 1)
                act.copy(o_sb[:, :], o_ps).then_inc(o_ready, 1)
                act.wait_ge(ot_ready, t + 1)
                wait_used(act, y_ready, t, 1)
                act.copy(oh[:, :, :].rearrange("p c s -> p (c s)"), ot_ps).then_inc(oh_ready, 1)
            over_tiles(act, head, step)

        @block.vector
        def _(dve):
            ch = Chain(dve, chain, 1, 6)

            def values(t, p):
                dve.wait_ge(qk_ready, t + 1)
                wait_used(dve, at_.pv_ready, t, 2)
                for b in range(2):
                    for parity in range(2):
                        src = slice(b * SEQ, (b + 1) * SEQ)
                        last = dve.scalar_tensor_tensor(
                            vd[parity * SEQ:(parity + 1) * SEQ, p, b, parity, :], ps[src, 1 + p, 3 * P:3 * P + AD],
                            1.0 / WS, v_bias[src, :], ALU.mult, ALU.add)
                last.then_inc(vd_ready, 1)

            def head():
                dve.memset(vd[:, :, :, :, :].rearrange("p a b c d -> p (a b c d)"), 0.0).then_inc(zeroed, 1)
                ln.stats(dve, ch, 0, 0)
                ln.normalise(dve, 0, 0)
                ln.low(dve, 0, 0)
                dve.wait_ge(const_in, 80)
                dve.wait_ge(zeroed, 1)
                values(0, 0)

            def step(t, p, has_next):
                ch.tile(t)
                if has_next:
                    ln.stats(dve, ch, t + 1, 1 - p)
                    ln.normalise(dve, t + 1, 1 - p)
                    ln.low(dve, t + 1, 1 - p)
                dve.wait_ge(at_.sc_ready, t + 1)
                wait_used(dve, at_.e_ready, t, 1)
                ch.link(dve.tensor_tensor(at_.s[:, :, :], at_.sc, repeat(mask[:, :], AH), ALU.add))
                at_.take_max(dve, ch)
                if has_next:
                    values(t + 1, 1 - p)
                at_.normalise(dve, ch, t)
                dve.wait_ge(oh_ready, t + 1)
                dve.tensor_tensor(ol[:, :, :].rearrange("p c s -> p (c s)"), ot_ps,
                                  oh[:, :, :].rearrange("p c s -> p (c s)"), ALU.subtract).then_inc(ol_ready, 1)
                dve.wait_ge(y_ready, t + 1)
                x = m.x_all[:, at(t), :]
                ch.link(dve.scalar_tensor_tensor(x, y, 1.0 / WS, x, ALU.mult, ALU.add))
                dve.tensor_tensor(x, x, o_bias[:, :], ALU.add).then_inc(x_done, 1)
            over_tiles(dve, head, step)

        @block.tensor
        def _(pe):
            def front(t, p):
                pe.wait_ge(ln.xl_ready, t + 1)
                wait_used(pe, vd_ready, t, 2)
                for j in range(3):
                    cols = slice(j * P, (j + 1) * P)
                    for c in range(KC):
                        mm3(pe, ps[:, 1 + p, cols], (wqk[0][:, c, cols], wqk[1][:, c, cols]), ln.operand(p, c),
                            c == 0, c == KC - 1)
                for c in range(KC):
                    last = mm3(pe, ps[:, 1 + p, 3 * P:3 * P + AD], ln.operand(p, c), (wv[0][:, c, :], wv[1][:, c, :]),
                               c == 0, c == KC - 1)
                last.then_inc(proj_ready, 1)

            def scores(t, p):
                pe.wait_ge(kd_ready, t + 1)
                wait_used(pe, at_.pt_ready, t, 1)
                for b in range(2):
                    rows = slice(b * SEQ, (b + 1) * SEQ)
                    for c in range(2):
                        last = pe.matmul(ps[rows, 4 + c, :].rearrange("p (h s) -> p h s", s=SEQ), qk[:, p, c, rows],
                                         kd[:, :, rows], start=True, stop=True)
                last.then_inc(at_.sc_ready, 1)

            def head():
                ln.transpose(pe, 0, 0)
                front(0, 0)

            def step(t, p, has_next):
                scores(t, p)
                if has_next:
                    ln.transpose(pe, t + 1, 1 - p)
                    front(t + 1, 1 - p)
                at_.transpose(pe, t)
                pe.wait_ge(at_.pt_ready, t + 1)
                pe.wait_ge(vd_ready, t + 1)
                wait_used(pe, o_ready, t, 1)
                for b in range(2):
                    rows = slice(b * SEQ, (b + 1) * SEQ)
                    for k in range(PAIRS):
                        last = pe.matmul(o_ps[rows, k * 2 * AD:(k + 1) * 2 * AD], at_.pt[:, k, rows],
                                         vd[:, p, b, :, :].rearrange("p a d -> p (a d)"), start=True, stop=True)
                last.then_inc(at_.pv_ready, 1)
                pe.wait_ge(o_ready, t + 1)
                wait_used(pe, ol_ready, t, 1)
                for c in range(KC):
                    last = pe.transpose(ot_ps[:, c * P:(c + 1) * P], o_sb[:, c * P:(c + 1) * P], m.ident[:, :])
                last.then_inc(ot_ready, 1)
                pe.wait_ge(ol_ready, t + 1)
                wait_used(pe, x_done, t, 1)
                for c in range(KC):
                    last = mm3(pe, y, (oh[:, c, :], ol[:, c, :]), (wo[0][:, c, :], wo[1][:, c, :]), c == 0, c == KC - 1)
                last.then_inc(y_ready, 1)
            over_tiles(pe, head, step)


FF = 704
QMAX, Q_EPS = 127.0, 1e-8
ROUND = 1.5 * 2.0 ** 23


def ffn_quantised(m):
    nc, d = m.nc, m.d
    G1, C2 = 2 * FF // P, -(-FF // P)
    tail = FF - (C2 - 1) * P
    with ExitStack() as ctx:
        sb = lambda n, s, t=F32: ctx.enter_context(nc.sbuf_tensor("f1_" + n, s, t))
        sem = ctx.enter_context(Semaphores(nc, "f1_"))
        ps = ctx.enter_context(nc.psum_tensor("f1_ps", [P, 8, 512], F32))
        w1 = sb("w1", [P, KC, 2 * FF], BF16)
        w2 = sb("w2", [P, C2, DM], BF16)
        s1 = sb("s1", [P, 2 * FF])
        s2 = sb("s2", [P, DM])
        with ExitStack() as c1:
            quantise_weights(m, c1, ps, w1, w2, s1, s2)
        ln = LayerNorm(m, ctx, sem, "f1", ps[:, 0, :])
        stat = sb("stat", [P, 2, 3])
        hstat = sb("hstat", [P, 3])
        xr = sb("xr", [P, DM])
        xq = sb("xq", [P, 2, DM], BF16)
        xt = sb("xt", [P, 2, KC, P], BF16)
        gate = sb("gate", [P, FF])
        up = sb("up", [P, FF])
        ex = sb("ex", [P, FF])
        hq = sb("hq", [P, C2 * P], BF16)
        ht = sb("ht", [P, C2, P], BF16)
        yt = sb("yt", [P, DM])
        chain, zeroed, gup = sem("chain"), sem("zeroed"), sem("gup_ready")
        xq_ready, xtp_ready, xt_ready, gu_ready, gate_ready, up_ready, ex_ready, hq_ready = (
            sem(n) for n in ("xq_ready", "xtp_ready", "xt_ready", "gu_ready", "gate_ready", "up_ready", "ex_ready", "hq_ready"))
        htp_ready, ht_ready, y_ready, x_done, den_ready = (sem(n) for n in ("htp_ready", "ht_ready", "y_ready", "x_done", "den_ready"))
        HF = FF // 2
        gate_ps, up_ps = ps[:, 1:3, 0:HF], ps[:, 3:5, 0:HF]
        xt_ps = ps[:, 0, 0:DM // 2].bitcast(BF16)
        ht_ps = ps[:, 5, 0:C2 * P // 2].bitcast(BF16)
        y_ps = lambda p: ps[:, 6 + p, 0:DM]
        halves = lambda a: a.rearrange("p (k n) -> p k n", k=2)
        block = ctx.enter_context(nc.Block())

        @block.gpsimd
        def _(pool):
            def step(t, p, has_next):
                if has_next:
                    ln.pool_step(pool, t + 1, 1 - p)
                pool.wait_ge(up_ready, t + 1)
                pool.wait_ge(ex_ready, t + 1)
                pool.tensor_tensor(gate[:, :], gate[:, :], up[:, :], ALU.mult).then_inc(gup, 1)
            over_tiles(pool, lambda: ln.pool(pool), step)

        @block.scalar
        def _(act):
            def x_transposed(t, p):
                act.wait_ge(xtp_ready, t + 1)
                wait_used(act, gu_ready, t, 2)
                act.copy(xt[:, p].rearrange("p c s -> p (c s)"), xt_ps).then_inc(xt_ready, 1)

            def step(t, p, has_next):
                act.wait_ge(gate_ready, t + 1)
                wait_used(act, hq_ready, t, 1)
                act.activation(ex[:, :], gate[:, :], ACT.Exp, scale=-1.0).then_inc(ex_ready, 1)
                if has_next:
                    x_transposed(t + 1, 1 - p)
                act.wait_ge(htp_ready, t + 1)
                wait_used(act, y_ready, t, 1)
                act.copy(ht[:, :, :].rearrange("p c s -> p (c s)"), ht_ps).then_inc(ht_ready, 1)
            over_tiles(act, lambda: x_transposed(0, 0), step)

        @block.vector
        def _(dve):
            ch = Chain(dve, chain, 5, 14)

            def scale(v, st):
                ch.link(dve.tensor_reduce(st[:, 0:1], v, AX, ALU.max, apply_absolute_value=True))
                ch.link(dve.tensor_scalar(st[:, 1:2], st[:, 0:1], 1.0 / QMAX, Q_EPS, ALU.mult, ALU.max))
                ch.link(dve.reciprocal(st[:, 2:3], st[:, 1:2]))

            def quantise_x(t, p):
                ln.stats(dve, ch, t, p)
                ln.normalise(dve, t, p)
                dve.wait_ge(ln.xn_ready, t + 1)
                scale(ln.xn[:, p], stat[:, p])
                ch.link(dve.tensor_scalar(xr[:, :], ln.xn[:, p], stat[:, p, 2:3], ROUND, ALU.mult, ALU.add))
                wait_used(dve, xtp_ready, t, 2)
                dve.tensor_scalar(xq[:, p], xr[:, :], -ROUND, None, ALU.add).then_inc(xq_ready, 1)

            def head():
                dve.memset(hq[:, :], 0.0).then_inc(zeroed, 1)
                dve.wait_ge(zeroed, 1)
                quantise_x(0, 0)

            def step(t, p, has_next):
                ch.tile(t)
                dve.wait_ge(gu_ready, t + 1)
                wait_used(dve, hq_ready, t, 1)
                dve.scalar_tensor_tensor(halves(gate[:, :]), gate_ps, stat[:, p, 1:2], halves(s1[:, 0:FF]),
                                         ALU.mult, ALU.mult).then_inc(gate_ready, 1)
                dve.scalar_tensor_tensor(halves(up[:, :]), up_ps, stat[:, p, 1:2], halves(s1[:, FF:]),
                                         ALU.mult, ALU.mult).then_inc(up_ready, 1)
                if has_next:
                    quantise_x(t + 1, 1 - p)
                dve.wait_ge(ex_ready, t + 1)
                ch.link(dve.tensor_scalar(ex[:, :], ex[:, :], 1.0, None, ALU.add))
                ch.link(dve.reciprocal(ex[:, :], ex[:, :]))
                dve.wait_ge(gup, t + 1)
                ch.link(dve.tensor_tensor(gate[:, :], gate[:, :], ex[:, :], ALU.mult))
                scale(gate[:, :], hstat[:, :])
                ch.link(dve.tensor_scalar(gate[:, :], gate[:, :], hstat[:, 2:3], ROUND, ALU.mult, ALU.add))
                wait_used(dve, htp_ready, t, 1)
                dve.tensor_scalar(hq[:, 0:FF], gate[:, :], -ROUND, None, ALU.add).then_inc(hq_ready, 1)
                dve.wait_ge(y_ready, t + 1)
                ch.link(dve.scalar_tensor_tensor(yt[:, :], y_ps(p), hstat[:, 1:2], s2[:, :], ALU.mult, ALU.mult))
                x = m.x_all[:, at(t), :]
                ch.link(dve.tensor_tensor(x, x, yt[:, :], ALU.add))
                dve.memset(ln.turn[:, :], 0.0).then_inc(x_done, 1)
            over_tiles(dve, head, step)

        @block.tensor
        def _(pe):
            def x_transpose(t, p):
                pe.wait_ge(xq_ready, t + 1)
                wait_used(pe, xt_ready, t, 1)
                for c in range(KC):
                    last = pe.transpose(xt_ps[:, c * P:(c + 1) * P], xq[:, p, c * P:(c + 1) * P], m.identb[:, :])
                last.then_inc(xtp_ready, 1)

            def step(t, p, has_next):
                pe.wait_ge(xt_ready, t + 1)
                wait_used(pe, up_ready, t, 1)
                for c in range(KC):
                    for k in range(4):
                        last = pe.matmul(ps[:, 1 + k, 0:HF], xt[:, p, c, :], w1[:, c, k * HF:(k + 1) * HF],
                                         start=c == 0, stop=c == KC - 1)
                last.then_inc(gu_ready, 1)
                if has_next:
                    x_transpose(t + 1, 1 - p)
                pe.wait_ge(hq_ready, t + 1)
                wait_used(pe, ht_ready, t, 1)
                for c in range(C2):
                    last = pe.transpose(ht_ps[:, c * P:(c + 1) * P], hq[:, c * P:(c + 1) * P], m.identb[:, :])
                last.then_inc(htp_ready, 1)
                pe.wait_ge(ht_ready, t + 1)
                wait_used(pe, x_done, t, 2)
                for c in range(C2):
                    k = P if c < C2 - 1 else tail
                    last = pe.matmul(y_ps(p), ht[0:k, c, :], w2[0:k, c, :], start=c == 0, stop=c == C2 - 1)
                last.then_inc(y_ready, 1)
            over_tiles(pe, lambda: x_transpose(0, 0), step)


def quantise_weights(m, ctx, ps, w1, w2, s1, s2):
    nc, d = m.nc, m.d
    G1, C2 = 2 * FF // P, -(-FF // P)
    sb = lambda n, s, t=F32: ctx.enter_context(nc.sbuf_tensor("fw_" + n, s, t))
    sem = ctx.enter_context(Semaphores(nc, "fw_"))
    wa = sb("wa", [P, G1, DM])
    wb = sb("wb", [P, KC, FF])
    qa = sb("qa", [P, G1, DM], BF16)
    qb = sb("qb", [P, KC, FF], BF16)
    NS = G1 + KC
    st = sb("st", [P, 3, NS])
    diag = sb("diag", [P, NS, P])
    loaded, chain, q_ready, diag_ready = sem("loaded"), sem("chain"), sem("q_ready"), sem("diag_ready")
    t_ready, t_left, r_ready, r_left = sem("t_ready"), sem("t_left"), sem("r_ready"), sem("r_left")
    jobs = [(qa[:, j, c * P:(c + 1) * P], P, w1[:, c, j * P:(j + 1) * P]) for j in range(G1) for c in range(KC)]
    jobs += [(qb[:, j, c * P:min(FF, (c + 1) * P)], min(FF, (c + 1) * P) - c * P, w2[0:min(FF, (c + 1) * P) - c * P, c, j * P:(j + 1) * P])
             for j in range(KC) for c in range(C2)]
    rows = [s1[:, j * P:(j + 1) * P] for j in range(G1)] + [s2[:, j * P:(j + 1) * P] for j in range(KC)]
    block = ctx.enter_context(nc.Block())

    @block.sync
    def _(sp):
        sp.dma_start(wa[:, :, :], d["f1_gu"].rearrange("p (j n) -> p j n", n=DM)).then_inc(loaded, 16)
        sp.dma_start(wb[:, :, :], d["f1_down"].rearrange("p (j n) -> p j n", n=FF)).then_inc(loaded, 16)
        sp.wait_ge(loaded, 32)

    @block.vector
    def _(dve):
        k = [0]

        def link(ins):
            k[0] += 1
            ins.then_inc(chain, 1)
            dve.wait_ge(chain, k[0])

        dve.wait_ge(loaded, 32)
        dve.tensor_reduce(st[:, 0, 0:G1], wa[:, :, :], AX, ALU.max, apply_absolute_value=True)
        link(dve.tensor_reduce(st[:, 0, G1:], wb[:, :, :], AX, ALU.max, apply_absolute_value=True))
        link(dve.tensor_scalar(st[:, 1, :], st[:, 0, :], 1.0 / QMAX, Q_EPS, ALU.mult, ALU.max))
        link(dve.reciprocal(st[:, 2, :], st[:, 1, :]))
        for j in range(G1):
            dve.tensor_scalar(wa[:, j, :], wa[:, j, :], st[:, 2, j:j + 1], ROUND, ALU.mult, ALU.add)
        for j in range(KC):
            last = dve.tensor_scalar(wb[:, j, :], wb[:, j, :], st[:, 2, G1 + j:G1 + j + 1], ROUND, ALU.mult, ALU.add)
        link(last)
        dve.tensor_scalar(qa[:, :, :], wa[:, :, :], -ROUND, None, ALU.add)
        dve.tensor_scalar(qb[:, :, :], wb[:, :, :], -ROUND, None, ALU.add).then_inc(q_ready, 1)
        dve.tensor_tensor(diag[:, :, :], repeat(m.ident[:, :], NS), spread(st[:, 1, :], P), ALU.mult).then_inc(diag_ready, 1)
        for i, (_, n, dst) in enumerate(jobs):
            dve.wait_ge(t_ready, i + 1)
            dve.tensor_copy(dst, ps[0:n, i % 4, 0:P // 2].bitcast(BF16)).then_inc(t_left, 1)

    @block.scalar
    def _(act):
        for i, dst in enumerate(rows):
            act.wait_ge(r_ready, i + 1)
            act.copy(dst, ps[:, 4 + i % 4, 0:P]).then_inc(r_left, 1)

    @block.tensor
    def _(pe):
        pe.wait_ge(q_ready, 1)
        for i, (src, n, _) in enumerate(jobs):
            if i >= 4:
                pe.wait_ge(t_left, i - 3)
            pe.transpose(ps[0:n, i % 4, 0:P // 2].bitcast(BF16), src, m.identb[:, :]).then_inc(t_ready, 1)
        pe.wait_ge(diag_ready, 1)
        for i in range(NS):
            if i >= 4:
                pe.wait_ge(r_left, i - 3)
            pe.matmul(ps[:, 4 + i % 4, 0:P], m.ones[:, :], diag[:, i, :], start=True, stop=True).then_inc(r_ready, 1)


BUILDERS = {0: attention_gqa, 1: attention_features, 2: ffn_lora, 3: attention_mqa, 4: attention_cross, 5: ffn_quantised}


def decoder_kernel(nc, d):
    with ExitStack() as ctx:
        m = Machine(nc, ctx, d)
        load_resident(m)
        for phase in PHASES:
            BUILDERS[phase](m)
        store_result(m)


def host_layout(i):
    f = lambda a: np.ascontiguousarray(a)
    a = {k: np.asarray(v) for k, v in i.items()}
    kmajor = lambda w: f(w.reshape(KC, P, -1).transpose(1, 0, 2).reshape(P, -1))
    out = {"x": f(a["x"].reshape(-1, DM)), "ident": np.eye(P, dtype=np.float32)}
    out["ffn0_base"] = kmajor(a["L0_ffn_W_base"].T)
    out["ffn0_a"] = kmajor(np.concatenate([a["L0_ffn_A"].reshape(-1, DM).T, a["L0_ffn_router_W"].T], 1))
    out["ffn0_b"] = f(a["L0_ffn_Bw"].transpose(0, 2, 1).reshape(P, DM))
    out["ffn0_bias"] = f(a["L0_ffn_b_base"].reshape(1, DM))
    out["desc"] = np.broadcast_to(np.arange(EXPERTS, 0, -1, dtype=np.float32), (P, EXPERTS)).copy()
    qkv = a["L0_attn_w_qkv"]
    nq, nk = HEADS * HD, KV * HD
    swap = lambda v, axis=0: np.concatenate(np.split(v, 2, axis)[::-1], axis)
    wk = qkv[nq:nq + nk]
    out["a0_q"] = kmajor(qkv[:nq].T)
    out["a0_k"] = kmajor(wk.T)
    out["a0_ks"] = kmajor(swap(wk.reshape(KV, HD, DM), 1).reshape(nk, DM).T)
    out["a0_v"] = kmajor(qkv[nq + nk:].T)
    out["a0_o"] = f(a["L0_attn_w_o"].T.reshape(HEADS, HD, DM).transpose(1, 0, 2).reshape(P, -1))
    qg, qb, kg, kb = (a["L0_attn_" + n] for n in ("qn_g", "qn_b", "kn_g", "kn_b"))
    out["a0_gb"] = f(np.stack([qg, qb, swap(qb), kg, kb, swap(kg), swap(kb), kb], 1))
    inv = (1.0 / np.float32(1e6) ** (np.arange(0, HD, 2, dtype=np.float32) / np.float32(HD))).astype(np.float32)
    ang = np.concatenate([inv, inv])[:, None] * np.arange(SEQ, dtype=np.float32)[None]
    sgn = np.where(np.arange(HD) < HD // 2, -1.0, 1.0)[:, None]
    out["rope"] = np.stack([np.cos(ang), sgn * np.sin(ang), -sgn * np.sin(ang)], 1).astype(np.float32)
    out["causal"] = np.tile(np.triu(np.full((SEQ, SEQ), NEG), 1), (2, 1)).astype(np.float32)
    x1 = {n: a["L1_xattn_" + n] for n in ("q_w", "ki_w", "vi_w", "o_w", "q_b", "ki_b", "vi_b", "o_b", "nq_s", "nki_s")}
    for n, k in (("q", "q_w"), ("k", "ki_w"), ("v", "vi_w")):
        out["x1_" + n] = kmajor(x1[k])
    out["x1_o"] = f(x1["o_w"].reshape(HEADS, HD, DM).transpose(1, 0, 2).reshape(P, -1))
    for n, k in (("bq", "q_b"), ("bk", "ki_b"), ("bv", "vi_b"), ("bo", "o_b")):
        out["x1_" + n] = f(x1[k].reshape(1, -1))
    out["x1_scales"] = f(np.stack([x1["nq_s"].reshape(HEADS, HD).T, x1["nki_s"].reshape(HEADS, HD).T], 1))
    c = a["ctx_2048"].reshape(-1, P, DM)
    out["ctx_t"] = f(c.transpose(0, 2, 1).reshape(-1, KC, P, P).transpose(0, 2, 1, 3).reshape(-1, P, DM))
    out["ctx"] = f(c)
    v = c.transpose(0, 2, 1).reshape(-1, KC, P, XU, XT).transpose(0, 2, 1, 3, 4)
    out["ctx_v"] = f(np.concatenate([v, np.ones_like(v[..., :1])], -1).reshape(-1, P, KC * XU * VC))
    sel = np.zeros((P, 4, XG, 4, 32), np.float32)
    one = np.zeros((4, 32, 1), np.float32)
    one[:, 3 * XT] = 1.0
    for tok in range(P):
        g, jj, i = tok // 32, tok % 32 // XT, tok % XT
        for part, thirds in enumerate(((0, 1), (2,), (0, 2), (1,))):
            for r in thirds:
                sel[tok, part, g, jj, r * XT + i] = 1.0
    out["x0_sel"] = sel.reshape(P, 4, XG * P)
    out["x0_one"] = one.reshape(P, 1)
    w1 = a["L1_attn_Wqkv_w"]
    bias = a["L1_attn_Wqkv_b"]
    wk = np.tile(w1[DM:DM + AD], (AG, 1))
    out["a1_qk"] = kmajor(np.concatenate([w1[:DM], wk], 0).T)
    out["a1_v"] = kmajor(w1[DM + AD:].T)
    out["a1_o"] = kmajor(a["L1_attn_out_w"].T)
    out["a1_bqk"] = f(np.concatenate([bias[:DM], np.tile(bias[DM:DM + AD], AG)]).reshape(3, P).T)
    out["a1_bv"] = f(bias[DM + AD:].reshape(1, AD))
    out["a1_bo"] = f(a["L1_attn_out_b"].reshape(1, DM))
    out["a1_own"] = np.kron(np.eye(AG), np.ones((AD, 1))).astype(np.float32)
    rows = lambda w: f(w.reshape(-1, P, w.shape[1]).transpose(1, 0, 2).reshape(P, -1))
    out["f1_gu"] = rows(a["L1_ffn_w_gate_up"])
    out["f1_down"] = rows(a["L1_ffn_w_down"])
    return out


def kernel(**inputs):
    import concourse.bacc as _bacc
    from concourse.bass_utils import run_bass_kernel_spmd as _run

    nc = _bacc.Bacc("TRN2", target_bir_lowering=False, num_devices=1)
    arrays, d = {}, {}
    for name, a in host_layout(inputs).items():
        arrays[f"in_{name}"] = a
        d[name] = nc.dram_tensor(f"in_{name}", a.shape, F32, kind="ExternalInput").ap()
    d["out"] = nc.dram_tensor("out_x", (64 * SEQ, DM), F32, kind="ExternalOutput").ap()
    decoder_kernel(nc, d)
    r = _run(nc, [arrays], core_ids=[0])
    return r.results[0]["out_x"].reshape(64, SEQ, DM)
```

```python
from contextlib import ExitStack

import numpy as np
import concourse.bass as bass
from concourse import mybir
from concourse.alu_op_type import AluOpType as ALU

F32 = mybir.dt.float32
F16 = mybir.dt.float16
BF16 = mybir.dt.bfloat16
ACT = mybir.ActivationFunctionType
AX = mybir.AxisListType.X

P = 128
TILES = 32
SEQ = 64
DM = 256
KC = DM // P
WS = 64.0
LN_EPS = 1e-5
NEG = -1.0e30
PHASES = (0, 1, 2, 3, 4, 5)


def over_tiles(eng, head, step):
    head()
    step(0, 0, True)
    step(1, 1, TILES > 2)
    if TILES > 4:
        with eng.Fori(1, TILES // 2 - 1) as i:
            step(2 * i, 0, True)
            step(2 * i + 1, 1, True)
    if TILES > 2:
        step(TILES - 2, 0, True)
        step(TILES - 1, 1, False)


def wait_used(eng, sem, t, buffers, per_tile=1, last=0):
    if isinstance(t, int) and t < buffers:
        return
    eng.wait_ge(sem, (t - buffers) * per_tile + (last or per_tile))


class Semaphores:

    def __init__(self, nc, tag):
        self.nc, self.tag, self.stack, self.all = nc, tag, ExitStack(), []

    def __enter__(self):
        return self

    def __call__(self, name):
        self.all.append(self.stack.enter_context(self.nc.semaphore(self.tag + name)))
        return self.all[-1]

    def __exit__(self, *error):
        if error[0] is None:
            with self.nc.Block() as block:
                @block.sync
                def _(sp):
                    for s in self.all:
                        sp.sem_clear(s)
        self.stack.close()


class Chain:

    def __init__(self, eng, sem, head, each, ahead=0):
        self.eng, self.sem, self.head, self.each, self.ahead, self.k, self.base = eng, sem, head, each, ahead, 0, 0

    def tile(self, t):
        assert not isinstance(t, int) or t or self.k == self.head
        self.base, self.k = self.head + t * self.each, 0
        if isinstance(t, int) and t == TILES - 1:
            self.base -= self.ahead

    def link(self, ins):
        ins.then_inc(self.sem, 1)
        self.k += 1
        self.eng.wait_ge(self.sem, self.base + self.k)


def mm3(pe, out, a, b, start, stop):
    pe.matmul(out, a[0], b[0], start=start, stop=False)
    pe.matmul(out, a[0], b[1], start=False, stop=False)
    return pe.matmul(out, a[1], b[0], start=False, stop=stop)


class Machine:

    def __init__(self, nc, ctx, d):
        self.nc, self.d = nc, d
        self.x_all = ctx.enter_context(nc.sbuf_tensor("x_all", [P, TILES, DM], F32))
        self.ident = ctx.enter_context(nc.sbuf_tensor("ident", [P, P], F32))
        self.identb = ctx.enter_context(nc.sbuf_tensor("identb", [P, P], BF16))
        self.ones = ctx.enter_context(nc.sbuf_tensor("ones", [P, P], F32))
        self.ones2 = ctx.enter_context(nc.sbuf_tensor("ones2", [P, DM], F32))
        self.onesh = ctx.enter_context(nc.sbuf_tensor("onesh", [P, P], F16))
        self.onesb = ctx.enter_context(nc.sbuf_tensor("onesb", [P, 1], BF16))
        self.mhalf = ctx.enter_context(nc.sbuf_tensor("mhalf", [P, 32], F32))


def load_resident(m):
    nc = m.nc
    with ExitStack() as ctx:
        sem = ctx.enter_context(Semaphores(nc, "in_"))
        x_in, id_in = sem("x_in"), sem("id_in")
        block = ctx.enter_context(nc.Block())

        @block.sync
        def _(sp):
            sp.dma_start(m.ident[:, :], m.d["ident"]).then_inc(id_in, 16)
            for s in range(0, TILES, 4 if TILES >= 4 else TILES):
                n = min(4, TILES)
                sp.dma_start(m.x_all[:, s:s + n, :],
                             m.d["x"][s * P:(s + n) * P, :].rearrange("(t p) d -> p t d", p=P)).then_inc(x_in, 16)
            sp.wait_ge(x_in, 16 * (TILES // min(4, TILES)))

        @block.vector
        def _(dve):
            dve.memset(m.ones[:, :], 1.0)
            dve.memset(m.onesh[:, :], 1.0)
            dve.memset(m.onesb[:, :], 1.0)
            dve.memset(m.ones2[:, :], 1.0)
            dve.memset(m.mhalf[:, :], -0.5)
            dve.wait_ge(id_in, 16)
            dve.tensor_copy(m.identb[:, :], m.ident[:, :])


def store_result(m):
    nc = m.nc
    with ExitStack() as ctx:
        sem = ctx.enter_context(Semaphores(nc, "out_"))
        x_out = sem("x_out")
        block = ctx.enter_context(nc.Block())

        @block.sync
        def _(sp):
            n = min(4, TILES)
            for s in range(0, TILES, n):
                sp.dma_start(m.d["out"][s * P:(s + n) * P, :].rearrange("(t p) d -> p t d", p=P),
                             m.x_all[:, s:s + n, :]).then_inc(x_out, 16)
            sp.wait_ge(x_out, 16 * (TILES // n))


STAGE = 2048


def split_weights(m, jobs, tag):
    nc = m.nc
    with ExitStack() as ctx:
        stage = [ctx.enter_context(nc.sbuf_tensor(f"stage{tag}{i}", [P, STAGE], F32)) for i in range(3)]
        mean = ctx.enter_context(nc.sbuf_tensor(f"mean{tag}", [P, STAGE // P], F32))
        sem = ctx.enter_context(Semaphores(nc, tag))
        loaded = [sem(f"w_loaded{i}") for i in range(3)]
        centred, high_done, low_done = sem("w_centred"), sem("w_high"), sem("w_low")
        pieces = []
        for src, hi, lo, centre in jobs:
            p, n = src.shape
            for c in range(0, n, STAGE):
                e = min(n, c + STAGE)
                pieces.append((p, e - c, src[:, c:e], hi[:, c:e], lo[:, c:e], centre))
        centres = [sum(x[5] for x in pieces[:i + 1]) for i in range(len(pieces))]
        block = ctx.enter_context(nc.Block())

        @block.sync
        def _(sp):
            for i, (p, n, src, hi, lo, centre) in enumerate(pieces):
                if i >= 3:
                    sp.wait_ge(low_done, i - 2)
                sp.dma_start(stage[i % 3][0:p, 0:n], src).then_inc(loaded[i % 3], 16)

        @block.scalar
        def _(act):
            for i, (p, n, src, hi, lo, centre) in enumerate(pieces):
                act.wait_ge(loaded[i % 3], 16 * (i // 3 + 1))
                if centre:
                    act.wait_ge(centred, 3 * centres[i])
                act.activation(hi, stage[i % 3][0:p, 0:n], ACT.Copy, scale=WS).then_inc(high_done, 1)

        @block.vector
        def _(dve):
            def take_means(i):
                if i >= len(pieces) or not pieces[i][5]:
                    return
                w = stage[i % 3][:, 0:pieces[i][1]].rearrange("p (h d) -> p h d", d=P)
                heads = pieces[i][1] // P
                dve.wait_ge(loaded[i % 3], 16 * (i // 3 + 1))
                dve.reduce_sum(mean[:, 0:heads], w, AX).then_inc(centred, 1)
                dve.wait_ge(centred, 3 * centres[i] - 2)
                dve.tensor_scalar(mean[:, 0:heads], mean[:, 0:heads], 1.0 / P, None, ALU.mult).then_inc(centred, 1)
                dve.wait_ge(centred, 3 * centres[i] - 1)
                dve.tensor_tensor(w, w, spread(mean[:, 0:heads], P), ALU.subtract).then_inc(centred, 1)
                dve.wait_ge(centred, 3 * centres[i])

            take_means(0)
            for i, (p, n, src, hi, lo, centre) in enumerate(pieces):
                take_means(i + 1)
                dve.wait_ge(high_done, i + 1)
                dve.scalar_tensor_tensor(lo, stage[i % 3][0:p, 0:n], WS, hi, ALU.mult, ALU.subtract).then_inc(low_done, 1)


def spread(a, n):
    return a.rearrange("p (k o) -> p k o", o=1).to_broadcast([a.shape[0], a.shape[1], n])


def repeat(a, n):
    return a.rearrange("p (o k) -> p o k", o=1).to_broadcast([a.shape[0], n, a.shape[1]])


class LayerNorm:

    def __init__(self, m, ctx, sem, tag, tp):
        nc, self.m, self.tp = m.nc, m, tp
        sb = lambda n, s, t: ctx.enter_context(nc.sbuf_tensor(n + tag, s, t))
        self.st = sb("ln_st", [P, 6], F32)
        self.mv = sb("ln_mv", [P, 2, 2], F32)
        self.ve = sb("ln_ve", [P, 2, 1], F32)
        self.rstd = sb("ln_rstd", [P, 2, 1], F32)
        self.turn = sb("ln_turn", [P, 1], F32)
        self.eps = sb("ln_eps", [P, 1], F32)
        self.xn = sb("ln_xn", [P, 2, DM], F32)
        self.xh = sb("ln_xh", [P, 2, KC, P], F16)
        self.xl = sb("ln_xl", [P, 2, KC, P], F16)
        self.eps_set = sem("eps_set")
        self.mv_ready = sem("mv_ready")
        self.pool_chain = sem("ln_pool")
        self.rstd_ready = sem("rstd_ready")
        self.xn_ready = sem("xn_ready")
        self.tp_ready = sem("tp_ready")
        self.xh_ready = sem("xh_ready")
        self.xl_ready = sem("xl_ready")

    def pool(self, pool):
        pool.memset(self.eps[:, :], LN_EPS).then_inc(self.eps_set, 1)
        pool.wait_ge(self.eps_set, 1)
        self.pool_step(pool, 0, 0)

    def pool_step(self, pool, t, p):
        pool.wait_ge(self.mv_ready, t + 1)
        pool.tensor_tensor(self.ve[:, p], self.mv[:, p, 1:2], self.eps[:, :], ALU.add).then_inc(self.pool_chain, 1)
        pool.wait_ge(self.pool_chain, t + 1)
        pool.tensor_tensor(self.rstd[:, p], self.ve[:, p], self.m.mhalf[:, 0:1], ALU.pow).then_inc(self.rstd_ready, 1)

    def stats(self, dve, ch, t, p):
        ch.link(dve.bn_stats(self.st[:, :], self.m.x_all[:, at(t), :]))
        dve.memset(self.turn[:, :], 0.0)
        dve.bn_aggr(self.mv[:, p], self.st[:, :]).then_inc(self.mv_ready, 1)

    def normalise(self, dve, t, p):
        dve.wait_ge(self.rstd_ready, t + 1)
        dve.wait_ge(self.mv_ready, t + 1)
        dve.tensor_scalar(self.xn[:, p], self.m.x_all[:, at(t), :], self.mv[:, p, 0:1], self.rstd[:, p],
                          ALU.subtract, ALU.mult).then_inc(self.xn_ready, 1)

    def transpose(self, pe, t, p):
        pe.wait_ge(self.xn_ready, t + 1)
        if not (isinstance(t, int) and t < 1):
            pe.wait_ge(self.xl_ready, t)
        for c in range(KC):
            last = pe.transpose(self.tp[:, c * P:(c + 1) * P], self.xn[:, p, c * P:(c + 1) * P], self.m.ident[:, :])
        last.then_inc(self.tp_ready, 1)

    def high(self, act, t, p, used, per_tile=1):
        act.wait_ge(self.tp_ready, t + 1)
        wait_used(act, used, t, 2, per_tile)
        act.copy(self.xh[:, p], self.tp[:, 0:DM]).then_inc(self.xh_ready, 1)

    def low(self, dve, t, p):
        dve.wait_ge(self.xh_ready, t + 1)
        dve.tensor_tensor(self.xl[:, p], self.tp[:, 0:DM], self.xh[:, p], ALU.subtract).then_inc(self.xl_ready, 1)

    def operand(self, p, c, lo=0, n=P):
        return self.xh[:, p, c, lo:lo + n], self.xl[:, p, c, lo:lo + n]


def dram_tile(a, t):
    return a[t, :, :] if isinstance(t, int) else a[bass.ds(t, 1), :, :].rearrange("a p n -> p (a n)")


def at(t):
    return t if isinstance(t, int) else bass.ds(t, 1)

HEADS, HD = 16, 128
KV = 4
REP = HEADS // KV
PAIRS = HEADS // 2


class Attend:

    def __init__(self, m, ctx, sem, tag, ps, w_out, v_cols):
        nc, self.m, self.ps, self.w_out, self.v_cols = m.nc, m, ps, w_out, v_cols
        sb = lambda n, s, t=F32: ctx.enter_context(nc.sbuf_tensor(tag + n, s, t))
        self.s = sb("s", [P, HEADS, SEQ])
        self.e = sb("e", [P, HEADS, SEQ])
        self.mx = sb("mx", [P, HEADS])
        self.den = sb("den", [P, HEADS])
        self.rden = sb("rden", [P, HEADS])
        self.pt = sb("pt", [P, PAIRS, P])
        if v_cols:
            self.v = sb("v", [P, 2, v_cols])
            self.oh = sb("oh", [P, 2, PAIRS, P], F16)
            self.ol = sb("ol", [P, 2, PAIRS, P], F16)
        self.sc_ready = sem("sc_ready")
        self.sc_left = sem("sc_left")
        self.mx_ready = sem("mx_ready")
        self.s_ready = sem("s_ready")
        self.e_ready = sem("e_ready")
        self.den_ready = sem("den_ready")
        self.p_ready = sem("p_ready")
        self.ptr_ready = sem("ptr_ready")
        self.pt_ready = sem("pt_ready")
        self.v_ready, self.v_count = None, 1
        self.pv_ready, self.pv_count = sem("pv_ready"), 2
        self.oh_ready = sem("oh_ready")
        self.ol_ready = sem("ol_ready")
        self.y_ready = sem("y_ready")
        self.y_added = sem("y_added")
        self.x_done = sem("x_done")
        self.sc = ps[:, 4:6, :].rearrange("p k (h s) -> p (k h) s", s=SEQ)
        self.ptp = ps[:, 4:6, :].rearrange("p k (h s) -> p (k h) s", s=P)
        self.ob = ps[:, 6:8, :].rearrange("p b (h s) -> p b h s", s=SEQ)
        self.o = self.ob.rearrange("p b h s -> p h b s")
        self.y = ps[:, 4, 0:DM]

    def take_max(self, dve):
        dve.reduce_max(self.mx[:, :], self.s[:, :, :], AX).then_inc(self.mx_ready, 1)

    def subtract_max(self, pool, t):
        pool.wait_ge(self.mx_ready, t + 1)
        pool.tensor_tensor(self.s[:, :, :], self.s[:, :, :], spread(self.mx[:, :], SEQ),
                           ALU.subtract).then_inc(self.s_ready, 1)

    def exponential(self, act, t, scales=(1.0,)):
        act.wait_ge(self.s_ready, t + 1)
        wait_used(act, self.ptr_ready, t, 1)
        n = len(scales)
        for i, scale in enumerate(scales):
            last = act.activation(self.e[:, i:HEADS:n, :], self.s[:, i:HEADS:n, :], ACT.Exp, scale=scale)
        last.then_inc(self.e_ready, 1)

    def denominator(self, dve, ch, t):
        dve.wait_ge(self.e_ready, t + 1)
        ch.link(dve.reduce_sum(self.den[:, :], self.e[:, :, :], AX))
        wait_used(dve, self.p_ready, t, 1)
        dve.reciprocal(self.rden[:, :], self.den[:, :]).then_inc(self.den_ready, 1)

    def normalise(self, pool, t):
        pool.wait_ge(self.den_ready, t + 1)
        pool.tensor_tensor(self.e[:, :, :], self.e[:, :, :], spread(self.rden[:, :], SEQ),
                           ALU.mult).then_inc(self.p_ready, 1)

    def transpose(self, pe, t, left):
        pe.wait_ge(self.p_ready, t + 1)
        wait_used(pe, left, t, 1)
        ev = self.e[:, :, :].rearrange("p (k b) s -> p k (b s)", b=2)
        for k in range(PAIRS):
            last = pe.transpose(self.ptp[:, k, :], ev[:, k], self.m.ident[:, :])
        last.then_inc(self.ptr_ready, 1)

    def copy_transposed(self, act, t):
        act.wait_ge(self.ptr_ready, t + 1)
        wait_used(act, self.pv_ready, t, 1, self.pv_count)
        act.copy(self.pt[:, :, :], self.ptp).then_inc(self.pt_ready, 1)

    def values(self, pe, t, p, r):
        if r == 0:
            pe.wait_ge(self.pt_ready, t + 1)
            pe.wait_ge(self.v_ready, self.v_count * (t + 1))
            wait_used(pe, self.ol_ready, t, 1, 2)
        else:
            pe.wait_ge(self.ol_ready, 2 * t + 1)
        for b in range(2):
            rows = slice(b * SEQ, (b + 1) * SEQ)
            if self.v_cols < HEADS * HD:
                for j in range(2):
                    g = 2 * r + j
                    last = pe.matmul(self.ob[:, b, 4 * j:4 * j + 4, :], self.v[rows, p, g * HD:(g + 1) * HD],
                                     self.pt[rows, 2 * g:2 * g + 2, :].rearrange("p k (h s) -> p (k h) s", s=SEQ),
                                     start=True, stop=True)
            else:
                for j in range(8):
                    h = 8 * r + j
                    last = pe.matmul(self.ob[:, b, j, :], self.v[rows, p, h * HD:(h + 1) * HD],
                                     self.pt[rows, h // 2, (h % 2) * SEQ:(h % 2 + 1) * SEQ], start=True, stop=True)
        last.then_inc(self.pv_ready, 1)

    def high(self, act, t, r):
        act.wait_ge(self.pv_ready, 2 * t + 1 + r)
        wait_used(act, self.y_ready, t, 1)
        act.copy(self.oh[:, r].rearrange("p h (b s) -> p h b s", b=2), self.o).then_inc(self.oh_ready, 1)

    def low(self, dve, t, r):
        dve.wait_ge(self.oh_ready, 2 * t + 1 + r)
        split = lambda a: a[:, r].rearrange("p h (b s) -> p h b s", b=2)
        dve.tensor_tensor(split(self.ol), self.o, split(self.oh), ALU.subtract).then_inc(self.ol_ready, 1)

    def project(self, pe, t, r, last_tile=False):
        pe.wait_ge(self.ol_ready, 2 * t + 1 + r)
        if r == 0 and not last_tile:
            pe.wait_ge(self.sc_left, t + 2)
        for j in range(8):
            h = 8 * r + j
            last = mm3(pe, self.y, (self.oh[:, r, j], self.ol[:, r, j]),
                       (self.w_out[0][:, h * DM:(h + 1) * DM], self.w_out[1][:, h * DM:(h + 1) * DM]), h == 0, h == 15)
        if r:
            last.then_inc(self.y_ready, 1)

    def add(self, dve, t, bias=None):
        dve.wait_ge(self.y_ready, t + 1)
        x = self.m.x_all[:, at(t), :]
        upd = dve.scalar_tensor_tensor(x, self.y, 1.0 / WS, x, ALU.mult, ALU.add)
        if bias is not None:
            upd.then_inc(self.y_added, 1)
            dve.wait_ge(self.y_added, t + 1)
            upd = dve.tensor_tensor(x, x, bias, ALU.add)
        upd.then_inc(self.x_done, 1)


def attention_gqa(m):
    nc, d = m.nc, m.d
    with ExitStack() as ctx:
        sb = lambda n, s, t=F32: ctx.enter_context(nc.sbuf_tensor("a0_" + n, s, t))
        sem = ctx.enter_context(Semaphores(nc, "a0_"))
        ps = ctx.enter_context(nc.psum_tensor("a0_ps", [P, 8, 512], F32))
        NQ, NK = HEADS * HD, KV * HD
        wq, wk, wks, wv = [[sb(f"{n}{i}", [P, KC, c], F16) for i in range(2)]
                           for n, c in (("wq", NQ), ("wk", NK), ("wks", NK), ("wv", NK))]
        wo = [sb(f"wo{i}", [P, HEADS * DM], F16) for i in range(2)]
        flat = lambda w: w[:, :, :].rearrange("p c n -> p (c n)")
        split_weights(m, [(d["a0_q"], flat(wq[0]), flat(wq[1]), 1), (d["a0_k"], flat(wk[0]), flat(wk[1]), 1),
                          (d["a0_ks"], flat(wks[0]), flat(wks[1]), 1), (d["a0_v"], flat(wv[0]), flat(wv[1]), 0),
                          (d["a0_o"], wo[0][:, :], wo[1][:, :], 0)], "a0")
        ln = LayerNorm(m, ctx, sem, "a0", ps[:, 0, :])
        at_ = Attend(m, ctx, sem, "a0", ps, wo, NK)
        rope = sb("rope", [P, 3, SEQ])
        gb = sb("gb", [P, 8])
        tab = sb("tab", [P, 10, SEQ])
        QC, QS, BQ, KC_, KS, BK, KCS, KSS, BKS, TMP = range(10)
        bq2 = sb("bq2", [P, 2, SEQ])
        mask = sb("mask", [P, SEQ])
        u = sb("u", [P, 2, HEADS, SEQ])
        w = sb("w", [P, 2, HEADS, SEQ])
        sq = sb("sq", [P, 2, HEADS, SEQ])
        sqh = sb("sqh", [P, 2, HEADS, SEQ], BF16)
        sql = sb("sql", [P, 2, HEADS, SEQ], BF16)
        st = sb("st", [P, HEADS, SEQ])
        sqk = sb("sqk", [P, NK])
        kt = sb("kt", [P, 2, NK])
        tmp = sb("tmp", [P, 2, NK])
        vk = sb("vk", [P, KV])
        rk = sb("rk", [P, KV])
        rkd = sb("rkd", [P, KV, P])
        vq = sb("vq", [P, HEADS])
        rq = sb("rq", [P, HEADS])
        s2m = sb("s2m", [P, 2 * KV, SEQ])
        const_in, tab_set = sem("const_in"), sem("tab_set")
        chain, pool_chain = sem("chain"), sem("pool_chain")
        k_ready, ks_ready, vp_ready, q_ready, ksum_ready = (sem(n) for n in ("k_ready", "ks_ready", "vp_ready", "q_ready", "ksum_ready"))
        sqh_ready, sql_ready, stp_ready, st_ready = sem("sqh_ready"), sem("sql_ready"), sem("stp_ready"), sem("st_ready")
        sqk_ready, sq_ready, uw_ready = sem("sqk_ready"), sem("sq_ready"), sem("uw_ready")
        kraw_ready, vk_ready, rkd_ready, rkb_ready, kt_ready = (sem(n) for n in ("kraw_ready", "vk_ready", "rkd_ready", "rkb_ready", "kt_ready"))
        s2_ready, var_ready, vq_ready, rq_ready = sem("s2_ready"), sem("var_ready"), sem("vq_ready"), sem("rq_ready")
        at_.v_ready = sem("v_ready")
        further = lambda t: not (isinstance(t, int) and t + 2 >= TILES)
        QBANK = (1, 2, 0, 3)
        s2_ps = ps[:, 6, :]
        sct = at_.sc
        var_ps = ps[:, 7, 0:HEADS]
        heads_of = lambda a: a.rearrange("p (h b s) -> p h b s", h=4, b=2)
        pair_of = lambda a, k, b: a[:, b, 2 * k:2 * k + 2, :].rearrange("p h s -> p (h s)")
        by_head = lambda a, g: a[:, :, 4 * g:4 * g + 4, :].rearrange("p b h s -> p h b s")
        seqs = lambda a: a.rearrange("p (r s) -> p r s", s=SEQ)
        block = ctx.enter_context(nc.Block())

        @block.sync
        def _(sp):
            sp.dma_start(rope[:, :, :], d["rope"]).then_inc(const_in, 16)
            sp.dma_start(gb[:, :], d["a0_gb"]).then_inc(const_in, 16)
            sp.dma_start(mask[:, :], d["causal"]).then_inc(const_in, 16)
            sp.wait_ge(const_in, 48)

        @block.gpsimd
        def _(pool):
            def key_rstd(t):
                pool.wait_ge(vk_ready, t + 1)
                pool.tensor_tensor(rk[:, :], vk[:, :], m.mhalf[:, 0:KV], ALU.pow).then_inc(pool_chain, 1)
                pool.wait_ge(pool_chain, t + 1)
                wait_used(pool, rkb_ready, t, 1)
                pool.tensor_tensor(rkd[:, :, :], repeat(m.ident[:, :], KV), spread(rk[:, :], P), ALU.mult).then_inc(rkd_ready, 1)

            def squares_low(t, g):
                pool.wait_ge(sqh_ready, 4 * t + g + 1)
                wait_used(pool, var_ready, t, 1)
                pool.tensor_tensor(by_head(sql, g), by_head(sq, g), by_head(sqh, g), ALU.subtract).then_inc(sql_ready, 1)

            def head():
                ln.pool(pool)
                ln.pool_step(pool, 1, 1)
                key_rstd(0)
                for g in range(4):
                    squares_low(0, g)

            def step(t, p, has_next):
                pool.wait_ge(vq_ready, t + 1)
                pool.tensor_tensor(rq[:, :], vq[:, :], m.mhalf[:, 0:HEADS], ALU.pow).then_inc(rq_ready, 1)
                if has_next:
                    key_rstd(t + 1)
                at_.subtract_max(pool, t)
                at_.normalise(pool, t)
                if has_next:
                    for g in range(3):
                        squares_low(t + 1, g)
                if further(t):
                    ln.pool_step(pool, t + 2, p)
                if has_next:
                    squares_low(t + 1, 3)
            over_tiles(pool, head, step)

        @block.scalar
        def _(act):
            def square_keys(t):
                act.wait_ge(k_ready, t + 1)
                wait_used(act, ksum_ready, t, 1)
                act.activation(sqk[:, :], ps[:, 1, :], ACT.Square).then_inc(sqk_ready, 1)

            def value(t, p):
                act.wait_ge(vp_ready, t + 1)
                wait_used(act, at_.pv_ready, t, 2, 2)
                act.activation(at_.v[:, p, :], ps[:, 3, :], ACT.Copy, scale=1.0 / WS).then_inc(at_.v_ready, 1)

            def square(t, g):
                act.wait_ge(q_ready, 4 * t + g + 1)
                wait_used(act, var_ready, t, 1)
                wait_used(act, sql_ready, t, 1, 4, g + 1)
                act.activation(by_head(sq, g), heads_of(ps[:, QBANK[g], :]), ACT.Square).then_inc(sq_ready, 1)
                act.activation(by_head(sqh, g), heads_of(ps[:, QBANK[g], :]), ACT.Square).then_inc(sqh_ready, 1)

            def scores_out(t):
                act.wait_ge(stp_ready, t + 1)
                wait_used(act, at_.sc_ready, t, 1)
                act.copy(st[:, :, :], sct).then_inc(st_ready, 1)

            def head():
                ln.high(act, 0, 0, q_ready, 4)
                square_keys(0)
                value(0, 0)
                for g in range(4):
                    square(0, g)

            def step(t, p, has_next):
                before = not (isinstance(t, int) and t == 0)
                if before:
                    at_.copy_transposed(act, t - 1)
                if has_next:
                    ln.high(act, t + 1, 1 - p, q_ready, 4)
                scores_out(t)
                if has_next:
                    square_keys(t + 1)
                if before:
                    at_.high(act, t - 1, 0)
                if has_next:
                    square(t + 1, 0)
                    square(t + 1, 1)
                at_.exponential(act, t)
                if has_next:
                    value(t + 1, 1 - p)
                if before:
                    at_.high(act, t - 1, 1)
                if has_next:
                    square(t + 1, 2)
                    square(t + 1, 3)
            over_tiles(act, head, step)
            at_.copy_transposed(act, TILES - 1)
            at_.high(act, TILES - 1, 0)
            at_.high(act, TILES - 1, 1)

        @block.vector
        def _(dve):
            ch = Chain(dve, chain, 18, 7, 1)

            def tables():
                ts = lambda o, a, s: ch.link(dve.tensor_scalar(tab[:, o, :], a, s, None, ALU.mult))
                cos, sgn, neg = rope[:, 0, :], rope[:, 1, :], rope[:, 2, :]
                dve.wait_ge(const_in, 48)
                qg, qb, qbs, kg, kb, kgs, kbs = (gb[:, i:i + 1] for i in range(7))
                ts(QC, cos, qg)
                ts(QS, neg, qg)
                ts(KC_, cos, kg)
                ts(KS, sgn, kgs)
                ts(KCS, cos, kgs)
                ts(KSS, neg, kg)
                for out, b0, b1, sn in ((BQ, qb, qbs, sgn), (BK, kb, kbs, sgn), (BKS, kbs, kb, neg)):
                    ts(TMP, sn, b1)
                    ch.link(dve.scalar_tensor_tensor(tab[:, out, :], cos, b0, tab[:, TMP, :], ALU.mult, ALU.add))
                ch.link(dve.tensor_copy(bq2[:, :, :], repeat(tab[:, BQ, :], 2)))

            def keys_raw(t):
                dve.wait_ge(sqk_ready, t + 1)
                dve.wait_ge(ks_ready, t + 1)
                k0, k1 = seqs(ps[:, 1, :]), seqs(ps[:, 2, :])
                bc = lambda i: repeat(tab[:, i, :], NK // SEQ)
                wait_used(dve, stp_ready, t, 1)
                dve.tensor_tensor(seqs(kt[:, 0, :]), k0, bc(KC_), ALU.mult)
                dve.tensor_tensor(seqs(tmp[:, 0, :]), k1, bc(KS), ALU.mult)
                dve.tensor_tensor(seqs(kt[:, 1, :]), k1, bc(KCS), ALU.mult)
                dve.tensor_tensor(seqs(tmp[:, 1, :]), k0, bc(KSS), ALU.mult).then_inc(kraw_ready, 1)
                dve.wait_ge(ksum_ready, t + 1)
                dve.tensor_scalar(vk[:, :], ps[:, 0, 0:KV], 1.0 / HD, LN_EPS * WS * WS, ALU.mult, ALU.add).then_inc(vk_ready, 1)
                dve.wait_ge(kraw_ready, t + 1)
                both = lambda a: a[:, :, :].rearrange("p a n -> p (a n)")
                ch.link(dve.tensor_tensor(both(kt), both(kt), both(tmp), ALU.add))

            def keys_scaled(t):
                bc = lambda i: repeat(tab[:, i, :], NK // SEQ)
                dve.wait_ge(rkb_ready, t + 1)
                ch.link(dve.tensor_tensor(kt[:, :, :], kt[:, :, :], repeat(ps[:, 0, :], 2), ALU.mult))
                ch.link(dve.tensor_tensor(seqs(kt[:, 0, :]), seqs(kt[:, 0, :]), bc(BK), ALU.add))
                dve.tensor_tensor(seqs(kt[:, 1, :]), seqs(kt[:, 1, :]), bc(BKS), ALU.add).then_inc(kt_ready, 1)

            def rotate_query(t, g):
                dve.wait_ge(sqh_ready, 4 * t + g + 1)
                wait_used(dve, stp_ready, t, 1)
                q = heads_of(ps[:, QBANK[g], :])
                table = lambda i: tab[:, i, :].rearrange("p (h b s) -> p h b s", h=1, b=1).to_broadcast([P, 4, 2, SEQ])
                dve.tensor_tensor(by_head(u, g), q, table(QC), ALU.mult)
                dve.tensor_tensor(by_head(w, g), q, table(QS), ALU.mult).then_inc(uw_ready, 1)

            def head():
                tables()
                ln.stats(dve, ch, 0, 0)
                ln.normalise(dve, 0, 0)
                ln.stats(dve, ch, 1, 1)
                ln.normalise(dve, 1, 1)
                ln.low(dve, 0, 0)
                keys_raw(0)
                rotate_query(0, 0)
                rotate_query(0, 1)
                keys_scaled(0)
                rotate_query(0, 2)
                rotate_query(0, 3)

            def step(t, p, has_next):
                ch.tile(t)
                before = not (isinstance(t, int) and t == 0)
                if has_next:
                    ln.low(dve, t + 1, 1 - p)
                dve.wait_ge(s2_ready, t + 1)
                ch.link(dve.scalar_tensor_tensor(s2m[:, :, :], seqs(s2_ps), HD ** -0.5, repeat(mask[:, :], 2 * KV), ALU.mult, ALU.add))
                dve.wait_ge(var_ready, t + 1)
                dve.tensor_scalar(vq[:, :], var_ps, 1.0, HD * LN_EPS * WS * WS, ALU.mult, ALU.add).then_inc(vq_ready, 1)
                if has_next:
                    keys_raw(t + 1)
                dve.wait_ge(at_.sc_ready, t + 1)
                dve.wait_ge(rq_ready, t + 1)
                wait_used(dve, at_.e_ready, t, 1)
                dve.tensor_tensor(at_.s[:, :, :], at_.sc, spread(rq[:, :], SEQ), ALU.mult).then_inc(at_.sc_left, 1)
                dve.wait_ge(at_.sc_left, t + 1)
                s4 = at_.s[:, :, :].rearrange("p (g r b) s -> p g r (b s)", r=2, b=2)
                s2b = s2m[:, :, :].rearrange("p (g o b) s -> p g o (b s)", o=1, b=2).to_broadcast([P, KV, 2, P])
                ch.link(dve.tensor_tensor(s4, s4, s2b, ALU.add))
                at_.take_max(dve)
                if before:
                    at_.low(dve, t - 1, 0)
                if has_next:
                    rotate_query(t + 1, 0)
                    keys_scaled(t + 1)
                    rotate_query(t + 1, 1)
                at_.denominator(dve, ch, t)
                if before:
                    at_.low(dve, t - 1, 1)
                if has_next:
                    rotate_query(t + 1, 2)
                if further(t):
                    ln.stats(dve, ch, t + 2, p)
                if has_next:
                    rotate_query(t + 1, 3)
                if further(t):
                    ln.normalise(dve, t + 2, p)
                if before:
                    at_.add(dve, t - 1)
            over_tiles(dve, head, step)
            at_.low(dve, TILES - 1, 0)
            at_.low(dve, TILES - 1, 1)
            at_.add(dve, TILES - 1)

        @block.tensor
        def _(pe):
            def keys(t, p, i):
                wt, ready = ((wk, k_ready), (wks, ks_ready))[i]
                pe.wait_ge(ln.xl_ready, t + 1)
                wait_used(pe, uw_ready, t, 1, 4, i + 1)
                for h in range(KV):
                    for c in range(KC):
                        cols = slice(h * HD, (h + 1) * HD)
                        last = mm3(pe, ps[:, 1 + i, cols], (wt[0][:, c, cols], wt[1][:, c, cols]),
                                   ln.operand(p, c), c == 0, c == KC - 1)
                last.then_inc(ready, 1)

            def value(t, p):
                wait_used(pe, uw_ready, t, 1, 4, 4)
                for c in range(KC):
                    last = mm3(pe, ps[:, 3, :], ln.operand(p, c), (wv[0][:, c, :], wv[1][:, c, :]), c == 0, c == KC - 1)
                last.then_inc(vp_ready, 1)

            def key_sums(t):
                pe.wait_ge(sqk_ready, t + 1)
                for h in range(KV):
                    last = pe.matmul(ps[:, 0, h:h + 1], sqk[:, h * P:(h + 1) * P], m.ones[:, 0:1], start=True, stop=True)
                last.then_inc(ksum_ready, 1)

            def key_factors(t):
                pe.wait_ge(rkd_ready, t + 1)
                pe.matmul(ps[:, 0, :], m.ones[:, :], rkd[:, :, :].rearrange("p h s -> p (h s)"),
                          start=True, stop=True).then_inc(rkb_ready, 1)

            def queries(t, p, g):
                if g < 2:
                    pe.wait_ge(kraw_ready, t + 1)
                elif g == 2:
                    pe.wait_ge(kt_ready, t + 1)
                else:
                    pe.wait_ge(at_.v_ready, t + 1)
                for h in range(4):
                    for c in range(KC):
                        cols = slice((4 * g + h) * HD, (4 * g + h + 1) * HD)
                        last = mm3(pe, ps[:, QBANK[g], h * P:(h + 1) * P], (wq[0][:, c, cols], wq[1][:, c, cols]),
                                   ln.operand(p, c), c == 0, c == KC - 1)
                last.then_inc(q_ready, 1)

            def bias_scores(t):
                pe.wait_ge(kt_ready, t + 1)
                wait_used(pe, at_.ol_ready, t, 2, 2)
                pe.matmul(s2_ps, bq2[:, :, :].rearrange("p a s -> p (a s)"), kt[:, 0, :], start=True, stop=True).then_inc(s2_ready, 1)

            def query_sums(t):
                pe.wait_ge(sql_ready, 4 * (t + 1))
                for b in range(2):
                    for k in range(PAIRS):
                        out = var_ps[:, 2 * k + b:2 * k + b + 1]
                        pe.matmul(out, pair_of(sqh, k, b), m.onesb[:, :], start=True, stop=False)
                        last = pe.matmul(out, pair_of(sql, k, b), m.onesb[:, :], start=False, stop=True)
                last.then_inc(var_ready, 1)

            def scores(t):
                pe.wait_ge(uw_ready, 4 * (t + 1))
                if not (isinstance(t, int) and t == 0):
                    pe.wait_ge(at_.pt_ready, t)
                for g in range(KV):
                    for b in range(2):
                        keys_ = slice(g * HD + b * SEQ, g * HD + (b + 1) * SEQ)
                        out = sct[b * SEQ:(b + 1) * SEQ, 4 * g:4 * g + 4, :]
                        pe.matmul(out, kt[:, 0, keys_], u[:, b, 4 * g:4 * g + 4, :], start=True, stop=False)
                        last = pe.matmul(out, kt[:, 1, keys_], w[:, b, 4 * g:4 * g + 4, :], start=False, stop=True)
                last.then_inc(stp_ready, 1)

            def turn_scores(t):
                pe.wait_ge(st_ready, t + 1)
                for k in range(PAIRS):
                    last = pe.transpose(at_.ptp[:, k, :], st[:, 2 * k:2 * k + 2, :].rearrange("p h s -> p (h s)"), m.ident[:, :])
                last.then_inc(at_.sc_ready, 1)

            def head():
                ln.transpose(pe, 0, 0)
                keys(0, 0, 0)
                keys(0, 0, 1)
                value(0, 0)
                key_sums(0)
                queries(0, 0, 0)
                queries(0, 0, 1)
                key_factors(0)
                queries(0, 0, 2)
                queries(0, 0, 3)

            def step(t, p, has_next):
                before = not (isinstance(t, int) and t == 0)
                if before:
                    at_.transpose(pe, t - 1, at_.x_done)
                if has_next:
                    pe.wait_ge(uw_ready, 4 * t + 3)
                    ln.transpose(pe, t + 1, 1 - p)
                bias_scores(t)
                scores(t)
                query_sums(t)
                if has_next:
                    keys(t + 1, 1 - p, 0)
                    keys(t + 1, 1 - p, 1)
                    key_sums(t + 1)
                turn_scores(t)
                if before:
                    pe.wait_ge(vq_ready, t + 1)
                    at_.values(pe, t - 1, 1 - p, 0)
                if has_next:
                    queries(t + 1, 1 - p, 0)
                    value(t + 1, 1 - p)
                    queries(t + 1, 1 - p, 1)
                    key_factors(t + 1)
                if before:
                    at_.project(pe, t - 1, 0)
                    at_.values(pe, t - 1, 1 - p, 1)
                if has_next:
                    queries(t + 1, 1 - p, 2)
                    queries(t + 1, 1 - p, 3)
                if before:
                    at_.project(pe, t - 1, 1)
            over_tiles(pe, head, step)
            t, p = TILES - 1, 1
            at_.transpose(pe, t, at_.x_done)
            for r in range(2):
                at_.values(pe, t, p, r)
                at_.project(pe, t, r, True)
EXPERTS, RANK, LORA_SCALE = 8, 16, 2.0


def ffn_lora(m):
    nc, d = m.nc, m.d
    H1 = EXPERTS * RANK
    with ExitStack() as ctx:
        sb = lambda n, s, t=F32: ctx.enter_context(nc.sbuf_tensor("f0_" + n, s, t))
        sem = ctx.enter_context(Semaphores(nc, "f0_"))
        ps = ctx.enter_context(nc.psum_tensor("f0_ps", [P, 8, 512], F32))
        wb = [sb(f"wb{i}", [P, KC, DM], F16) for i in range(2)]
        wa = [sb(f"wa{i}", [P, KC, H1 + EXPERTS], F16) for i in range(2)]
        wB = [sb(f"wB{i}", [P, DM], F16) for i in range(2)]
        flat = lambda w: w[:, :, :].rearrange("p c n -> p (c n)")
        split_weights(m, [(d["ffn0_base"], flat(wb[0]), flat(wb[1]), 0), (d["ffn0_a"], flat(wa[0]), flat(wa[1]), 0),
                          (d["ffn0_b"], wB[0][:, :], wB[1][:, :], 0)], "f0")
        ln = LayerNorm(m, ctx, sem, "f0", ps[:, 0, :])
        desc = sb("desc", [P, EXPERTS])
        bias = sb("bias", [P, DM])
        top = sb("top", [P, 1])
        cand = sb("cand", [P, EXPERTS])
        first = sb("first", [P, 1])
        pick = sb("pick", [P, EXPERTS])
        hm = sb("hm", [P, 2, H1])
        hh = sb("hh", [P, 2, P], F16)
        hl = sb("hl", [P, 2, P], F16)
        y_ps = lambda p: ps[:, 1 + p, 0:DM]
        a_ps = lambda p: ps[:, 3 + p, 0:H1 + EXPERTS]
        ht_ps = lambda p: ps[:, 5 + p, 0:P]
        const_in, chain = sem("const_in"), sem("chain")
        a_ready, h_ready, ht_ready = sem("a_ready"), sem("h_ready"), sem("ht_ready")
        hh_ready, hl_ready, y_ready, x_done = sem("hh_ready"), sem("hl_ready"), sem("y_ready"), sem("x_done")
        block = ctx.enter_context(nc.Block())

        @block.sync
        def _(sp):
            sp.dma_start(desc[:, :], d["desc"]).then_inc(const_in, 16)
            sp.dma_start(bias[:, :], d["ffn0_bias"].to_broadcast([P, DM])).then_inc(const_in, 16)
            sp.wait_ge(const_in, 32)

        @block.gpsimd
        def _(pool):
            def step(t, p, has_next):
                if has_next:
                    ln.pool_step(pool, t + 1, 1 - p)
            over_tiles(pool, lambda: ln.pool(pool), step)

        @block.scalar
        def _(act):
            def step(t, p, has_next):
                if has_next:
                    ln.high(act, t + 1, 1 - p, y_ready)
                act.wait_ge(ht_ready, t + 1)
                wait_used(act, y_ready, t, 2)
                act.copy(hh[:, p], ht_ps(p)).then_inc(hh_ready, 1)
            over_tiles(act, lambda: ln.high(act, 0, 0, y_ready), step)

        @block.vector
        def _(dve):
            ch = Chain(dve, chain, 1, 6)

            def head():
                ln.stats(dve, ch, 0, 0)
                ln.normalise(dve, 0, 0)
                ln.low(dve, 0, 0)
                dve.wait_ge(const_in, 32)

            def step(t, p, has_next):
                ch.tile(t)
                if has_next:
                    ln.stats(dve, ch, t + 1, 1 - p)
                else:
                    ch.k += 0
                dve.wait_ge(a_ready, t + 1)
                logits = a_ps(p)[:, H1:]
                ch.link(dve.reduce_max(top[:, :], logits, AX))
                ch.link(dve.scalar_tensor_tensor(cand[:, :], logits, top[:, :], desc[:, :], ALU.is_ge, ALU.mult))
                ch.link(dve.reduce_max(first[:, :], cand[:, :], AX))
                ch.link(dve.tensor_scalar(pick[:, :], cand[:, :], first[:, :], LORA_SCALE / WS, ALU.is_equal, ALU.mult))
                wait_used(dve, ht_ready, t, 2)
                dve.tensor_tensor(hm[:, p].rearrange("p (e r) -> p e r", r=RANK),
                                  a_ps(p)[:, 0:H1].rearrange("p (e r) -> p e r", r=RANK),
                                  spread(pick[:, :], RANK),
                                  ALU.mult).then_inc(h_ready, 1)
                if has_next:
                    ln.normalise(dve, t + 1, 1 - p)
                    ln.low(dve, t + 1, 1 - p)
                dve.wait_ge(hh_ready, t + 1)
                dve.tensor_tensor(hl[:, p], ht_ps(p), hh[:, p], ALU.subtract).then_inc(hl_ready, 1)
                dve.wait_ge(y_ready, t + 1)
                x = m.x_all[:, at(t), :]
                ch.link(dve.scalar_tensor_tensor(x, y_ps(p), 1.0 / WS, x, ALU.mult, ALU.add))
                dve.tensor_tensor(x, x, bias[:, :], ALU.add).then_inc(x_done, 1)
            over_tiles(dve, head, step)

        @block.tensor
        def _(pe):
            def step(t, p, has_next):
                pe.wait_ge(ln.xl_ready, t + 1)
                wait_used(pe, h_ready, t, 2)
                for c in range(KC):
                    last = mm3(pe, a_ps(p), ln.operand(p, c), (wa[0][:, c], wa[1][:, c]), c == 0, c == KC - 1)
                last.then_inc(a_ready, 1)
                wait_used(pe, x_done, t, 2)
                for c in range(KC):
                    mm3(pe, y_ps(p), ln.operand(p, c), (wb[0][:, c], wb[1][:, c]), c == 0, False)
                if has_next:
                    ln.transpose(pe, t + 1, 1 - p)
                pe.wait_ge(h_ready, t + 1)
                wait_used(pe, hl_ready, t, 2)
                pe.transpose(ht_ps(p), hm[:, p], m.ident[:, :]).then_inc(ht_ready, 1)
                pe.wait_ge(hl_ready, t + 1)
                mm3(pe, y_ps(p), (hh[:, p], hl[:, p]), (wB[0][:, :], wB[1][:, :]), False, True).then_inc(y_ready, 1)
            over_tiles(pe, lambda: ln.transpose(pe, 0, 0), step)
XH = 8
XT = SEQ // XH
XU = 2 * XH
XG = 4
VC = XT + 1


def attention_features(m):
    nc, d = m.nc, m.d
    with ExitStack() as ctx:
        sb = lambda n, s, t=F32: ctx.enter_context(nc.sbuf_tensor("x0_" + n, s, t))
        sem = ctx.enter_context(Semaphores(nc, "x0_"))
        ps = ctx.enter_context(nc.psum_tensor("x0_ps", [P, 8, 512], F32))
        ln = LayerNorm(m, ctx, sem, "x0", ps[:, 0, :])
        self_ = sb("sel_f", [P, 4, XG * P])
        sel = sb("sel", [P, 4, XG, P], F16)
        one_row = sb("one_row", [P, 1])
        nident = sb("nident", [P, P], F16)
        xh = sb("xh", [P, 2, DM], F16)
        xl = sb("xl", [P, 2, DM], F16)
        cf = sb("cf", [P, 2, DM])
        chi = sb("chi", [P, DM], F16)
        clo = sb("clo", [P, DM], F16)
        vt = sb("vt", [P, 2, KC, XU, VC])
        q = sb("q", [P, 2, XG, DM], F16)
        k = sb("k", [P, 2, XG, DM], F16)
        mx = sb("mx", [P, KC, XG, P], F16)
        e = sb("e", [P, 4, KC, DM])
        rec = sb("rec", [P, KC, XU])
        o = sb("o", [P, KC, XU, XT])
        const_in, zeroed, sel_set = sem("const_in"), sem("zeroed"), sem("sel_set")
        c_in = [sem(f"c_in{i}") for i in range(2)]
        v_in = [sem(f"v_in{i}") for i in range(2)]
        chain, xs_ready, chi_ready, clo_ready = sem("chain"), sem("xs_ready"), sem("chi_ready"), sem("clo_ready")
        qsel, ksel, q1_ready, k_ready, s1_ready, mx_ready, nm_ready, q2_ready = (
            sem(n) for n in ("qsel", "ksel", "q1_ready", "k_ready", "s1_ready", "mx_ready", "nm_ready", "q2_ready"))
        s2_ready, e_ready, pv_ready, o_ready, ot_ready, x_done = (
            sem(n) for n in ("s2_ready", "e_ready", "pv_ready", "o_ready", "ot_ready", "x_done"))
        q_ps = ps[:, 0:2, :].rearrange("p b (g n) -> p (b g) n", n=DM)
        k_ps = ps[:, 2, :].rearrange("p (g n) -> p g n", n=DM)
        ot_ps = ps[:, 2, 0:DM]
        o_ps = ps[:, 3, 0:KC * XU * VC].rearrange("p (c u v) -> p c u v", c=KC, v=VC)
        s1_ps = lambda u: ps[:, 4 + u % 2, :].rearrange("p (c n) -> p c n", n=DM)
        s2_ps = lambda u: ps[:, 6 + u % 2, :]
        further = lambda t: not (isinstance(t, int) and t + 2 >= TILES)
        block = ctx.enter_context(nc.Block())

        @block.sync
        def _(sp):
            sp.dma_start(self_[:, :, :], d["x0_sel"]).then_inc(const_in, 16)
            sp.dma_start(one_row[:, :], d["x0_one"]).then_inc(const_in, 16)

            def load(t, p):
                wait_used(sp, clo_ready, t, 2)
                sp.dma_start(cf[:, p], dram_tile(d["ctx"], t)).then_inc(c_in[p], 16)
                wait_used(sp, pv_ready, t, 2, XU)
                sp.dma_start(vt[:, p].rearrange("p c u v -> p (c u v)"), dram_tile(d["ctx_v"], t)).then_inc(v_in[p], 16)

            def head():
                load(0, 0)
                load(1, 1)

            def step(t, p, has_next):
                if further(t):
                    load(t + 2, p)
            over_tiles(sp, head, step)
            for p in range(2):
                sp.wait_ge(v_in[p], 8 * TILES)

        @block.gpsimd
        def _(pool):
            def split_context(t, p):
                pool.wait_ge(c_in[p], (t - p) * 8 + 16)
                wait_used(pool, ksel, t, 1, 2)
                pool.tensor_tensor(chi[:, :], cf[:, p], m.ones2[:, :], ALU.mult).then_inc(chi_ready, 1)
                pool.wait_ge(chi_ready, t + 1)
                pool.tensor_tensor(clo[:, :], cf[:, p], chi[:, :], ALU.subtract).then_inc(clo_ready, 1)

            def head():
                ln.pool(pool)
                split_context(0, 0)
                ln.pool_step(pool, 1, 1)

            def step(t, p, has_next):
                if has_next:
                    split_context(t + 1, 1 - p)
                if further(t):
                    ln.pool_step(pool, t + 2, p)
            over_tiles(pool, head, step)

        @block.scalar
        def _(act):
            def operands(t, p):
                act.wait_ge(qsel, t + 1)
                wait_used(act, s2_ready, t, 2, XU)
                act.copy(q[:, p], q_ps).then_inc(q1_ready, 1)
                for r in range(2):
                    act.wait_ge(ksel, 2 * t + r + 1)
                    act.activation(k[:, p, 2 * r:2 * r + 2], k_ps, ACT.Identity, bias=one_row[:, :]).then_inc(k_ready, 1)

            def shifted(t, p):
                act.wait_ge(nm_ready, t + 1)
                act.copy(q[:, p], q_ps).then_inc(q2_ready, 1)

            def head():
                act.wait_ge(const_in, 32)
                operands(0, 0)
                shifted(0, 0)

            def step(t, p, has_next):
                if has_next:
                    operands(t + 1, 1 - p)
                for u in range(XU):
                    act.wait_ge(s2_ready, XU * t + u + 1)
                    if isinstance(t, int) and t == 0:
                        if u >= 4:
                            act.wait_ge(pv_ready, u - 3)
                    else:
                        act.wait_ge(pv_ready, XU * t + u - 3)
                    act.activation(e[:, u % 4].rearrange("p c n -> p (c n)"), s2_ps(u), ACT.Exp,
                                   scale=XT ** -0.5).then_inc(e_ready, 1)
                if has_next:
                    shifted(t + 1, 1 - p)
            over_tiles(act, head, step)

        @block.vector
        def _(dve):
            ch = Chain(dve, chain, 4, 3, 2)

            def split_x(t, p):
                ln.stats(dve, ch, t, p)
                ln.normalise(dve, t, p)
                dve.wait_ge(ln.xn_ready, t + 1)
                wait_used(dve, qsel, t, 2)
                ch.link(dve.tensor_copy(xh[:, p], ln.xn[:, p]))
                dve.tensor_tensor(xl[:, p], ln.xn[:, p], xh[:, p], ALU.subtract).then_inc(xs_ready, 1)

            def maximum(t, u):
                dve.wait_ge(s1_ready, XU * t + u + 1)
                if u == 0:
                    wait_used(dve, nm_ready, t, 1)
                g, jj = divmod(u, 4)
                c = 32 * jj + 3 * XT
                dve.reduce_max(mx[:, :, g, c:c + 1].rearrange("p c o -> p (c o)"), s1_ps(u), AX).then_inc(mx_ready, 1)

            def normalise(t):
                dve.wait_ge(pv_ready, XU * (t + 1))
                wait_used(dve, ot_ready, t, 1)
                for c in range(KC):
                    last = dve.reciprocal(rec[:, c, :], o_ps[:, c, :, XT])
                ch.link(last)
                for c in range(KC):
                    last = dve.tensor_tensor(o[:, c], o_ps[:, c, :, 0:XT], spread(rec[:, c, :], XT), ALU.mult)
                last.then_inc(o_ready, 1)

            def finish(t):
                dve.wait_ge(ot_ready, t + 1)
                x = m.x_all[:, at(t), :]
                dve.tensor_tensor(x, x, ot_ps, ALU.add).then_inc(x_done, 1)

            def head():
                dve.memset(mx[:, :, :, :].rearrange("p a b c -> p (a b c)"), 0.0).then_inc(zeroed, 1)
                dve.wait_ge(const_in, 32)
                dve.tensor_scalar(nident[:, :], m.ident[:, :], -1.0, None, ALU.mult)
                dve.tensor_copy(sel[:, :, :, :].rearrange("p a g c -> p a (g c)"), self_[:, :, :]).then_inc(sel_set, 1)
                split_x(0, 0)
                split_x(1, 1)
                dve.wait_ge(zeroed, 1)
                for u in range(XU):
                    maximum(0, u)

            def step(t, p, has_next):
                ch.tile(t)
                first = isinstance(t, int) and t == 0
                if not first:
                    normalise(t - 1)
                else:
                    ch.link(dve.memset(ln.turn[:, :], 0.0))
                for u in range(XU):
                    if has_next:
                        maximum(t + 1, u)
                    if u == 2 and not first:
                        finish(t - 1)
                    if u == 5 and further(t):
                        split_x(t + 2, p)
            over_tiles(dve, head, step)
            ch.tile(TILES)
            ch.base -= 2 * ch.ahead
            normalise(TILES - 1)
            finish(TILES - 1)

        @block.tensor
        def _(pe):
            def select_q(t, p):
                pe.wait_ge(xs_ready, t + 1)
                wait_used(pe, q2_ready, t, 1)
                for g in range(XG):
                    pe.matmul(q_ps[:, g], sel[:, 0, g], xh[:, p], start=g % 2 == 0, stop=False, skip_group_check=True)
                    last = pe.matmul(q_ps[:, g], sel[:, 1, g], xl[:, p], start=False, stop=False, skip_group_check=True)
                last.then_inc(qsel, 1)

            def select_k(t):
                pe.wait_ge(clo_ready, t + 1)
                for r in range(2):
                    if r:
                        pe.wait_ge(k_ready, 2 * t + 1)
                    else:
                        wait_used(pe, x_done, t, 3)
                        wait_used(pe, k_ready, t, 1, 2)
                    for i in range(2):
                        g = 2 * r + i
                        pe.matmul(k_ps[:, i], sel[:, 2, g], chi[:, :], start=True, stop=False)
                        last = pe.matmul(k_ps[:, i], sel[:, 3, g], clo[:, :], start=False, stop=True)
                    last.then_inc(ksel, 1)

            def rows(u):
                g, jj = divmod(u, 4)
                return g, slice(32 * jj, 32 * jj + 32)

            def scores(t, p, u):
                g, r = rows(u)
                if u == 0:
                    pe.wait_ge(q1_ready, t + 1)
                if u % 8 == 0:
                    pe.wait_ge(k_ready, 2 * t + 1 + u // 8)
                if isinstance(t, int) and t == 0:
                    if u >= 2:
                        pe.wait_ge(mx_ready, u - 1)
                else:
                    pe.wait_ge(mx_ready, XU * t + u - 1)
                for c in range(KC):
                    last = pe.matmul(s1_ps(u)[:, c], q[r, p, g, c * P:(c + 1) * P], k[r, p, g], start=True, stop=True)
                last.then_inc(s1_ready, 1)

            def shifted_scores(t, p, u):
                g, r = rows(u)
                if u == 0:
                    pe.wait_ge(q2_ready, t + 1)
                if isinstance(t, int) and t == 0:
                    if u >= 2:
                        pe.wait_ge(e_ready, u - 1)
                else:
                    pe.wait_ge(e_ready, XU * t + u - 1)
                for c in range(KC):
                    last = pe.matmul(s2_ps(u)[:, c * DM:(c + 1) * DM], k[r, p, g, c * P:(c + 1) * P], q[r, p, g],
                                     start=True, stop=True)
                last.then_inc(s2_ready, 1)

            def values(t, p, u):
                pe.wait_ge(e_ready, XU * t + u + 1)
                if u == 0:
                    pe.wait_ge(v_in[p], (t - p) * 8 + 16)
                    wait_used(pe, o_ready, t, 1)
                for c in range(KC):
                    for n in range(KC):
                        last = pe.matmul(o_ps[:, c, u, :], e[:, u % 4, n, c * P:(c + 1) * P],
                                         vt[:, p, n, u, :], start=n == 0, stop=n == KC - 1)
                last.then_inc(pv_ready, 1)

            def add_maxima(t):
                pe.wait_ge(mx_ready, XU * (t + 1))
                pe.wait_ge(q1_ready, t + 1)
                for g in range(XG):
                    for c in range(KC):
                        last = pe.matmul(q_ps[:, g, c * P:(c + 1) * P], mx[:, c, g, :], nident[:, :],
                                         start=False, stop=True, skip_group_check=True)
                last.then_inc(nm_ready, 1)

            def head():
                pe.wait_ge(sel_set, 1)
                select_q(0, 0)
                select_k(0)
                for u in range(XU):
                    scores(0, 0, u)
                add_maxima(0)

            def transpose_out(t):
                pe.wait_ge(o_ready, t + 1)
                for c in range(KC):
                    last = pe.transpose(ot_ps[:, c * P:(c + 1) * P], o[:, c].rearrange("p u i -> p (u i)"), m.ident[:, :])
                last.then_inc(ot_ready, 1)

            def step(t, p, has_next):
                if has_next:
                    select_q(t + 1, 1 - p)
                    select_k(t + 1)
                for u in range(XU + 1):
                    if u < XU:
                        if has_next:
                            scores(t + 1, 1 - p, u)
                        shifted_scores(t, p, u)
                    if u == 1 and not (isinstance(t, int) and t == 0):
                        if has_next:
                            pe.wait_ge(k_ready, 2 * (t + 2))
                        transpose_out(t - 1)
                    if u:
                        values(t, p, u - 1)
                if has_next:
                    add_maxima(t + 1)
            over_tiles(pe, head, step)
            transpose_out(TILES - 1)
RMS_EPS = 1e-6
BR = 64


def bias_rows(m, jobs, tag):
    nc = m.nc
    with ExitStack() as ctx:
        n_all = sum(src.shape[1] for src, _ in jobs)
        stage = ctx.enter_context(nc.sbuf_tensor(f"bstage{tag}", [1, n_all], F32))
        sem = ctx.enter_context(Semaphores(nc, tag))
        loaded, zeroed, high_done = sem("b_loaded"), sem("b_zeroed"), sem("b_high")
        starts = [sum(src.shape[1] for src, _ in jobs[:i]) for i in range(len(jobs))]
        block = ctx.enter_context(nc.Block())

        @block.sync
        def _(sp):
            for (src, rows), s in zip(jobs, starts):
                sp.dma_start(stage[0:1, s:s + src.shape[1]], src).then_inc(loaded, 16)
            sp.wait_ge(loaded, 16 * len(jobs))

        @block.scalar
        def _(act):
            act.wait_ge(loaded, 16 * len(jobs))
            act.wait_ge(zeroed, len(jobs))
            for (src, rows), s in zip(jobs, starts):
                act.activation(rows[0:1, :], stage[0:1, s:s + src.shape[1]], ACT.Copy, scale=WS).then_inc(high_done, 1)

        @block.vector
        def _(dve):
            for _, rows in jobs:
                dve.memset(rows, 0.0).then_inc(zeroed, 1)
            for i, ((src, rows), s) in enumerate(zip(jobs, starts)):
                dve.wait_ge(high_done, i + 1)
                dve.scalar_tensor_tensor(rows[32:33, :], stage[0:1, s:s + src.shape[1]], WS, rows[0:1, :],
                                         ALU.mult, ALU.subtract)


def attention_cross(m):
    nc, d = m.nc, m.d
    NI = HEADS * HD
    with ExitStack() as ctx:
        sb = lambda n, s, t=F32: ctx.enter_context(nc.sbuf_tensor("x1_" + n, s, t))
        sem = ctx.enter_context(Semaphores(nc, "x1_"))
        ps = ctx.enter_context(nc.psum_tensor("x1_ps", [P, 8, 512], F32))
        wq, wk, wv = [[sb(f"{n}{i}", [P, KC, NI], F16) for i in range(2)] for n in ("wq", "wk", "wv")]
        wo = [sb(f"wo{i}", [P, HEADS * DM], F16) for i in range(2)]
        bq, bk, bv = (sb(n, [BR, NI], F16) for n in ("bq", "bk", "bv"))
        flat = lambda w: w[:, :, :].rearrange("p c n -> p (c n)")
        split_weights(m, [(d["x1_q"], flat(wq[0]), flat(wq[1]), 0), (d["x1_k"], flat(wk[0]), flat(wk[1]), 0),
                          (d["x1_v"], flat(wv[0]), flat(wv[1]), 0), (d["x1_o"], wo[0][:, :], wo[1][:, :], 0)], "x1")
        bias_rows(m, [(d["x1_bq"], bq[:, :]), (d["x1_bk"], bk[:, :]), (d["x1_bv"], bv[:, :])], "x1")
        ln = LayerNorm(m, ctx, sem, "x1", ps[:, 0, :])
        at_ = Attend(m, ctx, sem, "x1", ps, wo, NI)
        cf = sb("cf", [P, 2, KC, P])
        chi = sb("chi", [P, 2, KC, P], F16)
        clo = sb("clo", [P, 2, KC, P], F16)
        qs = sb("qs", [P, 2, HEADS])
        qk_scale = sb("qk_scale", [P, HEADS])
        bo = sb("bo", [P, DM])
        q = sb("q", [P, HEADS, P])
        k = sb("k", [P, HEADS, P])
        sq = sb("sq", [P, 4, 512])
        sum4 = sb("sum4", [P, 2, 512])
        sum2 = sb("sum2", [P, 2, P])
        sums = sb("sums", [P, 2, P])
        var = sb("var", [P, 3])
        rms = sb("rms", [P, 3])
        rkd = sb("rkd", [P, P])
        rkb = sb("rkb", [P, P])
        const_in, scale_set, ctx_in = sem("const_in"), sem("scale_set"), [sem(f"ctx_in{i}") for i in range(2)]
        chain = sem("chain")
        chi_ready, clo_ready, proj_ready = sem("chi_ready"), sem("clo_ready"), sem("proj_ready")
        act_left, dve_left = sem("act_left"), sem("dve_left")
        sum4_ready, sum2_ready, sums_ready = sem("sum4_ready"), sem("sum2_ready"), sem("sums_ready")
        ss_ready, var_ready, rms_ready, rkd_ready = sem("ss_ready"), sem("var_ready"), sem("rms_ready"), sem("rkd_ready")
        rkp_ready, rkb_ready = sem("rkp_ready"), sem("rkb_ready")
        at_.v_ready, at_.v_count = act_left, 12
        bank = lambda e: (e + 1) % 4
        further = lambda t: not (isinstance(t, int) and t + 2 >= TILES)
        block = ctx.enter_context(nc.Block())


        @block.sync
        def _(sp):
            sp.dma_start(qs[:, :, :], d["x1_scales"]).then_inc(const_in, 16)
            sp.dma_start(bo[:, :], d["x1_bo"].to_broadcast([P, DM])).then_inc(const_in, 16)

            def load_context(t, p):
                wait_used(sp, clo_ready, t, 2)
                sp.dma_start(cf[:, p].rearrange("p c s -> p (c s)"), dram_tile(d["ctx_t"], t)).then_inc(ctx_in[p], 16)

            load_context(0, 0)
            load_context(1, 1)
            if TILES > 2:
                with sp.Fori(1, TILES // 2) as i:
                    load_context(2 * i, 0)
                    load_context(2 * i + 1, 1)
            for p in range(2):
                sp.wait_ge(ctx_in[p], 16 * (TILES // 2))
            sp.wait_ge(const_in, 32)

        @block.gpsimd
        def _(pool):
            def split_context(t, p):
                pool.wait_ge(ctx_in[p], (t - p) * 8 + 16)
                wait_used(pool, proj_ready, t, 2, 12)
                pool.tensor_tensor(chi[:, p], cf[:, p], repeat(m.ones[:, :], KC), ALU.mult).then_inc(chi_ready, 1)
                pool.wait_ge(chi_ready, t + 1)
                pool.tensor_tensor(clo[:, p], cf[:, p], chi[:, p], ALU.subtract).then_inc(clo_ready, 1)

            def sum_squares(t, i):
                pool.wait_ge(act_left, 12 * t + 4 * i + 4)
                pool.tensor_tensor(sum4[:, :, :], sq[:, 0:2, :], sq[:, 2:4, :], ALU.add).then_inc(sum4_ready, 1)
                pool.wait_ge(sum4_ready, 2 * t + i + 1)
                pool.tensor_tensor(sum4[:, 0, :], sum4[:, 0, :], sum4[:, 1, :], ALU.add).then_inc(sum2_ready, 1)
                pool.wait_ge(sum2_ready, 2 * (2 * t + i) + 1)
                halves = sum4[:, 0, :].rearrange("p (a n) -> p a n", a=2)
                pool.tensor_tensor(sum2[:, :, :].rearrange("p a n -> p (a n)"), halves[:, 0], halves[:, 1], ALU.add).then_inc(sum2_ready, 1)
                pool.wait_ge(sum2_ready, 2 * (2 * t + i) + 2)
                wait_used(pool, ss_ready, t, 1)
                pool.tensor_tensor(sums[:, i, :], sum2[:, 0, :], sum2[:, 1, :], ALU.add).then_inc(sums_ready, 1)

            def factors(t):
                pool.wait_ge(var_ready, t + 1)
                wait_used(pool, at_.e_ready, t, 1)
                pool.tensor_tensor(rms[:, :], var[:, :], m.mhalf[:, 0:3], ALU.pow).then_inc(rms_ready, 1)
                pool.wait_ge(rms_ready, t + 1)
                wait_used(pool, rkp_ready, t, 1)
                pool.tensor_tensor(rkd[:, :], m.ident[:, :], rms[:, 2:3].to_broadcast([P, P]), ALU.mult).then_inc(rkd_ready, 1)

            def front(t):
                sum_squares(t, 0)
                sum_squares(t, 1)
                factors(t)

            def head():
                ln.pool(pool)
                split_context(0, 0)
                ln.pool_step(pool, 1, 1)
                split_context(1, 1)
                front(0)

            def step(t, p, has_next):
                at_.subtract_max(pool, t)
                at_.normalise(pool, t)
                if further(t):
                    split_context(t + 2, p)
                if has_next:
                    sum_squares(t + 1, 0)
                if further(t):
                    ln.pool_step(pool, t + 2, p)
                if has_next:
                    sum_squares(t + 1, 1)
                    factors(t + 1)
            over_tiles(pool, head, step)

        @block.scalar
        def _(act):
            def square(t, e):
                act.wait_ge(proj_ready, 12 * t + e + 1)
                if e >= 4:
                    act.wait_ge(sum4_ready, 2 * t + 1)
                else:
                    wait_used(act, sum4_ready, t, 1, 2)
                act.activation(sq[:, e % 4, :], ps[:, bank(e), :], ACT.Square).then_inc(act_left, 1)

            def value(t, p, g):
                act.wait_ge(proj_ready, 12 * t + 8 + g + 1)
                wait_used(act, at_.pv_ready, t, 2, 2)
                act.activation(at_.v[:, p, g * 512:(g + 1) * 512], ps[:, bank(8 + g), :], ACT.Copy,
                               scale=1.0 / WS).then_inc(act_left, 1)

            def head():
                ln.high(act, 0, 0, proj_ready, 12)
                for e in range(8):
                    square(0, e)
                for g in range(4):
                    value(0, 0, g)

            def step(t, p, has_next):
                before = not (isinstance(t, int) and t == 0)
                act.wait_ge(rkp_ready, t + 1)
                wait_used(act, at_.sc_left, t, 1)
                act.copy(rkb[:, :], ps[:, 1, 0:P]).then_inc(rkb_ready, 1)
                if before:
                    at_.copy_transposed(act, t - 1)
                if has_next:
                    ln.high(act, t + 1, 1 - p, proj_ready, 12)
                    square(t + 1, 0)
                if before:
                    at_.high(act, t - 1, 0)
                act.wait_ge(rms_ready, t + 1)
                at_.exponential(act, t, (rms[:, 0:1], rms[:, 1:2]))
                if has_next:
                    square(t + 1, 1)
                    square(t + 1, 2)
                if before:
                    at_.high(act, t - 1, 1)
                if has_next:
                    for e in range(3, 8):
                        square(t + 1, e)
                    for g in range(4):
                        value(t + 1, 1 - p, g)
            over_tiles(act, head, step)
            at_.copy_transposed(act, TILES - 1)
            at_.high(act, TILES - 1, 0)
            at_.high(act, TILES - 1, 1)

        @block.vector
        def _(dve):
            ch = Chain(dve, chain, 2, 2, 1)

            def leave(t, e):
                dve.wait_ge(act_left, 12 * t + e + 1)
                wait_used(dve, at_.sc_ready, t, 1)
                g = e % 4
                src = ps[:, bank(e), :].rearrange("p (h s) -> p h s", s=P)
                if e >= 4:
                    ins = dve.tensor_tensor(q[:, 4 * g:4 * g + 4, :], src, spread(qk_scale[:, 4 * g:4 * g + 4], P), ALU.mult)
                else:
                    ins = dve.tensor_copy(k[:, 4 * g:4 * g + 4, :], src)
                ins.then_inc(dve_left, 1)

            def variances(t):
                dve.wait_ge(ss_ready, t + 1)
                wait_used(dve, rms_ready, t, 1)
                dve.tensor_scalar(var[:, 2:3], ps[:, 1, 2:3], 1.0 / NI, RMS_EPS * WS * WS, ALU.mult, ALU.add)
                dve.tensor_scalar(var[:, 0:2], ps[:, 1, 0:2], HD / NI, HD * RMS_EPS * WS * WS,
                                  ALU.mult, ALU.add).then_inc(var_ready, 1)

            def head():
                dve.wait_ge(const_in, 32)
                dve.tensor_tensor(qk_scale[:, :], qs[:, 0, :], qs[:, 1, :], ALU.mult).then_inc(scale_set, 1)
                ln.stats(dve, ch, 0, 0)
                ln.normalise(dve, 0, 0)
                ln.stats(dve, ch, 1, 1)
                ln.normalise(dve, 1, 1)
                ln.low(dve, 0, 0)
                dve.wait_ge(scale_set, 1)
                for e in range(8):
                    leave(0, e)
                variances(0)

            def step(t, p, has_next):
                ch.tile(t)
                before = not (isinstance(t, int) and t == 0)
                if has_next:
                    ln.low(dve, t + 1, 1 - p)
                dve.wait_ge(at_.sc_ready, t + 1)
                dve.wait_ge(rkb_ready, t + 1)
                wait_used(dve, at_.e_ready, t, 1)
                by_k = lambda a: a.rearrange("p (k b) s -> p k (b s)", b=2)
                dve.tensor_tensor(by_k(at_.s[:, :, :]), by_k(at_.sc), repeat(rkb[:, :], PAIRS), ALU.mult).then_inc(at_.sc_left, 1)
                dve.wait_ge(at_.sc_left, t + 1)
                at_.take_max(dve)
                if has_next:
                    leave(t + 1, 0)
                if before:
                    at_.low(dve, t - 1, 0)
                at_.denominator(dve, ch, t)
                if has_next:
                    leave(t + 1, 1)
                    leave(t + 1, 2)
                if before:
                    at_.low(dve, t - 1, 1)
                if has_next:
                    leave(t + 1, 3)
                    leave(t + 1, 4)
                if further(t):
                    ln.stats(dve, ch, t + 2, p)
                if has_next:
                    leave(t + 1, 5)
                if before:
                    at_.add(dve, t - 1, bo[:, :])
                if has_next:
                    leave(t + 1, 6)
                    leave(t + 1, 7)
                if further(t):
                    ln.normalise(dve, t + 2, p)
                if has_next:
                    variances(t + 1)
            over_tiles(dve, head, step)
            at_.low(dve, TILES - 1, 0)
            at_.low(dve, TILES - 1, 1)
            at_.add(dve, TILES - 1, bo[:, :])

        @block.tensor
        def _(pe):
            def project_heads(t, p, e, w, bias, operand):
                g = e % 4
                for h in range(4):
                    cols = slice((4 * g + h) * HD, (4 * g + h + 1) * HD)
                    out = ps[:, bank(e), h * P:(h + 1) * P]
                    for c in range(KC):
                        mm3(pe, out, (w[0][:, c, cols], w[1][:, c, cols]), operand(p, c), c == 0, False)
                    last = pe.matmul(out, bias[:, cols], m.onesh[0:BR, :], start=False, stop=True)
                last.then_inc(proj_ready, 1)

            def context(p, c):
                return chi[:, p, c, :], clo[:, p, c, :]

            def front(t, p, groups):
                for e in groups:
                    if e == 0:
                        pe.wait_ge(clo_ready, t + 1)
                        wait_used(pe, rkb_ready, t, 1)
                    if e == 3:
                        pe.wait_ge(ln.xl_ready, t + 1)
                    if e >= 4:
                        pe.wait_ge(dve_left, 8 * t + e - 3)
                    else:
                        wait_used(pe, act_left, t, 1, 12, 9 + e)
                    if e < 4:
                        project_heads(t, p, e, wk, bk, context)
                    elif e < 8:
                        project_heads(t, p, e, wq, bq, ln.operand)
                    else:
                        cols = slice((e - 8) * 512, (e - 7) * 512)
                        out = ps[:, bank(e), :]
                        for c in range(KC):
                            mm3(pe, out, context(p, c), (wv[0][:, c, cols], wv[1][:, c, cols]), c == 0, False)
                        pe.matmul(out, m.onesh[0:BR, :], bv[:, cols], start=False, stop=True).then_inc(proj_ready, 1)

            def sums_of_squares(t):
                pe.wait_ge(sums_ready, 2 * (t + 1))
                pe.wait_ge(act_left, 12 * t + 9)
                for half in range(2):
                    for b in range(2):
                        pe.matmul(ps[half * SEQ:(half + 1) * SEQ, 1, b:b + 1], sums[:, 1, b * SEQ:(b + 1) * SEQ],
                                  m.ones[:, 0:1], start=True, stop=True)
                pe.matmul(ps[:, 1, 2:3], sums[:, 0, :], m.ones[:, 0:1], start=True, stop=True).then_inc(ss_ready, 1)

            def key_factors(t):
                pe.wait_ge(rkd_ready, t + 1)
                pe.matmul(ps[:, 1, 0:P], m.ones[:, :], rkd[:, :], start=True, stop=True).then_inc(rkp_ready, 1)

            def scores(t):
                pe.wait_ge(dve_left, 8 * (t + 1))
                if not (isinstance(t, int) and t == 0):
                    pe.wait_ge(at_.pt_ready, t)
                for h in range(HEADS):
                    for b in range(2):
                        tok = slice(b * SEQ, (b + 1) * SEQ)
                        rows = slice(h % 2 * SEQ, (h % 2 + 1) * SEQ)
                        last = pe.matmul(at_.sc[rows, h // 2 * 2 + b, :], q[:, h, tok], k[:, h, tok], start=True, stop=True)
                last.then_inc(at_.sc_ready, 1)

            def head():
                ln.transpose(pe, 0, 0)
                front(0, 0, range(12))
                sums_of_squares(0)

            def step(t, p, has_next):
                before = not (isinstance(t, int) and t == 0)
                if before:
                    at_.transpose(pe, t - 1, at_.x_done)
                if has_next:
                    pe.wait_ge(act_left, 12 * (t + 1))
                    ln.transpose(pe, t + 1, 1 - p)
                key_factors(t)
                if has_next:
                    front(t + 1, 1 - p, range(1))
                scores(t)
                if before:
                    at_.values(pe, t - 1, 1 - p, 0)
                if has_next:
                    front(t + 1, 1 - p, range(1, 3))
                if before:
                    at_.project(pe, t - 1, 0)
                    at_.values(pe, t - 1, 1 - p, 1)
                if has_next:
                    front(t + 1, 1 - p, range(3, 5))
                if before:
                    at_.project(pe, t - 1, 1)
                if has_next:
                    front(t + 1, 1 - p, range(5, 12))
                    sums_of_squares(t + 1)
            over_tiles(pe, head, step)
            t, p = TILES - 1, 1
            at_.transpose(pe, t, at_.x_done)
            for r in range(2):
                at_.values(pe, t, p, r)
                at_.project(pe, t, r, True)
AH, AD = 16, 16
AG = P // AD


def attention_mqa(m):
    nc, d = m.nc, m.d
    with ExitStack() as ctx:
        sb = lambda n, s, t=F32: ctx.enter_context(nc.sbuf_tensor("a1_" + n, s, t))
        sem = ctx.enter_context(Semaphores(nc, "a1_"))
        ps = ctx.enter_context(nc.psum_tensor("a1_ps", [P, 8, 512], F32))
        wqk = [sb(f"wqk{i}", [P, KC, 3 * P], F16) for i in range(2)]
        wv = [sb(f"wv{i}", [P, KC, AD], F16) for i in range(2)]
        wo = [sb(f"wo{i}", [P, KC, DM], F16) for i in range(2)]
        flat = lambda w: w[:, :, :].rearrange("p c n -> p (c n)")
        split_weights(m, [(d["a1_qk"], flat(wqk[0]), flat(wqk[1]), 0), (d["a1_v"], flat(wv[0]), flat(wv[1]), 0),
                          (d["a1_o"], flat(wo[0]), flat(wo[1]), 0)], "a1")
        ln = LayerNorm(m, ctx, sem, "a1", ps[:, 0, :])
        qk_bias = sb("qk_bias", [P, 3])
        v_bias = sb("v_bias", [P, AD])
        o_bias = sb("o_bias", [P, DM])
        mask = sb("mask", [P, SEQ])
        maskb = sb("maskb", [P, SEQ], BF16)
        own = sb("own", [P, AG])
        qk = sb("qk", [P, 2, 3, P])
        kd = sb("kd", [P, AG, P])
        v = sb("v", [P, 2, AD])
        s = sb("s", [P, AH, SEQ])
        e = sb("e", [P, AH, SEQ])
        mx = sb("mx", [P, AH])
        den = sb("den", [P, AH])
        rden = sb("rden", [P, AH])
        pt = sb("pt", [P, AG, P])
        o_sb = sb("o_sb", [P, 2, P])
        oh = sb("oh", [P, 2, P], F16)
        ol = sb("ol", [P, 2, P], F16)
        const_in, mask_set, chain = sem("const_in"), sem("mask_set"), sem("chain")
        proj_ready, qk_ready, kd_ready, v_ready = sem("proj_ready"), sem("qk_ready"), sem("kd_ready"), sem("v_ready")
        sc_ready, mx_ready, s_ready, e_ready, den_ready, rden_ready = (
            sem(n) for n in ("sc_ready", "mx_ready", "s_ready", "e_ready", "den_ready", "rden_ready"))
        ptr_ready, pt_ready, pv_ready, o_ready, ot_ready, oh_ready, ol_ready = (
            sem(n) for n in ("ptr_ready", "pt_ready", "pv_ready", "o_ready", "ot_ready", "oh_ready", "ol_ready"))
        y_ready, y_added, x_done = sem("y_ready"), sem("y_added"), sem("x_done")
        proj = ps[:, 1, :]
        ot_ps = ps[:, 2, 0:2 * P].rearrange("p (b n) -> p b n", b=2)
        y = ps[:, 3, 0:DM]
        sc = ps[:, 4:6, :].rearrange("p a (h s) -> p (a h) s", s=SEQ)
        ptp = ps[:, 4:6, :].rearrange("p a (h s) -> p (a h) s", s=P)
        o_ps = ps[:, 6:8, 0:P]
        started = lambda t, lag: not (isinstance(t, int) and t < lag)
        further = lambda t: not (isinstance(t, int) and t + 2 >= TILES)
        block = ctx.enter_context(nc.Block())

        @block.sync
        def _(sp):
            sp.dma_start(qk_bias[:, :], d["a1_bqk"]).then_inc(const_in, 16)
            sp.dma_start(v_bias[:, :], d["a1_bv"].to_broadcast([P, AD])).then_inc(const_in, 16)
            sp.dma_start(o_bias[:, :], d["a1_bo"].to_broadcast([P, DM])).then_inc(const_in, 16)
            sp.dma_start(mask[:, :], d["causal"]).then_inc(const_in, 16)
            sp.dma_start(own[:, :], d["a1_own"]).then_inc(const_in, 16)
            sp.wait_ge(const_in, 80)

        @block.gpsimd
        def _(pool):
            def diagonal_keys(t, p):
                pool.wait_ge(qk_ready, t + 1)
                wait_used(pool, sc_ready, t, 1)
                pool.tensor_tensor(kd[:, :, :], repeat(qk[:, p, 2, :], AG), spread(own[:, :], P), ALU.mult).then_inc(kd_ready, 1)

            def head():
                ln.pool(pool)
                ln.pool_step(pool, 1, 1)
                pool.wait_ge(const_in, 80)
                diagonal_keys(0, 0)

            def step(t, p, has_next):
                if further(t):
                    ln.pool_step(pool, t + 2, p)
                if has_next:
                    diagonal_keys(t + 1, 1 - p)
            over_tiles(pool, head, step)

        @block.scalar
        def _(act):
            def query_key(t, p):
                act.wait_ge(proj_ready, t + 1)
                wait_used(act, sc_ready, t, 2)
                for c in range(3):
                    last = act.activation(qk[:, p, c, :], proj[:, c * P:(c + 1) * P], ACT.Identity,
                                          scale=1.0 / WS, bias=qk_bias[:, c:c + 1])
                last.then_inc(qk_ready, 1)

            def copy_transposed(t):
                act.wait_ge(ptr_ready, t + 1)
                wait_used(act, pv_ready, t, 1)
                act.copy(pt[:, :, :], ptp).then_inc(pt_ready, 1)

            def exponential(t):
                act.wait_ge(s_ready, t + 1)
                wait_used(act, ptr_ready, t, 1)
                wait_used(act, den_ready, t, 1)
                act.activation(e[:, :, :], s[:, :, :], ACT.Exp, scale=AD ** -0.5).then_inc(e_ready, 1)

            def high(t):
                act.wait_ge(ot_ready, t + 1)
                wait_used(act, y_ready, t, 1)
                act.copy(oh[:, :, :].rearrange("p c (b s) -> p b c s", b=2),
                         ot_ps.rearrange("p b (c s) -> p b c s", c=2)).then_inc(oh_ready, 1)

            def head():
                act.wait_ge(const_in, 80)
                ln.high(act, 0, 0, proj_ready)
                query_key(0, 0)

            def step(t, p, has_next):
                if started(t, 1):
                    copy_transposed(t - 1)
                if has_next:
                    ln.high(act, t + 1, 1 - p, proj_ready)
                    query_key(t + 1, 1 - p)
                exponential(t)
                if started(t, 1):
                    high(t - 1)
            over_tiles(act, head, step)
            copy_transposed(TILES - 1)
            high(TILES - 1)

        @block.vector
        def _(dve):
            ch = Chain(dve, chain, 2, 1, 1)

            def values(t, p):
                dve.wait_ge(qk_ready, t + 1)
                wait_used(dve, pv_ready, t, 2)
                dve.scalar_tensor_tensor(v[:, p, :], proj[:, 3 * P:3 * P + AD], 1.0 / WS, v_bias[:, :],
                                         ALU.mult, ALU.add).then_inc(v_ready, 1)

            def maximum(t):
                dve.wait_ge(sc_ready, t + 1)
                dve.reduce_max(mx[:, :], sc, AX).then_inc(mx_ready, 1)
                dve.wait_ge(mx_ready, t + 1)
                wait_used(dve, e_ready, t, 1)
                dve.tensor_tensor(s[:, :, :], sc, spread(mx[:, :], SEQ), ALU.subtract).then_inc(s_ready, 1)

            def denominator(t):
                dve.wait_ge(e_ready, t + 1)
                wait_used(dve, o_ready, t, 1)
                dve.reduce_sum(den[:, :], e[:, :, :], AX).then_inc(den_ready, 1)
                dve.wait_ge(den_ready, t + 1)
                dve.reciprocal(rden[:, :], den[:, :]).then_inc(rden_ready, 1)

            def divide(t):
                dve.wait_ge(pv_ready, t + 1)
                dve.wait_ge(rden_ready, t + 1)
                wait_used(dve, ot_ready, t, 1)
                dve.tensor_tensor(o_sb[:, :, :].rearrange("p b (k d) -> p b k d", d=AD),
                                  o_ps.rearrange("p b (k d) -> p b k d", d=AD),
                                  rden[:, :].rearrange("p (k b o) -> p b k o", b=2, o=1).to_broadcast([P, 2, AG, AD]),
                                  ALU.mult).then_inc(o_ready, 1)

            def low(t):
                dve.wait_ge(oh_ready, t + 1)
                by_b = lambda a: a[:, :, :].rearrange("p c (b s) -> p b c s", b=2)
                dve.tensor_tensor(by_b(ol), ot_ps.rearrange("p b (c s) -> p b c s", c=2), by_b(oh),
                                  ALU.subtract).then_inc(ol_ready, 1)

            def add(t):
                dve.wait_ge(y_ready, t + 1)
                x = m.x_all[:, at(t), :]
                dve.scalar_tensor_tensor(x, y, 1.0 / WS, x, ALU.mult, ALU.add).then_inc(y_added, 1)
                dve.wait_ge(y_added, t + 1)
                dve.tensor_tensor(x, x, o_bias[:, :], ALU.add).then_inc(x_done, 1)

            def head():
                ln.stats(dve, ch, 0, 0)
                ln.normalise(dve, 0, 0)
                ln.stats(dve, ch, 1, 1)
                ln.normalise(dve, 1, 1)
                dve.wait_ge(const_in, 80)
                dve.tensor_copy(maskb[:, :], mask[:, :]).then_inc(mask_set, 1)
                ln.low(dve, 0, 0)
                values(0, 0)

            def step(t, p, has_next):
                ch.tile(t)
                if has_next:
                    ln.low(dve, t + 1, 1 - p)
                if started(t, 2):
                    add(t - 2)
                if further(t):
                    ln.stats(dve, ch, t + 2, p)
                if further(t):
                    ln.normalise(dve, t + 2, p)
                maximum(t)
                if started(t, 1):
                    divide(t - 1)
                if has_next:
                    values(t + 1, 1 - p)
                denominator(t)
                if started(t, 1):
                    low(t - 1)
            over_tiles(dve, head, step)
            divide(TILES - 1)
            low(TILES - 1)
            add(TILES - 2)
            add(TILES - 1)

        @block.tensor
        def _(pe):
            def front(t, p):
                pe.wait_ge(ln.xl_ready, t + 1)
                wait_used(pe, v_ready, t, 1)
                for j in range(3):
                    cols = slice(j * P, (j + 1) * P)
                    for c in range(KC):
                        mm3(pe, proj[:, cols], (wqk[0][:, c, cols], wqk[1][:, c, cols]), ln.operand(p, c),
                            c == 0, c == KC - 1)
                for c in range(KC):
                    last = mm3(pe, proj[:, 3 * P:3 * P + AD], ln.operand(p, c), (wv[0][:, c, :], wv[1][:, c, :]),
                               c == 0, c == KC - 1)
                last.then_inc(proj_ready, 1)

            def scores(t, p):
                pe.wait_ge(kd_ready, t + 1)
                if started(t, 1):
                    pe.wait_ge(pt_ready, t)
                for a in range(2):
                    for c in range(2):
                        rows = slice(c * SEQ, (c + 1) * SEQ)
                        for b in range(2):
                            tok = slice(b * SEQ, (b + 1) * SEQ)
                            out = sc[rows, a * 8 + b:a * 8 + 8:2, :]
                            pe.matmul(out, m.identb[:, rows], repeat(maskb[:, :], 4), start=True, stop=False)
                            last = pe.matmul(out, qk[:, p, c, tok], kd[:, 4 * a:4 * a + 4, tok], start=False, stop=True)
                last.then_inc(sc_ready, 1)

            def transpose(t):
                pe.wait_ge(e_ready, t + 1)
                pe.wait_ge(s_ready, t + 1)
                for k in range(AG):
                    last = pe.transpose(ptp[:, k, :], e[:, 2 * k:2 * k + 2, :].rearrange("p b s -> p (b s)"), m.ident[:, :])
                last.then_inc(ptr_ready, 1)

            def products(t, p):
                pe.wait_ge(pt_ready, t + 1)
                pe.wait_ge(v_ready, t + 1)
                wait_used(pe, o_ready, t, 1)
                for b in range(2):
                    rows = slice(b * SEQ, (b + 1) * SEQ)
                    for k in range(AG):
                        last = pe.matmul(o_ps[:, b, k * AD:(k + 1) * AD], pt[rows, k, :], v[rows, p, :], start=True, stop=True)
                last.then_inc(pv_ready, 1)

            def transpose_o(t):
                pe.wait_ge(o_ready, t + 1)
                wait_used(pe, ol_ready, t, 1)
                for b in range(2):
                    last = pe.transpose(ot_ps[:, b, :], o_sb[:, b, :], m.ident[:, :])
                last.then_inc(ot_ready, 1)

            def output(t):
                pe.wait_ge(ol_ready, t + 1)
                wait_used(pe, x_done, t, 1)
                for c in range(2):
                    last = mm3(pe, y, (oh[:, c, :], ol[:, c, :]), (wo[0][:, c, :], wo[1][:, c, :]), c == 0, c == 1)
                last.then_inc(y_ready, 1)

            def head():
                ln.transpose(pe, 0, 0)
                front(0, 0)
                pe.wait_ge(mask_set, 1)

            def step(t, p, has_next):
                if started(t, 1):
                    transpose(t - 1)
                if has_next:
                    ln.transpose(pe, t + 1, 1 - p)
                if started(t, 2):
                    output(t - 2)
                if has_next:
                    front(t + 1, 1 - p)
                scores(t, p)
                if started(t, 1):
                    products(t - 1, 1 - p)
                    transpose_o(t - 1)
            over_tiles(pe, head, step)
            transpose(TILES - 1)
            output(TILES - 2)
            products(TILES - 1, 1)
            transpose_o(TILES - 1)
            output(TILES - 1)


FF = 704
QMAX, Q_EPS = 127.0, 1e-8
ROUND = 1.5 * 2.0 ** 23


def ffn_quantised(m):
    nc, d = m.nc, m.d
    G1, C2 = 2 * FF // P, -(-FF // P)
    tail = FF - (C2 - 1) * P
    with ExitStack() as ctx:
        sb = lambda n, s, t=F32: ctx.enter_context(nc.sbuf_tensor("f1_" + n, s, t))
        sem = ctx.enter_context(Semaphores(nc, "f1_"))
        ps = ctx.enter_context(nc.psum_tensor("f1_ps", [P, 8, 512], F32))
        w1 = sb("w1", [P, KC, 2 * FF], BF16)
        w2 = sb("w2", [P, C2, DM], BF16)
        s1 = sb("s1", [P, 2 * FF])
        s2 = sb("s2", [P, DM])
        with ExitStack() as c1:
            quantise_weights(m, c1, ps, w1, w2, s1, s2)
        ln = LayerNorm(m, ctx, sem, "f1", ps[:, 0, :])
        stat = sb("stat", [P, 2, 3])
        hstat = sb("hstat", [P, 3])
        xr = sb("xr", [P, DM])
        xq = sb("xq", [P, 2, DM], BF16)
        xt = sb("xt", [P, 2, KC, P], BF16)
        gate = sb("gate", [P, FF])
        up = sb("up", [P, FF])
        ex = sb("ex", [P, FF])
        hq = sb("hq", [P, C2 * P], BF16)
        ht = sb("ht", [P, C2, P], BF16)
        yt = sb("yt", [P, DM])
        chain, zeroed, gup = sem("chain"), sem("zeroed"), sem("gup_ready")
        xq_ready, xtp_ready, xt_ready, gu_ready, gate_ready, up_ready, ex_ready, hq_ready = (
            sem(n) for n in ("xq_ready", "xtp_ready", "xt_ready", "gu_ready", "gate_ready", "up_ready", "ex_ready", "hq_ready"))
        htp_ready, ht_ready, y_ready, x_done, den_ready = (sem(n) for n in ("htp_ready", "ht_ready", "y_ready", "x_done", "den_ready"))
        HF = FF // 2
        gate_ps, up_ps = ps[:, 1:3, 0:HF], ps[:, 3:5, 0:HF]
        xt_ps = ps[:, 0, 0:DM // 2].bitcast(BF16)
        ht_ps = ps[:, 5, 0:C2 * P // 2].bitcast(BF16)
        y_ps = lambda p: ps[:, 6 + p, 0:DM]
        halves = lambda a: a.rearrange("p (k n) -> p k n", k=2)
        block = ctx.enter_context(nc.Block())

        @block.gpsimd
        def _(pool):
            def step(t, p, has_next):
                if has_next:
                    ln.pool_step(pool, t + 1, 1 - p)
                pool.wait_ge(up_ready, t + 1)
                pool.wait_ge(ex_ready, t + 1)
                pool.tensor_tensor(gate[:, :], gate[:, :], up[:, :], ALU.mult).then_inc(gup, 1)
            over_tiles(pool, lambda: ln.pool(pool), step)

        @block.scalar
        def _(act):
            def x_transposed(t, p):
                act.wait_ge(xtp_ready, t + 1)
                wait_used(act, gu_ready, t, 2)
                act.copy(xt[:, p].rearrange("p c s -> p (c s)"), xt_ps).then_inc(xt_ready, 1)

            def step(t, p, has_next):
                act.wait_ge(gate_ready, t + 1)
                wait_used(act, hq_ready, t, 1)
                act.activation(ex[:, :], gate[:, :], ACT.Exp, scale=-1.0).then_inc(ex_ready, 1)
                if has_next:
                    x_transposed(t + 1, 1 - p)
                act.wait_ge(htp_ready, t + 1)
                wait_used(act, y_ready, t, 1)
                act.copy(ht[:, :, :].rearrange("p c s -> p (c s)"), ht_ps).then_inc(ht_ready, 1)
            over_tiles(act, lambda: x_transposed(0, 0), step)

        @block.vector
        def _(dve):
            ch = Chain(dve, chain, 5, 14)

            def scale(v, st):
                ch.link(dve.tensor_reduce(st[:, 0:1], v, AX, ALU.max, apply_absolute_value=True))
                ch.link(dve.tensor_scalar(st[:, 1:2], st[:, 0:1], 1.0 / QMAX, Q_EPS, ALU.mult, ALU.max))
                ch.link(dve.reciprocal(st[:, 2:3], st[:, 1:2]))

            def quantise_x(t, p):
                ln.stats(dve, ch, t, p)
                ln.normalise(dve, t, p)
                dve.wait_ge(ln.xn_ready, t + 1)
                scale(ln.xn[:, p], stat[:, p])
                ch.link(dve.tensor_scalar(xr[:, :], ln.xn[:, p], stat[:, p, 2:3], ROUND, ALU.mult, ALU.add))
                wait_used(dve, xtp_ready, t, 2)
                dve.tensor_scalar(xq[:, p], xr[:, :], -ROUND, None, ALU.add).then_inc(xq_ready, 1)

            def head():
                dve.memset(hq[:, :], 0.0).then_inc(zeroed, 1)
                dve.wait_ge(zeroed, 1)
                quantise_x(0, 0)

            def step(t, p, has_next):
                ch.tile(t)
                dve.wait_ge(gu_ready, t + 1)
                wait_used(dve, hq_ready, t, 1)
                dve.scalar_tensor_tensor(halves(gate[:, :]), gate_ps, stat[:, p, 1:2], halves(s1[:, 0:FF]),
                                         ALU.mult, ALU.mult).then_inc(gate_ready, 1)
                dve.scalar_tensor_tensor(halves(up[:, :]), up_ps, stat[:, p, 1:2], halves(s1[:, FF:]),
                                         ALU.mult, ALU.mult).then_inc(up_ready, 1)
                if has_next:
                    quantise_x(t + 1, 1 - p)
                dve.wait_ge(ex_ready, t + 1)
                ch.link(dve.tensor_scalar(ex[:, :], ex[:, :], 1.0, None, ALU.add))
                ch.link(dve.reciprocal(ex[:, :], ex[:, :]))
                dve.wait_ge(gup, t + 1)
                ch.link(dve.tensor_tensor(gate[:, :], gate[:, :], ex[:, :], ALU.mult))
                scale(gate[:, :], hstat[:, :])
                ch.link(dve.tensor_scalar(gate[:, :], gate[:, :], hstat[:, 2:3], ROUND, ALU.mult, ALU.add))
                wait_used(dve, htp_ready, t, 1)
                dve.tensor_scalar(hq[:, 0:FF], gate[:, :], -ROUND, None, ALU.add).then_inc(hq_ready, 1)
                dve.wait_ge(y_ready, t + 1)
                ch.link(dve.scalar_tensor_tensor(yt[:, :], y_ps(p), hstat[:, 1:2], s2[:, :], ALU.mult, ALU.mult))
                x = m.x_all[:, at(t), :]
                ch.link(dve.tensor_tensor(x, x, yt[:, :], ALU.add))
                dve.memset(ln.turn[:, :], 0.0).then_inc(x_done, 1)
            over_tiles(dve, head, step)

        @block.tensor
        def _(pe):
            def x_transpose(t, p):
                pe.wait_ge(xq_ready, t + 1)
                wait_used(pe, xt_ready, t, 1)
                for c in range(KC):
                    last = pe.transpose(xt_ps[:, c * P:(c + 1) * P], xq[:, p, c * P:(c + 1) * P], m.identb[:, :])
                last.then_inc(xtp_ready, 1)

            def step(t, p, has_next):
                pe.wait_ge(xt_ready, t + 1)
                wait_used(pe, up_ready, t, 1)
                for c in range(KC):
                    for k in range(4):
                        last = pe.matmul(ps[:, 1 + k, 0:HF], xt[:, p, c, :], w1[:, c, k * HF:(k + 1) * HF],
                                         start=c == 0, stop=c == KC - 1)
                last.then_inc(gu_ready, 1)
                if has_next:
                    x_transpose(t + 1, 1 - p)
                pe.wait_ge(hq_ready, t + 1)
                wait_used(pe, ht_ready, t, 1)
                for c in range(C2):
                    last = pe.transpose(ht_ps[:, c * P:(c + 1) * P], hq[:, c * P:(c + 1) * P], m.identb[:, :])
                last.then_inc(htp_ready, 1)
                pe.wait_ge(ht_ready, t + 1)
                wait_used(pe, x_done, t, 2)
                for c in range(C2):
                    k = P if c < C2 - 1 else tail
                    last = pe.matmul(y_ps(p), ht[0:k, c, :], w2[0:k, c, :], start=c == 0, stop=c == C2 - 1)
                last.then_inc(y_ready, 1)
            over_tiles(pe, lambda: x_transpose(0, 0), step)


def quantise_weights(m, ctx, ps, w1, w2, s1, s2):
    nc, d = m.nc, m.d
    G1, C2 = 2 * FF // P, -(-FF // P)
    sb = lambda n, s, t=F32: ctx.enter_context(nc.sbuf_tensor("fw_" + n, s, t))
    sem = ctx.enter_context(Semaphores(nc, "fw_"))
    wa = sb("wa", [P, G1, DM])
    wb = sb("wb", [P, KC, FF])
    qa = sb("qa", [P, G1, DM], BF16)
    qb = sb("qb", [P, KC, FF], BF16)
    NS = G1 + KC
    st = sb("st", [P, 3, NS])
    diag = sb("diag", [P, NS, P])
    loaded, chain, q_ready, diag_ready = sem("loaded"), sem("chain"), sem("q_ready"), sem("diag_ready")
    t_ready, t_left, r_ready, r_left = sem("t_ready"), sem("t_left"), sem("r_ready"), sem("r_left")
    jobs = [(qa[:, j, c * P:(c + 1) * P], P, w1[:, c, j * P:(j + 1) * P]) for j in range(G1) for c in range(KC)]
    jobs += [(qb[:, j, c * P:min(FF, (c + 1) * P)], min(FF, (c + 1) * P) - c * P, w2[0:min(FF, (c + 1) * P) - c * P, c, j * P:(j + 1) * P])
             for j in range(KC) for c in range(C2)]
    rows = [s1[:, j * P:(j + 1) * P] for j in range(G1)] + [s2[:, j * P:(j + 1) * P] for j in range(KC)]
    block = ctx.enter_context(nc.Block())

    @block.sync
    def _(sp):
        sp.dma_start(wa[:, :, :], d["f1_gu"].rearrange("p (j n) -> p j n", n=DM)).then_inc(loaded, 16)
        sp.dma_start(wb[:, :, :], d["f1_down"].rearrange("p (j n) -> p j n", n=FF)).then_inc(loaded, 16)
        sp.wait_ge(loaded, 32)

    @block.vector
    def _(dve):
        k = [0]

        def link(ins):
            k[0] += 1
            ins.then_inc(chain, 1)
            dve.wait_ge(chain, k[0])

        dve.wait_ge(loaded, 32)
        dve.tensor_reduce(st[:, 0, 0:G1], wa[:, :, :], AX, ALU.max, apply_absolute_value=True)
        link(dve.tensor_reduce(st[:, 0, G1:], wb[:, :, :], AX, ALU.max, apply_absolute_value=True))
        link(dve.tensor_scalar(st[:, 1, :], st[:, 0, :], 1.0 / QMAX, Q_EPS, ALU.mult, ALU.max))
        link(dve.reciprocal(st[:, 2, :], st[:, 1, :]))
        for j in range(G1):
            dve.tensor_scalar(wa[:, j, :], wa[:, j, :], st[:, 2, j:j + 1], ROUND, ALU.mult, ALU.add)
        for j in range(KC):
            last = dve.tensor_scalar(wb[:, j, :], wb[:, j, :], st[:, 2, G1 + j:G1 + j + 1], ROUND, ALU.mult, ALU.add)
        link(last)
        dve.tensor_scalar(qa[:, :, :], wa[:, :, :], -ROUND, None, ALU.add)
        dve.tensor_scalar(qb[:, :, :], wb[:, :, :], -ROUND, None, ALU.add).then_inc(q_ready, 1)
        dve.tensor_tensor(diag[:, :, :], repeat(m.ident[:, :], NS), spread(st[:, 1, :], P), ALU.mult).then_inc(diag_ready, 1)
        for i, (_, n, dst) in enumerate(jobs):
            dve.wait_ge(t_ready, i + 1)
            dve.tensor_copy(dst, ps[0:n, i % 4, 0:P // 2].bitcast(BF16)).then_inc(t_left, 1)

    @block.scalar
    def _(act):
        for i, dst in enumerate(rows):
            act.wait_ge(r_ready, i + 1)
            act.copy(dst, ps[:, 4 + i % 4, 0:P]).then_inc(r_left, 1)

    @block.tensor
    def _(pe):
        pe.wait_ge(q_ready, 1)
        for i, (src, n, _) in enumerate(jobs):
            if i >= 4:
                pe.wait_ge(t_left, i - 3)
            pe.transpose(ps[0:n, i % 4, 0:P // 2].bitcast(BF16), src, m.identb[:, :]).then_inc(t_ready, 1)
        pe.wait_ge(diag_ready, 1)
        for i in range(NS):
            if i >= 4:
                pe.wait_ge(r_left, i - 3)
            pe.matmul(ps[:, 4 + i % 4, 0:P], m.ones[:, :], diag[:, i, :], start=True, stop=True).then_inc(r_ready, 1)


BUILDERS = {0: attention_gqa, 1: attention_features, 2: ffn_lora, 3: attention_mqa, 4: attention_cross, 5: ffn_quantised}


def decoder_kernel(nc, d):
    with ExitStack() as ctx:
        m = Machine(nc, ctx, d)
        load_resident(m)
        for phase in PHASES:
            BUILDERS[phase](m)
        store_result(m)


def host_layout(i):
    f = lambda a: np.ascontiguousarray(a)
    a = {k: np.asarray(v) for k, v in i.items()}
    kmajor = lambda w: f(w.reshape(KC, P, -1).transpose(1, 0, 2).reshape(P, -1))
    out = {"x": f(a["x"].reshape(-1, DM)), "ident": np.eye(P, dtype=np.float32)}
    out["ffn0_base"] = kmajor(a["L0_ffn_W_base"].T)
    out["ffn0_a"] = kmajor(np.concatenate([a["L0_ffn_A"].reshape(-1, DM).T, a["L0_ffn_router_W"].T], 1))
    out["ffn0_b"] = f(a["L0_ffn_Bw"].transpose(0, 2, 1).reshape(P, DM))
    out["ffn0_bias"] = f(a["L0_ffn_b_base"].reshape(1, DM))
    out["desc"] = np.broadcast_to(np.arange(EXPERTS, 0, -1, dtype=np.float32), (P, EXPERTS)).copy()
    qkv = a["L0_attn_w_qkv"]
    nq, nk = HEADS * HD, KV * HD
    swap = lambda v, axis=0: np.concatenate(np.split(v, 2, axis)[::-1], axis)
    wk = qkv[nq:nq + nk]
    out["a0_q"] = kmajor(qkv[:nq].T)
    out["a0_k"] = kmajor(wk.T)
    out["a0_ks"] = kmajor(swap(wk.reshape(KV, HD, DM), 1).reshape(nk, DM).T)
    out["a0_v"] = kmajor(qkv[nq + nk:].T)
    out["a0_o"] = f(a["L0_attn_w_o"].T.reshape(HEADS, HD, DM).transpose(1, 0, 2).reshape(P, -1))
    qg, qb, kg, kb = (a["L0_attn_" + n] for n in ("qn_g", "qn_b", "kn_g", "kn_b"))
    out["a0_gb"] = f(np.stack([qg, qb, swap(qb), kg, kb, swap(kg), swap(kb), kb], 1))
    inv = (1.0 / np.float32(1e6) ** (np.arange(0, HD, 2, dtype=np.float32) / np.float32(HD))).astype(np.float32)
    ang = np.concatenate([inv, inv])[:, None] * np.arange(SEQ, dtype=np.float32)[None]
    sgn = np.where(np.arange(HD) < HD // 2, -1.0, 1.0)[:, None]
    out["rope"] = np.stack([np.cos(ang), sgn * np.sin(ang), -sgn * np.sin(ang)], 1).astype(np.float32)
    out["causal"] = np.tile(np.triu(np.full((SEQ, SEQ), NEG), 1), (2, 1)).astype(np.float32)
    x1 = {n: a["L1_xattn_" + n] for n in ("q_w", "ki_w", "vi_w", "o_w", "q_b", "ki_b", "vi_b", "o_b", "nq_s", "nki_s")}
    for n, k in (("q", "q_w"), ("k", "ki_w"), ("v", "vi_w")):
        out["x1_" + n] = kmajor(x1[k])
    out["x1_o"] = f(x1["o_w"].reshape(HEADS, HD, DM).transpose(1, 0, 2).reshape(P, -1))
    for n, k in (("bq", "q_b"), ("bk", "ki_b"), ("bv", "vi_b"), ("bo", "o_b")):
        out["x1_" + n] = f(x1[k].reshape(1, -1))
    out["x1_scales"] = f(np.stack([x1["nq_s"].reshape(HEADS, HD).T, x1["nki_s"].reshape(HEADS, HD).T], 1))
    c = a["ctx_2048"].reshape(-1, P, DM)
    out["ctx_t"] = f(c.transpose(0, 2, 1).reshape(-1, KC, P, P).transpose(0, 2, 1, 3).reshape(-1, P, DM))
    out["ctx"] = f(c)
    v = c.transpose(0, 2, 1).reshape(-1, KC, P, XU, XT).transpose(0, 2, 1, 3, 4)
    out["ctx_v"] = f(np.concatenate([v, np.ones_like(v[..., :1])], -1).reshape(-1, P, KC * XU * VC))
    sel = np.zeros((P, 4, XG, 4, 32), np.float32)
    one = np.zeros((4, 32, 1), np.float32)
    one[:, 3 * XT] = 1.0
    for tok in range(P):
        g, jj, i = tok // 32, tok % 32 // XT, tok % XT
        for part, thirds in enumerate(((0, 1), (2,), (0, 2), (1,))):
            for r in thirds:
                sel[tok, part, g, jj, r * XT + i] = 1.0
    out["x0_sel"] = sel.reshape(P, 4, XG * P)
    out["x0_one"] = one.reshape(P, 1)
    w1 = a["L1_attn_Wqkv_w"]
    bias = a["L1_attn_Wqkv_b"]
    wk = np.tile(w1[DM:DM + AD], (AG, 1))
    out["a1_qk"] = kmajor(np.concatenate([w1[:DM], wk], 0).T)
    out["a1_v"] = kmajor(w1[DM + AD:].T)
    out["a1_o"] = kmajor(a["L1_attn_out_w"].T)
    out["a1_bqk"] = f(np.concatenate([bias[:DM], np.tile(bias[DM:DM + AD], AG)]).reshape(3, P).T)
    out["a1_bv"] = f(bias[DM + AD:].reshape(1, AD))
    out["a1_bo"] = f(a["L1_attn_out_b"].reshape(1, DM))
    out["a1_own"] = np.kron(np.eye(AG), np.ones((AD, 1))).astype(np.float32)
    rows = lambda w: f(w.reshape(-1, P, w.shape[1]).transpose(1, 0, 2).reshape(P, -1))
    out["f1_gu"] = rows(a["L1_ffn_w_gate_up"])
    out["f1_down"] = rows(a["L1_ffn_w_down"])
    return out


def kernel(**inputs):
    import concourse.bacc as _bacc
    from concourse.bass_utils import run_bass_kernel_spmd as _run

    nc = _bacc.Bacc("TRN2", target_bir_lowering=False, num_devices=1)
    arrays, d = {}, {}
    for name, a in host_layout(inputs).items():
        arrays[f"in_{name}"] = a
        d[name] = nc.dram_tensor(f"in_{name}", a.shape, F32, kind="ExternalInput").ap()
    d["out"] = nc.dram_tensor("out_x", (64 * SEQ, DM), F32, kind="ExternalOutput").ap()
    decoder_kernel(nc, d)
    r = _run(nc, [arrays], core_ids=[0])
    return r.results[0]["out_x"].reshape(64, SEQ, DM)
```

```python
from contextlib import ExitStack

import numpy as np
import concourse.bass as bass
from concourse import mybir
from concourse.alu_op_type import AluOpType as ALU

F32 = mybir.dt.float32
F16 = mybir.dt.float16
BF16 = mybir.dt.bfloat16
ACT = mybir.ActivationFunctionType
AX = mybir.AxisListType.X

P = 128
TILES = 32
SEQ = 64
DM = 256
KC = DM // P
WS = 64.0
LN_EPS = 1e-5
NEG = -1.0e30


def over_tiles(eng, head, step):
    head()
    step(0, 0, True)
    step(1, 1, TILES > 2)
    if TILES > 4:
        with eng.Fori(1, TILES // 2 - 1) as i:
            step(2 * i, 0, True)
            step(2 * i + 1, 1, True)
    if TILES > 2:
        step(TILES - 2, 0, True)
        step(TILES - 1, 1, False)


def wait_used(eng, sem, t, buffers, per_tile=1, last=0):
    if isinstance(t, int) and t < buffers:
        return
    eng.wait_ge(sem, (t - buffers) * per_tile + (last or per_tile))


class Semaphores:

    def __init__(self, nc, tag):
        self.nc, self.tag, self.stack, self.all = nc, tag, ExitStack(), []

    def __enter__(self):
        return self

    def __call__(self, name):
        self.all.append(self.stack.enter_context(self.nc.semaphore(self.tag + name)))
        return self.all[-1]

    def __exit__(self, *error):
        if error[0] is None:
            with self.nc.Block() as block:
                @block.sync
                def _(sp):
                    for s in self.all:
                        sp.sem_clear(s)
        self.stack.close()


class Chain:

    def __init__(self, eng, sem, head, each, ahead=0):
        self.eng, self.sem, self.head, self.each, self.ahead, self.k, self.base = eng, sem, head, each, ahead, 0, 0

    def tile(self, t):
        assert not isinstance(t, int) or t or self.k == self.head
        self.base, self.k = self.head + t * self.each, 0
        if isinstance(t, int) and t == TILES - 1:
            self.base -= self.ahead

    def link(self, ins):
        ins.then_inc(self.sem, 1)
        self.k += 1
        self.eng.wait_ge(self.sem, self.base + self.k)


def mm3(pe, out, a, b, start, stop):
    pe.matmul(out, a[0], b[0], start=start, stop=False)
    pe.matmul(out, a[0], b[1], start=False, stop=False)
    return pe.matmul(out, a[1], b[0], start=False, stop=stop)


class Machine:

    def __init__(self, nc, ctx, d):
        self.nc, self.d = nc, d
        self.x_all = ctx.enter_context(nc.sbuf_tensor("x_all", [P, TILES, DM], F32))
        self.ident = ctx.enter_context(nc.sbuf_tensor("ident", [P, P], F32))
        self.identb = ctx.enter_context(nc.sbuf_tensor("identb", [P, P], BF16))
        self.ones = ctx.enter_context(nc.sbuf_tensor("ones", [P, P], F32))
        self.ones2 = ctx.enter_context(nc.sbuf_tensor("ones2", [P, DM], F32))
        self.onesh = ctx.enter_context(nc.sbuf_tensor("onesh", [P, P], F16))
        self.onesb = ctx.enter_context(nc.sbuf_tensor("onesb", [P, 1], BF16))
        self.mhalf = ctx.enter_context(nc.sbuf_tensor("mhalf", [P, 32], F32))


def load_resident(m):
    nc = m.nc
    with ExitStack() as ctx:
        sem = ctx.enter_context(Semaphores(nc, "in_"))
        x_in, id_in = sem("x_in"), sem("id_in")
        block = ctx.enter_context(nc.Block())

        @block.sync
        def _(sp):
            sp.dma_start(m.ident[:, :], m.d["ident"]).then_inc(id_in, 16)
            for s in range(0, TILES, 4):
                sp.dma_start(m.x_all[:, s:s + 4, :],
                             m.d["x"][s * P:(s + 4) * P, :].rearrange("(t p) d -> p t d", p=P)).then_inc(x_in, 16)
            sp.wait_ge(x_in, 4 * TILES)

        @block.vector
        def _(dve):
            dve.memset(m.ones[:, :], 1.0)
            dve.memset(m.onesh[:, :], 1.0)
            dve.memset(m.onesb[:, :], 1.0)
            dve.memset(m.ones2[:, :], 1.0)
            dve.memset(m.mhalf[:, :], -0.5)
            dve.wait_ge(id_in, 16)
            dve.tensor_copy(m.identb[:, :], m.ident[:, :])


STAGE = 2048


def split_weights(m, jobs, tag):
    nc = m.nc
    with ExitStack() as ctx:
        stage = [ctx.enter_context(nc.sbuf_tensor(f"stage{tag}{i}", [P, STAGE], F32)) for i in range(3)]
        mean = ctx.enter_context(nc.sbuf_tensor(f"mean{tag}", [P, STAGE // P], F32))
        sem = ctx.enter_context(Semaphores(nc, tag))
        loaded = [sem(f"w_loaded{i}") for i in range(3)]
        centred, high_done, low_done = sem("w_centred"), sem("w_high"), sem("w_low")
        pieces = []
        for src, hi, lo, centre in jobs:
            p, n = src.shape
            for c in range(0, n, STAGE):
                e = min(n, c + STAGE)
                pieces.append((p, e - c, src[:, c:e], hi[:, c:e], lo[:, c:e], centre))
        centres = [sum(x[5] for x in pieces[:i + 1]) for i in range(len(pieces))]
        block = ctx.enter_context(nc.Block())

        @block.sync
        def _(sp):
            for i, (p, n, src, hi, lo, centre) in enumerate(pieces):
                if i >= 3:
                    sp.wait_ge(low_done, i - 2)
                sp.dma_start(stage[i % 3][0:p, 0:n], src).then_inc(loaded[i % 3], 16)

        @block.scalar
        def _(act):
            for i, (p, n, src, hi, lo, centre) in enumerate(pieces):
                act.wait_ge(loaded[i % 3], 16 * (i // 3 + 1))
                if centre:
                    act.wait_ge(centred, 3 * centres[i])
                act.activation(hi, stage[i % 3][0:p, 0:n], ACT.Copy, scale=WS).then_inc(high_done, 1)

        @block.vector
        def _(dve):
            def take_means(i):
                if i >= len(pieces) or not pieces[i][5]:
                    return
                w = stage[i % 3][:, 0:pieces[i][1]].rearrange("p (h d) -> p h d", d=P)
                heads = pieces[i][1] // P
                dve.wait_ge(loaded[i % 3], 16 * (i // 3 + 1))
                dve.reduce_sum(mean[:, 0:heads], w, AX).then_inc(centred, 1)
                dve.wait_ge(centred, 3 * centres[i] - 2)
                dve.tensor_scalar(mean[:, 0:heads], mean[:, 0:heads], 1.0 / P, None, ALU.mult).then_inc(centred, 1)
                dve.wait_ge(centred, 3 * centres[i] - 1)
                dve.tensor_tensor(w, w, spread(mean[:, 0:heads], P), ALU.subtract).then_inc(centred, 1)
                dve.wait_ge(centred, 3 * centres[i])

            take_means(0)
            for i, (p, n, src, hi, lo, centre) in enumerate(pieces):
                take_means(i + 1)
                dve.wait_ge(high_done, i + 1)
                dve.scalar_tensor_tensor(lo, stage[i % 3][0:p, 0:n], WS, hi, ALU.mult, ALU.subtract).then_inc(low_done, 1)


def spread(a, n):
    return a.rearrange("p (k o) -> p k o", o=1).to_broadcast([a.shape[0], a.shape[1], n])


def repeat(a, n):
    return a.rearrange("p (o k) -> p o k", o=1).to_broadcast([a.shape[0], n, a.shape[1]])


class LayerNorm:

    def __init__(self, m, ctx, sem, tag, tp):
        nc, self.m, self.tp = m.nc, m, tp
        sb = lambda n, s, t: ctx.enter_context(nc.sbuf_tensor(n + tag, s, t))
        self.st = sb("ln_st", [P, 6], F32)
        self.mv = sb("ln_mv", [P, 2, 2], F32)
        self.ve = sb("ln_ve", [P, 2, 1], F32)
        self.rstd = sb("ln_rstd", [P, 2, 1], F32)
        self.turn = sb("ln_turn", [P, 1], F32)
        self.eps = sb("ln_eps", [P, 1], F32)
        self.xn = sb("ln_xn", [P, 2, DM], F32)
        self.xh = sb("ln_xh", [P, 2, KC, P], F16)
        self.xl = sb("ln_xl", [P, 2, KC, P], F16)
        self.eps_set = sem("eps_set")
        self.mv_ready = sem("mv_ready")
        self.pool_chain = sem("ln_pool")
        self.rstd_ready = sem("rstd_ready")
        self.xn_ready = sem("xn_ready")
        self.tp_ready = sem("tp_ready")
        self.xh_ready = sem("xh_ready")
        self.xl_ready = sem("xl_ready")

    def pool(self, pool):
        pool.memset(self.eps[:, :], LN_EPS).then_inc(self.eps_set, 1)
        pool.wait_ge(self.eps_set, 1)
        self.pool_step(pool, 0, 0)

    def pool_step(self, pool, t, p):
        pool.wait_ge(self.mv_ready, t + 1)
        pool.tensor_tensor(self.ve[:, p], self.mv[:, p, 1:2], self.eps[:, :], ALU.add).then_inc(self.pool_chain, 1)
        pool.wait_ge(self.pool_chain, t + 1)
        pool.tensor_tensor(self.rstd[:, p], self.ve[:, p], self.m.mhalf[:, 0:1], ALU.pow).then_inc(self.rstd_ready, 1)

    def stats(self, dve, ch, t, p):
        ch.link(dve.bn_stats(self.st[:, :], self.m.x_all[:, at(t), :]))
        dve.memset(self.turn[:, :], 0.0)
        dve.bn_aggr(self.mv[:, p], self.st[:, :]).then_inc(self.mv_ready, 1)

    def normalise(self, dve, t, p):
        dve.wait_ge(self.rstd_ready, t + 1)
        dve.wait_ge(self.mv_ready, t + 1)
        dve.tensor_scalar(self.xn[:, p], self.m.x_all[:, at(t), :], self.mv[:, p, 0:1], self.rstd[:, p],
                          ALU.subtract, ALU.mult).then_inc(self.xn_ready, 1)

    def transpose(self, pe, t, p):
        pe.wait_ge(self.xn_ready, t + 1)
        if not (isinstance(t, int) and t < 1):
            pe.wait_ge(self.xl_ready, t)
        for c in range(KC):
            last = pe.transpose(self.tp[:, c * P:(c + 1) * P], self.xn[:, p, c * P:(c + 1) * P], self.m.ident[:, :])
        last.then_inc(self.tp_ready, 1)

    def high(self, act, t, p, used, per_tile=1):
        act.wait_ge(self.tp_ready, t + 1)
        wait_used(act, used, t, 2, per_tile)
        act.copy(self.xh[:, p], self.tp[:, 0:DM]).then_inc(self.xh_ready, 1)

    def low(self, dve, t, p):
        dve.wait_ge(self.xh_ready, t + 1)
        dve.tensor_tensor(self.xl[:, p], self.tp[:, 0:DM], self.xh[:, p], ALU.subtract).then_inc(self.xl_ready, 1)

    def operand(self, p, c, lo=0, n=P):
        return self.xh[:, p, c, lo:lo + n], self.xl[:, p, c, lo:lo + n]


def dram_tile(a, t):
    return a[t, :, :] if isinstance(t, int) else a[bass.ds(t, 1), :, :].rearrange("a p n -> p (a n)")


def at(t):
    return t if isinstance(t, int) else bass.ds(t, 1)

HEADS, HD = 16, 128
KV = 4
REP = HEADS // KV
PAIRS = HEADS // 2
X1_COLS = 4 * KC * HEADS * HD
X1_PIECE = X1_COLS // TILES


class Attend:

    def __init__(self, m, ctx, sem, tag, ps, w_out, v_cols):
        nc, self.m, self.ps, self.w_out, self.v_cols = m.nc, m, ps, w_out, v_cols
        sb = lambda n, s, t=F32: ctx.enter_context(nc.sbuf_tensor(tag + n, s, t))
        self.s = sb("s", [P, HEADS, SEQ])
        self.e = sb("e", [P, HEADS, SEQ])
        self.mx = sb("mx", [P, HEADS])
        self.den = sb("den", [P, HEADS])
        self.rden = sb("rden", [P, HEADS])
        self.pt = sb("pt", [P, PAIRS, P])
        self.v = sb("v", [P, 2, v_cols])
        self.oh = sb("oh", [P, 2, PAIRS, P], F16)
        self.ol = sb("ol", [P, 2, PAIRS, P], F16)
        self.sc_ready = sem("sc_ready")
        self.sc_left = sem("sc_left")
        self.mx_ready = sem("mx_ready")
        self.s_ready = sem("s_ready")
        self.e_ready = sem("e_ready")
        self.den_ready = sem("den_ready")
        self.p_ready = sem("p_ready")
        self.ptr_ready = sem("ptr_ready")
        self.pt_ready = sem("pt_ready")
        self.v_ready, self.v_count = None, 1
        self.pv_ready = sem("pv_ready")
        self.oh_ready = sem("oh_ready")
        self.ol_ready = sem("ol_ready")
        self.y_ready = sem("y_ready")
        self.y_added = sem("y_added")
        self.x_done = sem("x_done")
        self.sc = ps[:, 4:6, :].rearrange("p k (h s) -> p (k h) s", s=SEQ)
        self.ptp = ps[:, 4:6, :].rearrange("p k (h s) -> p (k h) s", s=P)
        self.ob = ps[:, 6:8, :].rearrange("p b (h s) -> p b h s", s=SEQ)
        self.o = self.ob.rearrange("p b h s -> p h b s")
        self.y = ps[:, 4, 0:DM]

    def take_max(self, dve):
        dve.reduce_max(self.mx[:, :], self.s[:, :, :], AX).then_inc(self.mx_ready, 1)

    def subtract_max(self, pool, t):
        pool.wait_ge(self.mx_ready, t + 1)
        pool.tensor_tensor(self.s[:, :, :], self.s[:, :, :], spread(self.mx[:, :], SEQ),
                           ALU.subtract).then_inc(self.s_ready, 1)

    def exponential(self, act, t, scales=(1.0,)):
        act.wait_ge(self.s_ready, t + 1)
        wait_used(act, self.ptr_ready, t, 1)
        n = len(scales)
        for i, scale in enumerate(scales):
            last = act.activation(self.e[:, i:HEADS:n, :], self.s[:, i:HEADS:n, :], ACT.Exp, scale=scale)
        last.then_inc(self.e_ready, 1)

    def denominator(self, dve, ch, t):
        dve.wait_ge(self.e_ready, t + 1)
        ch.link(dve.reduce_sum(self.den[:, :], self.e[:, :, :], AX))
        wait_used(dve, self.p_ready, t, 1)
        dve.reciprocal(self.rden[:, :], self.den[:, :]).then_inc(self.den_ready, 1)

    def normalise(self, pool, t):
        pool.wait_ge(self.den_ready, t + 1)
        pool.tensor_tensor(self.e[:, :, :], self.e[:, :, :], spread(self.rden[:, :], SEQ),
                           ALU.mult).then_inc(self.p_ready, 1)

    def transpose(self, pe, t, left):
        pe.wait_ge(self.p_ready, t + 1)
        wait_used(pe, left, t, 1)
        ev = self.e[:, :, :].rearrange("p (k b) s -> p k (b s)", b=2)
        for k in range(PAIRS):
            last = pe.transpose(self.ptp[:, k, :], ev[:, k], self.m.ident[:, :])
        last.then_inc(self.ptr_ready, 1)

    def copy_transposed(self, act, t):
        act.wait_ge(self.ptr_ready, t + 1)
        wait_used(act, self.pv_ready, t, 1, 2)
        act.copy(self.pt[:, :, :], self.ptp).then_inc(self.pt_ready, 1)

    def values(self, pe, t, p, r):
        if r == 0:
            pe.wait_ge(self.pt_ready, t + 1)
            pe.wait_ge(self.v_ready, self.v_count * (t + 1))
            wait_used(pe, self.ol_ready, t, 1, 2)
        else:
            pe.wait_ge(self.ol_ready, 2 * t + 1)
        for b in range(2):
            rows = slice(b * SEQ, (b + 1) * SEQ)
            if self.v_cols < HEADS * HD:
                for j in range(2):
                    g = 2 * r + j
                    last = pe.matmul(self.ob[:, b, 4 * j:4 * j + 4, :], self.v[rows, p, g * HD:(g + 1) * HD],
                                     self.pt[rows, 2 * g:2 * g + 2, :].rearrange("p k (h s) -> p (k h) s", s=SEQ),
                                     start=True, stop=True)
            else:
                for j in range(8):
                    h = 8 * r + j
                    last = pe.matmul(self.ob[:, b, j, :], self.v[rows, p, h * HD:(h + 1) * HD],
                                     self.pt[rows, h // 2, (h % 2) * SEQ:(h % 2 + 1) * SEQ], start=True, stop=True)
        last.then_inc(self.pv_ready, 1)

    def high(self, act, t, r):
        act.wait_ge(self.pv_ready, 2 * t + 1 + r)
        wait_used(act, self.y_ready, t, 1)
        act.copy(self.oh[:, r].rearrange("p h (b s) -> p h b s", b=2), self.o).then_inc(self.oh_ready, 1)

    def low(self, dve, t, r):
        dve.wait_ge(self.oh_ready, 2 * t + 1 + r)
        split = lambda a: a[:, r].rearrange("p h (b s) -> p h b s", b=2)
        dve.tensor_tensor(split(self.ol), self.o, split(self.oh), ALU.subtract).then_inc(self.ol_ready, 1)

    def project(self, pe, t, r, last_tile=False):
        pe.wait_ge(self.ol_ready, 2 * t + 1 + r)
        if r == 0 and not last_tile:
            pe.wait_ge(self.sc_left, t + 2)
        for j in range(8):
            h = 8 * r + j
            last = mm3(pe, self.y, (self.oh[:, r, j], self.ol[:, r, j]),
                       (self.w_out[0][:, h * DM:(h + 1) * DM], self.w_out[1][:, h * DM:(h + 1) * DM]), h == 0, h == 15)
        if r:
            last.then_inc(self.y_ready, 1)

    def add(self, dve, t, bias=None):
        dve.wait_ge(self.y_ready, t + 1)
        x = self.m.x_all[:, at(t), :]
        upd = dve.scalar_tensor_tensor(x, self.y, 1.0 / WS, x, ALU.mult, ALU.add)
        if bias is not None:
            upd.then_inc(self.y_added, 1)
            dve.wait_ge(self.y_added, t + 1)
            upd = dve.tensor_tensor(x, x, bias, ALU.add)
        upd.then_inc(self.x_done, 1)


def attention_gqa(m):
    nc, d = m.nc, m.d
    with ExitStack() as ctx:
        sb = lambda n, s, t=F32: ctx.enter_context(nc.sbuf_tensor("a0_" + n, s, t))
        sem = ctx.enter_context(Semaphores(nc, "a0_"))
        ps = ctx.enter_context(nc.psum_tensor("a0_ps", [P, 8, 512], F32))
        NQ, NK = HEADS * HD, KV * HD
        wq, wk, wv = [[sb(f"{n}{i}", [P, KC, c], F16) for i in range(2)]
                      for n, c in (("wq", NQ), ("wk", NK), ("wv", NK))]
        wo = [sb(f"wo{i}", [P, HEADS * DM], F16) for i in range(2)]
        flat = lambda w: w[:, :, :].rearrange("p c n -> p (c n)")
        split_weights(m, [(d["a0_q"], flat(wq[0]), flat(wq[1]), 1), (d["a0_k"], flat(wk[0]), flat(wk[1]), 1),
                          (d["a0_v"], flat(wv[0]), flat(wv[1]), 0),
                          (d["a0_o"], wo[0][:, :], wo[1][:, :], 0)], "a0")
        ln = LayerNorm(m, ctx, sem, "a0", ps[:, 0, :])
        at_ = Attend(m, ctx, sem, "a0", ps, wo, NK)
        rope = sb("rope", [P, 2, SEQ])
        gb = sb("gb", [P, 2, 4])
        tab = sb("tab", [P, 7, SEQ])
        QC, QW, BQ, KC_, KW, BK, TMP = range(7)
        bq2 = sb("bq2", [P, 2, SEQ])
        mask = sb("mask", [P, SEQ])
        u = sb("u", [P, 2, HEADS, SEQ])
        w = sb("w", [P, 2, HEADS, SEQ])
        qsw = sb("qsw", [P, 2, HEADS, SEQ])
        sq = sb("sq", [P, 2, HEADS, SEQ])
        sqh = sb("sqh", [P, 2, HEADS, SEQ], BF16)
        sql = sb("sql", [P, 2, HEADS, SEQ], BF16)
        st = sb("st", [P, HEADS, SEQ])
        sqk = sb("sqk", [P, NK])
        kt = sb("kt", [P, NK])
        ksw = sb("ksw", [P, NK])
        tmp = sb("tmp", [P, NK])
        vk = sb("vk", [P, KV])
        rk = sb("rk", [P, KV])
        rkd = sb("rkd", [P, KV, P])
        vq = sb("vq", [P, HEADS])
        rq = sb("rq", [P, HEADS])
        s2m = sb("s2m", [P, 2 * KV, SEQ])
        const_in, tab_set = sem("const_in"), sem("tab_set")
        chain, pool_chain = sem("chain"), sem("pool_chain")
        k_ready, vp_ready, q_ready, ksum_ready = (sem(n) for n in ("k_ready", "vp_ready", "q_ready", "ksum_ready"))
        ksw_ready, qsw_ready, u_ready, w_ready = (sem(n) for n in ("ksw_ready", "qsw_ready", "u_ready", "w_ready"))
        sqh_ready, sql_ready, stp_ready, st_ready = sem("sqh_ready"), sem("sql_ready"), sem("stp_ready"), sem("st_ready")
        sqk_ready, sq_ready, uw_ready = sem("sqk_ready"), sem("sq_ready"), sem("uw_ready")
        kraw_ready, vk_ready, rkd_ready, rkb_ready, kt_ready = (sem(n) for n in ("kraw_ready", "vk_ready", "rkd_ready", "rkb_ready", "kt_ready"))
        s2_ready, var_ready, vq_ready, rq_ready = sem("s2_ready"), sem("var_ready"), sem("vq_ready"), sem("rq_ready")
        at_.v_ready = sem("v_ready")
        further = lambda t: not (isinstance(t, int) and t + 2 >= TILES)
        QBANK = (2, 1, 0, 3)
        s2_ps = ps[:, 6, :]
        sct = at_.sc
        var_ps = ps[:, 7, 0:HEADS]
        heads_of = lambda a: a.rearrange("p (h b s) -> p h b s", h=4, b=2)
        pair_of = lambda a, k, b: a[:, b, 2 * k:2 * k + 2, :].rearrange("p h s -> p (h s)")
        by_head = lambda a, g: a[:, :, 4 * g:4 * g + 4, :].rearrange("p b h s -> p h b s")
        table = lambda i: tab[:, i, :].rearrange("p (h b s) -> p h b s", h=1, b=1).to_broadcast([P, 4, 2, SEQ])
        swapped = ((slice(0, HD // 2), slice(HD // 2, HD)), (slice(HD // 2, HD), slice(0, HD // 2)))
        seqs = lambda a: a.rearrange("p (r s) -> p r s", s=SEQ)
        block = ctx.enter_context(nc.Block())

        @block.sync
        def _(sp):
            sp.dma_start(rope[:, :, :], d["rope"]).then_inc(const_in, 16)
            sp.dma_start(gb[:, :], d["a0_gb"]).then_inc(const_in, 16)
            sp.dma_start(mask[:, :], d["causal"]).then_inc(const_in, 16)
            sp.wait_ge(const_in, 48)

        @block.gpsimd
        def _(pool):
            def key_rstd(t):
                pool.wait_ge(vk_ready, t + 1)
                pool.tensor_tensor(rk[:, :], vk[:, :], m.mhalf[:, 0:KV], ALU.pow).then_inc(pool_chain, 1)
                pool.wait_ge(pool_chain, t + 1)
                wait_used(pool, rkb_ready, t, 1)
                pool.tensor_tensor(rkd[:, :, :], repeat(m.ident[:, :], KV), spread(rk[:, :], P), ALU.mult).then_inc(rkd_ready, 1)

            def swapped_part(t, g):
                pool.wait_ge(qsw_ready, 4 * t + g + 1)
                wait_used(pool, uw_ready, t, 1, 4, g + 1)
                pool.tensor_tensor(by_head(w, g), by_head(qsw, g), table(QW), ALU.mult).then_inc(w_ready, 1)

            def squares_low(t, g):
                pool.wait_ge(sqh_ready, 4 * t + g + 1)
                wait_used(pool, var_ready, t, 1)
                pool.tensor_tensor(by_head(sql, g), by_head(sq, g), by_head(sqh, g), ALU.subtract).then_inc(sql_ready, 1)

            def head():
                ln.pool(pool)
                ln.pool_step(pool, 1, 1)
                key_rstd(0)
                pool.wait_ge(tab_set, 1)
                for g in range(4):
                    swapped_part(0, g)
                    squares_low(0, g)

            def step(t, p, has_next):
                pool.wait_ge(vq_ready, t + 1)
                pool.tensor_tensor(rq[:, :], vq[:, :], m.mhalf[:, 0:HEADS], ALU.pow).then_inc(rq_ready, 1)
                if has_next:
                    key_rstd(t + 1)
                    swapped_part(t + 1, 0)
                    squares_low(t + 1, 0)
                at_.subtract_max(pool, t)
                if has_next:
                    swapped_part(t + 1, 1)
                    squares_low(t + 1, 1)
                at_.normalise(pool, t)
                if further(t):
                    ln.pool_step(pool, t + 2, p)
                if has_next:
                    for g in (2, 3):
                        swapped_part(t + 1, g)
                        squares_low(t + 1, g)
            over_tiles(pool, head, step)

        @block.scalar
        def _(act):
            def square_keys(t):
                act.wait_ge(k_ready, t + 1)
                wait_used(act, ksum_ready, t, 1)
                act.activation(sqk[:, :], ps[:, 1, :], ACT.Square).then_inc(sqk_ready, 1)
                wait_used(act, kraw_ready, t, 1)
                for to, of in swapped:
                    last = act.copy(ksw[to, :], ps[of, 1, :])
                last.then_inc(ksw_ready, 1)

            def value(t, p):
                act.wait_ge(vp_ready, t + 1)
                wait_used(act, at_.pv_ready, t, 2, 2)
                act.activation(at_.v[:, p, :], ps[:, 3, :], ACT.Copy, scale=1.0 / WS).then_inc(at_.v_ready, 1)

            def square(t, g):
                act.wait_ge(q_ready, 4 * t + g + 1)
                wait_used(act, var_ready, t, 1)
                wait_used(act, sql_ready, t, 1, 4, g + 1)
                act.activation(by_head(sq, g), heads_of(ps[:, QBANK[g], :]), ACT.Square).then_inc(sq_ready, 1)
                act.activation(by_head(sqh, g), heads_of(ps[:, QBANK[g], :]), ACT.Square).then_inc(sqh_ready, 1)
                wait_used(act, w_ready, t, 1, 4, g + 1)
                for to, of in swapped:
                    last = act.copy(by_head(qsw[to], g), heads_of(ps[of, QBANK[g], :]))
                last.then_inc(qsw_ready, 1)

            def scores_out(t):
                act.wait_ge(stp_ready, t + 1)
                wait_used(act, at_.sc_ready, t, 1)
                act.copy(st[:, :, :], sct).then_inc(st_ready, 1)

            def head():
                ln.high(act, 0, 0, q_ready, 4)
                square_keys(0)
                value(0, 0)
                for g in range(4):
                    square(0, g)

            def step(t, p, has_next):
                before = not (isinstance(t, int) and t == 0)
                if before:
                    at_.copy_transposed(act, t - 1)
                if has_next:
                    ln.high(act, t + 1, 1 - p, q_ready, 4)
                scores_out(t)
                if has_next:
                    square_keys(t + 1)
                    square(t + 1, 0)
                if before:
                    at_.high(act, t - 1, 0)
                if has_next:
                    square(t + 1, 1)
                at_.exponential(act, t)
                if has_next:
                    value(t + 1, 1 - p)
                if before:
                    at_.high(act, t - 1, 1)
                if has_next:
                    square(t + 1, 2)
                    square(t + 1, 3)
            over_tiles(act, head, step)
            at_.copy_transposed(act, TILES - 1)
            at_.high(act, TILES - 1, 0)
            at_.high(act, TILES - 1, 1)

        @block.vector
        def _(dve):
            ch = Chain(dve, chain, 12, 6, 1)

            def tables():
                ts = lambda o, a, s: ch.link(dve.tensor_scalar(tab[:, o, :], a, s, None, ALU.mult))
                cos, sgn = rope[:, 0, :], rope[:, 1, :]
                dve.wait_ge(const_in, 48)
                for i, (c, swap, b) in enumerate(((QC, QW, BQ), (KC_, KW, BK))):
                    ts(c, cos, gb[:, i, 0:1])
                    ts(swap, sgn, gb[:, i, 3:4])
                    ts(TMP, sgn, gb[:, i, 2:3])
                    ch.link(dve.scalar_tensor_tensor(tab[:, b, :], cos, gb[:, i, 1:2], tab[:, TMP, :], ALU.mult, ALU.add))
                dve.tensor_copy(bq2[:, :, :], repeat(tab[:, BQ, :], 2)).then_inc(tab_set, 1)

            def keys_raw(t):
                dve.wait_ge(ksw_ready, t + 1)
                bc = lambda i: repeat(tab[:, i, :], NK // SEQ)
                wait_used(dve, stp_ready, t, 1)
                dve.tensor_tensor(seqs(kt[:, :]), seqs(ps[:, 1, :]), bc(KC_), ALU.mult)
                dve.tensor_tensor(seqs(tmp[:, :]), seqs(ksw[:, :]), bc(KW), ALU.mult).then_inc(kraw_ready, 1)
                dve.wait_ge(ksum_ready, t + 1)
                dve.tensor_scalar(vk[:, :], ps[:, 0, 0:KV], 1.0 / HD, LN_EPS * WS * WS, ALU.mult, ALU.add).then_inc(vk_ready, 1)
                dve.wait_ge(kraw_ready, t + 1)
                ch.link(dve.tensor_tensor(kt[:, :], kt[:, :], tmp[:, :], ALU.add))

            def keys_scaled(t):
                dve.wait_ge(rkb_ready, t + 1)
                ch.link(dve.tensor_tensor(kt[:, :], kt[:, :], ps[:, 0, :], ALU.mult))
                dve.tensor_tensor(seqs(kt[:, :]), seqs(kt[:, :]), repeat(tab[:, BK, :], NK // SEQ), ALU.add).then_inc(kt_ready, 1)

            def rotate_query(t, g):
                dve.wait_ge(qsw_ready, 4 * t + g + 1)
                wait_used(dve, stp_ready, t, 1)
                dve.tensor_tensor(by_head(u, g), heads_of(ps[:, QBANK[g], :]), table(QC), ALU.mult).then_inc(u_ready, 1)

            def add_swapped(t, g):
                dve.wait_ge(u_ready, 4 * t + g + 1)
                dve.wait_ge(w_ready, 4 * t + g + 1)
                dve.tensor_tensor(by_head(u, g), by_head(u, g), by_head(w, g), ALU.add).then_inc(uw_ready, 1)

            def head():
                tables()
                ln.stats(dve, ch, 0, 0)
                ln.normalise(dve, 0, 0)
                ln.stats(dve, ch, 1, 1)
                ln.normalise(dve, 1, 1)
                ln.low(dve, 0, 0)
                keys_raw(0)
                rotate_query(0, 0)
                rotate_query(0, 1)
                keys_scaled(0)
                rotate_query(0, 2)
                rotate_query(0, 3)
                for g in range(4):
                    add_swapped(0, g)

            def step(t, p, has_next):
                ch.tile(t)
                before = not (isinstance(t, int) and t == 0)
                if has_next:
                    ln.low(dve, t + 1, 1 - p)
                dve.wait_ge(s2_ready, t + 1)
                ch.link(dve.scalar_tensor_tensor(s2m[:, :, :], seqs(s2_ps), HD ** -0.5, repeat(mask[:, :], 2 * KV), ALU.mult, ALU.add))
                dve.wait_ge(var_ready, t + 1)
                dve.tensor_scalar(vq[:, :], var_ps, 1.0, HD * LN_EPS * WS * WS, ALU.mult, ALU.add).then_inc(vq_ready, 1)
                if has_next:
                    keys_raw(t + 1)
                dve.wait_ge(at_.sc_ready, t + 1)
                dve.wait_ge(rq_ready, t + 1)
                wait_used(dve, at_.e_ready, t, 1)
                dve.tensor_tensor(at_.s[:, :, :], at_.sc, spread(rq[:, :], SEQ), ALU.mult).then_inc(at_.sc_left, 1)
                dve.wait_ge(at_.sc_left, t + 1)
                s4 = at_.s[:, :, :].rearrange("p (g r b) s -> p g r (b s)", r=2, b=2)
                s2b = s2m[:, :, :].rearrange("p (g o b) s -> p g o (b s)", o=1, b=2).to_broadcast([P, KV, 2, P])
                ch.link(dve.tensor_tensor(s4, s4, s2b, ALU.add))
                if before:
                    at_.low(dve, t - 1, 0)
                at_.take_max(dve)
                if has_next:
                    rotate_query(t + 1, 0)
                    keys_scaled(t + 1)
                    rotate_query(t + 1, 1)
                    add_swapped(t + 1, 0)
                at_.denominator(dve, ch, t)
                if before:
                    at_.low(dve, t - 1, 1)
                if further(t):
                    ln.stats(dve, ch, t + 2, p)
                if has_next:
                    rotate_query(t + 1, 2)
                    add_swapped(t + 1, 1)
                if further(t):
                    ln.normalise(dve, t + 2, p)
                if has_next:
                    rotate_query(t + 1, 3)
                if before:
                    at_.add(dve, t - 1)
                if has_next:
                    add_swapped(t + 1, 2)
                    add_swapped(t + 1, 3)
            over_tiles(dve, head, step)
            at_.low(dve, TILES - 1, 0)
            at_.low(dve, TILES - 1, 1)
            at_.add(dve, TILES - 1)

        @block.tensor
        def _(pe):
            def keys(t, p):
                pe.wait_ge(ln.xl_ready, t + 1)
                wait_used(pe, u_ready, t, 1, 4, 2)
                for h in range(KV):
                    for c in range(KC):
                        cols = slice(h * HD, (h + 1) * HD)
                        last = mm3(pe, ps[:, 1, cols], (wk[0][:, c, cols], wk[1][:, c, cols]),
                                   ln.operand(p, c), c == 0, c == KC - 1)
                last.then_inc(k_ready, 1)

            def value(t, p):
                wait_used(pe, u_ready, t, 1, 4, 4)
                for c in range(KC):
                    last = mm3(pe, ps[:, 3, :], ln.operand(p, c), (wv[0][:, c, :], wv[1][:, c, :]), c == 0, c == KC - 1)
                last.then_inc(vp_ready, 1)

            def key_sums(t):
                pe.wait_ge(sqk_ready, t + 1)
                for h in range(KV):
                    last = pe.matmul(ps[:, 0, h:h + 1], sqk[:, h * P:(h + 1) * P], m.ones[:, 0:1], start=True, stop=True)
                last.then_inc(ksum_ready, 1)

            def key_factors(t):
                pe.wait_ge(rkd_ready, t + 1)
                pe.matmul(ps[:, 0, :], m.ones[:, :], rkd[:, :, :].rearrange("p h s -> p (h s)"),
                          start=True, stop=True).then_inc(rkb_ready, 1)

            def queries(t, p, g):
                if g == 0:
                    wait_used(pe, u_ready, t, 1, 4, 1)
                elif g == 1:
                    pe.wait_ge(kraw_ready, t + 1)
                elif g == 2:
                    pe.wait_ge(kt_ready, t + 1)
                else:
                    pe.wait_ge(at_.v_ready, t + 1)
                for h in range(4):
                    for c in range(KC):
                        cols = slice((4 * g + h) * HD, (4 * g + h + 1) * HD)
                        last = mm3(pe, ps[:, QBANK[g], h * P:(h + 1) * P], (wq[0][:, c, cols], wq[1][:, c, cols]),
                                   ln.operand(p, c), c == 0, c == KC - 1)
                last.then_inc(q_ready, 1)

            def bias_scores(t):
                pe.wait_ge(kt_ready, t + 1)
                wait_used(pe, at_.ol_ready, t, 2, 2)
                pe.matmul(s2_ps, bq2[:, :, :].rearrange("p a s -> p (a s)"), kt[:, :], start=True, stop=True).then_inc(s2_ready, 1)

            def query_sums(t):
                pe.wait_ge(sql_ready, 4 * (t + 1))
                for b in range(2):
                    for k in range(PAIRS):
                        out = var_ps[:, 2 * k + b:2 * k + b + 1]
                        pe.matmul(out, pair_of(sqh, k, b), m.onesb[:, :], start=True, stop=False)
                        last = pe.matmul(out, pair_of(sql, k, b), m.onesb[:, :], start=False, stop=True)
                last.then_inc(var_ready, 1)

            def scores(t):
                pe.wait_ge(uw_ready, 4 * (t + 1))
                if not (isinstance(t, int) and t == 0):
                    pe.wait_ge(at_.pt_ready, t)
                for g in range(KV):
                    for b in range(2):
                        keys_ = slice(g * HD + b * SEQ, g * HD + (b + 1) * SEQ)
                        last = pe.matmul(sct[b * SEQ:(b + 1) * SEQ, 4 * g:4 * g + 4, :], kt[:, keys_],
                                         u[:, b, 4 * g:4 * g + 4, :], start=True, stop=True)
                last.then_inc(stp_ready, 1)

            def turn_scores(t):
                pe.wait_ge(st_ready, t + 1)
                for k in range(PAIRS):
                    last = pe.transpose(at_.ptp[:, k, :], st[:, 2 * k:2 * k + 2, :].rearrange("p h s -> p (h s)"), m.ident[:, :])
                last.then_inc(at_.sc_ready, 1)

            def head():
                ln.transpose(pe, 0, 0)
                keys(0, 0)
                value(0, 0)
                key_sums(0)
                queries(0, 0, 0)
                queries(0, 0, 1)
                key_factors(0)
                queries(0, 0, 2)
                queries(0, 0, 3)

            def step(t, p, has_next):
                before = not (isinstance(t, int) and t == 0)
                if before:
                    at_.transpose(pe, t - 1, at_.x_done)
                if has_next:
                    pe.wait_ge(u_ready, 4 * t + 3)
                    ln.transpose(pe, t + 1, 1 - p)
                bias_scores(t)
                scores(t)
                query_sums(t)
                if has_next:
                    keys(t + 1, 1 - p)
                    value(t + 1, 1 - p)
                    key_sums(t + 1)
                    queries(t + 1, 1 - p, 0)
                turn_scores(t)
                if before:
                    pe.wait_ge(vq_ready, t + 1)
                    at_.values(pe, t - 1, 1 - p, 0)
                if has_next:
                    queries(t + 1, 1 - p, 1)
                    key_factors(t + 1)
                if before:
                    at_.project(pe, t - 1, 0)
                    at_.values(pe, t - 1, 1 - p, 1)
                if has_next:
                    queries(t + 1, 1 - p, 2)
                    queries(t + 1, 1 - p, 3)
                if before:
                    at_.project(pe, t - 1, 1)
            over_tiles(pe, head, step)
            t, p = TILES - 1, 1
            at_.transpose(pe, t, at_.x_done)
            for r in range(2):
                at_.values(pe, t, p, r)
                at_.project(pe, t, r, True)
EXPERTS, RANK, LORA_SCALE = 8, 16, 2.0


def ffn_lora(m):
    nc, d = m.nc, m.d
    H1 = EXPERTS * RANK
    with ExitStack() as ctx:
        sb = lambda n, s, t=F32: ctx.enter_context(nc.sbuf_tensor("f0_" + n, s, t))
        sem = ctx.enter_context(Semaphores(nc, "f0_"))
        ps = ctx.enter_context(nc.psum_tensor("f0_ps", [P, 8, 512], F32))
        wb = [sb(f"wb{i}", [P, KC, DM], F16) for i in range(2)]
        wa = [sb(f"wa{i}", [P, KC, H1 + EXPERTS], F16) for i in range(2)]
        wB = [sb(f"wB{i}", [P, DM], F16) for i in range(2)]
        flat = lambda w: w[:, :, :].rearrange("p c n -> p (c n)")
        split_weights(m, [(d["ffn0_base"], flat(wb[0]), flat(wb[1]), 0), (d["ffn0_a"], flat(wa[0]), flat(wa[1]), 0),
                          (d["ffn0_b"], wB[0][:, :], wB[1][:, :], 0)], "f0")
        ln = LayerNorm(m, ctx, sem, "f0", ps[:, 0, :])
        desc = sb("desc", [P, EXPERTS])
        bias = sb("bias", [P, DM])
        top = sb("top", [P, 1])
        cand = sb("cand", [P, EXPERTS])
        first = sb("first", [P, 1])
        pick = sb("pick", [P, EXPERTS])
        hm = sb("hm", [P, 2, H1])
        hh = sb("hh", [P, 2, P], F16)
        hl = sb("hl", [P, 2, P], F16)
        y_ps = lambda p: ps[:, 1 + p, 0:DM]
        a_ps = lambda p: ps[:, 3 + p, 0:H1 + EXPERTS]
        ht_ps = lambda p: ps[:, 5 + p, 0:P]
        const_in, chain = sem("const_in"), sem("chain")
        a_ready, h_ready, ht_ready = sem("a_ready"), sem("h_ready"), sem("ht_ready")
        hh_ready, hl_ready, y_ready, x_done = sem("hh_ready"), sem("hl_ready"), sem("y_ready"), sem("x_done")
        y_added = sem("y_added")
        further = lambda t: not (isinstance(t, int) and t + 2 >= TILES)
        block = ctx.enter_context(nc.Block())

        @block.sync
        def _(sp):
            sp.dma_start(desc[:, :], d["desc"]).then_inc(const_in, 16)
            sp.dma_start(bias[:, :], d["ffn0_bias"].to_broadcast([P, DM])).then_inc(const_in, 16)
            sp.wait_ge(const_in, 32)

        @block.gpsimd
        def _(pool):
            def head():
                ln.pool(pool)
                ln.pool_step(pool, 1, 1)

            def step(t, p, has_next):
                if further(t):
                    ln.pool_step(pool, t + 2, p)
            over_tiles(pool, head, step)

        @block.scalar
        def _(act):
            def head():
                ln.high(act, 0, 0, y_ready)
                ln.high(act, 1, 1, y_ready)

            def step(t, p, has_next):
                act.wait_ge(ht_ready, t + 1)
                wait_used(act, y_ready, t, 2)
                act.copy(hh[:, p], ht_ps(p)).then_inc(hh_ready, 1)
                if further(t):
                    ln.high(act, t + 2, p, y_ready)
            over_tiles(act, head, step)

        @block.vector
        def _(dve):
            ch = Chain(dve, chain, 2, 5, 1)

            def route(t, p):
                dve.wait_ge(a_ready, t + 1)
                logits = a_ps(p)[:, H1:]
                ch.link(dve.reduce_max(top[:, :], logits, AX))
                ch.link(dve.scalar_tensor_tensor(cand[:, :], logits, top[:, :], desc[:, :], ALU.is_ge, ALU.mult))
                ch.link(dve.reduce_max(first[:, :], cand[:, :], AX))
                ch.link(dve.tensor_scalar(pick[:, :], cand[:, :], first[:, :], LORA_SCALE / WS, ALU.is_equal, ALU.mult))
                wait_used(dve, ht_ready, t, 2)
                dve.tensor_tensor(hm[:, p].rearrange("p (e r) -> p e r", r=RANK),
                                  a_ps(p)[:, 0:H1].rearrange("p (e r) -> p e r", r=RANK),
                                  spread(pick[:, :], RANK),
                                  ALU.mult).then_inc(h_ready, 1)

            def head():
                ln.stats(dve, ch, 0, 0)
                ln.normalise(dve, 0, 0)
                ln.stats(dve, ch, 1, 1)
                ln.normalise(dve, 1, 1)
                ln.low(dve, 0, 0)
                ln.low(dve, 1, 1)
                dve.wait_ge(const_in, 32)

            def step(t, p, has_next):
                ch.tile(t)
                if further(t):
                    ln.stats(dve, ch, t + 2, p)
                route(t, p)
                if further(t):
                    ln.normalise(dve, t + 2, p)
                dve.wait_ge(hh_ready, t + 1)
                dve.tensor_tensor(hl[:, p], ht_ps(p), hh[:, p], ALU.subtract).then_inc(hl_ready, 1)
                dve.wait_ge(y_ready, t + 1)
                x = m.x_all[:, at(t), :]
                dve.scalar_tensor_tensor(x, y_ps(p), 1.0 / WS, x, ALU.mult, ALU.add).then_inc(y_added, 1)
                dve.wait_ge(y_added, t + 1)
                dve.tensor_tensor(x, x, bias[:, :], ALU.add).then_inc(x_done, 1)
                if further(t):
                    ln.low(dve, t + 2, p)
            over_tiles(dve, head, step)

        @block.tensor
        def _(pe):
            def projections(t, p):
                pe.wait_ge(ln.xl_ready, t + 1)
                wait_used(pe, h_ready, t, 2)
                for c in range(KC):
                    last = mm3(pe, a_ps(p), ln.operand(p, c), (wa[0][:, c], wa[1][:, c]), c == 0, c == KC - 1)
                last.then_inc(a_ready, 1)
                wait_used(pe, x_done, t, 2)
                for c in range(KC):
                    mm3(pe, y_ps(p), ln.operand(p, c), (wb[0][:, c], wb[1][:, c]), c == 0, False)

            def head():
                ln.transpose(pe, 0, 0)
                ln.transpose(pe, 1, 1)
                projections(0, 0)

            def step(t, p, has_next):
                if has_next:
                    projections(t + 1, 1 - p)
                pe.wait_ge(h_ready, t + 1)
                wait_used(pe, hl_ready, t, 2)
                pe.transpose(ht_ps(p), hm[:, p], m.ident[:, :]).then_inc(ht_ready, 1)
                pe.wait_ge(hl_ready, t + 1)
                mm3(pe, y_ps(p), (hh[:, p], hl[:, p]), (wB[0][:, :], wB[1][:, :]), False, True).then_inc(y_ready, 1)
                if further(t):
                    ln.transpose(pe, t + 2, p)
            over_tiles(pe, head, step)

XH = 8
XT = SEQ // XH
XU = 2 * XH
XG = 4
VC = XT + 1


def attention_features(m):
    nc, d = m.nc, m.d
    with ExitStack() as ctx:
        sb = lambda n, s, t=F32: ctx.enter_context(nc.sbuf_tensor("x0_" + n, s, t))
        sem = ctx.enter_context(Semaphores(nc, "x0_"))
        ps = ctx.enter_context(nc.psum_tensor("x0_ps", [P, 8, 512], F32))
        ln = LayerNorm(m, ctx, sem, "x0", ps[:, 0, :])
        self_ = sb("sel_f", [P, 4, XG * P])
        sel = sb("sel", [P, 4, XG, P], F16)
        one_row = sb("one_row", [P, 1])
        nident = sb("nident", [P, P], F16)
        xh = sb("xh", [P, 2, DM], F16)
        xl = sb("xl", [P, 2, DM], F16)
        cf = sb("cf", [P, 2, DM])
        chi = sb("chi", [P, DM], F16)
        clo = sb("clo", [P, DM], F16)
        vt = sb("vt", [P, 2, KC, XU, VC])
        q = sb("q", [P, 2, XG, DM], F16)
        k = sb("k", [P, 2, XG, DM], F16)
        mx = sb("mx", [P, KC, XG, P], F16)
        e = sb("e", [P, 4, KC, DM])
        o = sb("o", [P, XG, DM])
        gather = sb("gather", [P, 2, 32])
        rec = sb("rec", [P, DM])
        res = sb("res", [P, DM])
        const_in, zeroed, sel_set = sem("const_in"), sem("zeroed"), sem("sel_set")
        c_in = [sem(f"c_in{i}") for i in range(2)]
        v_in = [sem(f"v_in{i}") for i in range(2)]
        chain, xs_ready, chi_ready, clo_ready = sem("chain"), sem("xs_ready"), sem("chi_ready"), sem("clo_ready")
        qsel, ksel, q1_ready, k_ready, s1_ready, mx_ready, nm_ready, q2_ready = (
            sem(n) for n in ("qsel", "ksel", "q1_ready", "k_ready", "s1_ready", "mx_ready", "nm_ready", "q2_ready"))
        s2_ready, e_ready, pv_ready, o_ready, fin_ready, x_done = (
            sem(n) for n in ("s2_ready", "e_ready", "pv_ready", "o_ready", "fin_ready", "x_done"))
        rec_ready, res_ready = sem("rec_ready"), sem("res_ready")
        q_ps = ps[:, 0:2, :].rearrange("p b (g n) -> p (b g) n", n=DM)
        k_ps = ps[:, 2, :].rearrange("p (g n) -> p g n", n=DM)
        fin_ps = ps[:, 2, :].rearrange("p (i n) -> p i n", n=DM)
        o_ps = ps[:, 3, :].rearrange("p (g n) -> p g n", n=DM)
        s1_ps = lambda u: ps[:, 4 + u % 2, :].rearrange("p (c n) -> p c n", n=DM)
        s2_ps = lambda u: ps[:, 6 + u % 2, :]
        further = lambda t: not (isinstance(t, int) and t + 2 >= TILES)
        block = ctx.enter_context(nc.Block())

        @block.sync
        def _(sp):
            sp.dma_start(self_[:, :, :], d["x0_sel"]).then_inc(const_in, 16)
            sp.dma_start(one_row[:, :], d["x0_one"]).then_inc(const_in, 16)
            sp.dma_start(gather[:, :, :], d["x0_gather"]).then_inc(const_in, 16)

            def load(t, p):
                wait_used(sp, clo_ready, t, 2)
                sp.dma_start(cf[:, p], dram_tile(d["ctx"], t)).then_inc(c_in[p], 16)
                wait_used(sp, pv_ready, t, 2, XU)
                sp.dma_start(vt[:, p].rearrange("p c u v -> p (c u v)"), dram_tile(d["ctx_v"], t)).then_inc(v_in[p], 16)

            def head():
                load(0, 0)
                load(1, 1)

            def step(t, p, has_next):
                if further(t):
                    load(t + 2, p)
            over_tiles(sp, head, step)
            for p in range(2):
                sp.wait_ge(v_in[p], 8 * TILES)

        @block.gpsimd
        def _(pool):
            def split_context(t, p):
                pool.wait_ge(c_in[p], (t - p) * 8 + 16)
                wait_used(pool, ksel, t, 1, 2)
                pool.tensor_tensor(chi[:, :], cf[:, p], m.ones2[:, :], ALU.mult).then_inc(chi_ready, 1)
                pool.wait_ge(chi_ready, t + 1)
                pool.tensor_tensor(clo[:, :], cf[:, p], chi[:, :], ALU.subtract).then_inc(clo_ready, 1)

            def head():
                ln.pool(pool)
                split_context(0, 0)
                ln.pool_step(pool, 1, 1)

            def step(t, p, has_next):
                if has_next:
                    split_context(t + 1, 1 - p)
                if further(t):
                    ln.pool_step(pool, t + 2, p)
            over_tiles(pool, head, step)

        @block.scalar
        def _(act):
            def queries(t, p):
                act.wait_ge(qsel, t + 1)
                wait_used(act, s2_ready, t, 2, XU)
                act.copy(q[:, p], q_ps).then_inc(q1_ready, 1)

            def context(t, p, r):
                act.wait_ge(ksel, 2 * t + r + 1)
                wait_used(act, s2_ready, t, 2, XU)
                act.activation(k[:, p, 2 * r:2 * r + 2], k_ps, ACT.Identity, bias=one_row[:, :]).then_inc(k_ready, 1)

            def shifted(t, p):
                act.wait_ge(nm_ready, t + 1)
                act.copy(q[:, p], q_ps).then_inc(q2_ready, 1)

            def head():
                act.wait_ge(const_in, 48)
                context(0, 0, 0)
                queries(0, 0)
                context(0, 0, 1)
                shifted(0, 0)

            def step(t, p, has_next):
                def values_out(r):
                    act.wait_ge(pv_ready, XU * t + 8 * (r + 1))
                    wait_used(act, fin_ready, t, 1)
                    act.copy(o[:, 2 * r:2 * r + 2], o_ps).then_inc(o_ready, 1)

                if has_next:
                    context(t + 1, 1 - p, 0)
                for u in range(XU):
                    act.wait_ge(s2_ready, XU * t + u + 1)
                    if isinstance(t, int) and t == 0:
                        if u >= 4:
                            act.wait_ge(pv_ready, u - 3)
                    else:
                        act.wait_ge(pv_ready, XU * t + u - 3)
                    act.activation(e[:, u % 4].rearrange("p c n -> p (c n)"), s2_ps(u), ACT.Exp,
                                   scale=XT ** -0.5).then_inc(e_ready, 1)
                    if u == 0 and has_next:
                        queries(t + 1, 1 - p)
                        context(t + 1, 1 - p, 1)
                    if u == 8:
                        values_out(0)
                values_out(1)
                if has_next:
                    shifted(t + 1, 1 - p)
            over_tiles(act, head, step)

        @block.vector
        def _(dve):
            ch = Chain(dve, chain, 4, 2, 2)

            def split_x(t, p):
                ln.stats(dve, ch, t, p)
                ln.normalise(dve, t, p)
                dve.wait_ge(ln.xn_ready, t + 1)
                wait_used(dve, qsel, t, 2)
                ch.link(dve.tensor_copy(xh[:, p], ln.xn[:, p]))
                dve.tensor_tensor(xl[:, p], ln.xn[:, p], xh[:, p], ALU.subtract).then_inc(xs_ready, 1)

            def maximum(t, u):
                dve.wait_ge(s1_ready, XU * t + u + 1)
                if u == 0:
                    wait_used(dve, nm_ready, t, 1)
                g, jj = divmod(u, 4)
                c = 32 * jj + 3 * XT
                dve.reduce_max(mx[:, :, g, c:c + 1].rearrange("p c o -> p (c o)"), s1_ps(u), AX).then_inc(mx_ready, 1)

            def finish(t, part):
                x = m.x_all[:, at(t), :]
                half = slice(part * P, (part + 1) * P)
                if part < 2:
                    dve.wait_ge(fin_ready, t + 1)
                    dve.reciprocal(rec[:, half], fin_ps[:, 1, half]).then_inc(rec_ready, 1)
                elif part == 2:
                    dve.wait_ge(rec_ready, 2 * (t + 1))
                    dve.tensor_tensor(res[:, :], fin_ps[:, 0], rec[:, :], ALU.mult).then_inc(res_ready, 1)
                else:
                    dve.wait_ge(res_ready, t + 1)
                    dve.tensor_tensor(x, x, res[:, :], ALU.add).then_inc(x_done, 1)

            def head():
                dve.memset(mx[:, :, :, :].rearrange("p a b c -> p (a b c)"), 0.0)
                dve.memset(ps[:, 3, :], 0.0).then_inc(zeroed, 1)
                dve.wait_ge(const_in, 48)
                dve.tensor_scalar(nident[:, :], m.ident[:, :], -1.0, None, ALU.mult)
                dve.tensor_copy(sel[:, :, :, :].rearrange("p a g c -> p a (g c)"), self_[:, :, :]).then_inc(sel_set, 1)
                split_x(0, 0)
                split_x(1, 1)
                dve.wait_ge(zeroed, 1)
                for u in range(XU):
                    maximum(0, u)

            def step(t, p, has_next):
                ch.tile(t)
                first = isinstance(t, int) and t == 0
                for u in range(XU):
                    if has_next:
                        maximum(t + 1, u)
                    if u in (3, 4, 5, 6) and not first:
                        finish(t - 1, u - 3)
                    if u == 10 and further(t):
                        split_x(t + 2, p)
            over_tiles(dve, head, step)
            for part in range(4):
                finish(TILES - 1, part)

        @block.tensor
        def _(pe):
            def select_q(t, p):
                pe.wait_ge(xs_ready, t + 1)
                wait_used(pe, q2_ready, t, 1)
                for g in range(XG):
                    pe.matmul(q_ps[:, g], sel[:, 0, g], xh[:, p], start=g % 2 == 0, stop=False, skip_group_check=True)
                    last = pe.matmul(q_ps[:, g], sel[:, 1, g], xl[:, p], start=False, stop=False, skip_group_check=True)
                last.then_inc(qsel, 1)

            def select_k(t, r):
                pe.wait_ge(clo_ready, t + 1)
                if r:
                    pe.wait_ge(k_ready, 2 * t + 1)
                else:
                    wait_used(pe, res_ready, t, 3)
                    wait_used(pe, k_ready, t, 1, 2)
                for i in range(2):
                    g = 2 * r + i
                    pe.matmul(k_ps[:, i], sel[:, 2, g], chi[:, :], start=True, stop=False)
                    last = pe.matmul(k_ps[:, i], sel[:, 3, g], clo[:, :], start=False, stop=True)
                last.then_inc(ksel, 1)

            def rows(u):
                g, jj = divmod(u, 4)
                return g, slice(32 * jj, 32 * jj + 32)

            def scores(t, p, u):
                g, r = rows(u)
                if u == 0:
                    pe.wait_ge(q1_ready, t + 1)
                if u % 8 == 0:
                    pe.wait_ge(k_ready, 2 * t + 1 + u // 8)
                if isinstance(t, int) and t == 0:
                    if u >= 2:
                        pe.wait_ge(mx_ready, u - 1)
                else:
                    pe.wait_ge(mx_ready, XU * t + u - 1)
                for c in range(KC):
                    last = pe.matmul(s1_ps(u)[:, c], q[r, p, g, c * P:(c + 1) * P], k[r, p, g], start=True, stop=True)
                last.then_inc(s1_ready, 1)

            def shifted_scores(t, p, u):
                g, r = rows(u)
                if u == 0:
                    pe.wait_ge(q2_ready, t + 1)
                if isinstance(t, int) and t == 0:
                    if u >= 2:
                        pe.wait_ge(e_ready, u - 1)
                else:
                    pe.wait_ge(e_ready, XU * t + u - 1)
                for c in range(KC):
                    last = pe.matmul(s2_ps(u)[:, c * DM:(c + 1) * DM], k[r, p, g, c * P:(c + 1) * P], q[r, p, g],
                                     start=True, stop=True)
                last.then_inc(s2_ready, 1)

            def values(t, p, u):
                pe.wait_ge(e_ready, XU * t + u + 1)
                if u == 0:
                    pe.wait_ge(v_in[p], (t - p) * 8 + 16)
                    wait_used(pe, o_ready, t, 1, 2)
                if u == XU // 2:
                    pe.wait_ge(o_ready, 2 * t + 1)
                g, jj = divmod(u, 4)
                for n in range(KC):
                    last = pe.matmul(o_ps[32 * jj:32 * jj + VC, g % 2, :], vt[:, p, n, u, :], e[:, u % 4, n, :],
                                     start=n == 0, stop=n == KC - 1)
                last.then_inc(pv_ready, 1)

            def add_maxima(t):
                pe.wait_ge(mx_ready, XU * (t + 1))
                pe.wait_ge(q1_ready, t + 1)
                for g in range(XG):
                    for c in range(KC):
                        last = pe.matmul(q_ps[:, g, c * P:(c + 1) * P], mx[:, c, g, :], nident[:, :],
                                         start=False, stop=True, skip_group_check=True)
                last.then_inc(nm_ready, 1)

            def head():
                pe.wait_ge(sel_set, 1)
                pe.wait_ge(zeroed, 1)
                select_k(0, 0)
                select_q(0, 0)
                select_k(0, 1)
                for u in range(XU):
                    scores(0, 0, u)
                add_maxima(0)

            def gather_output(t):
                pe.wait_ge(o_ready, 2 * (t + 1))
                wait_used(pe, res_ready, t, 1)
                for g in range(XG):
                    for i in range(2):
                        last = pe.matmul(fin_ps[32 * g:32 * g + 32, i, :], gather[:, i, :], o[:, g, :], start=True, stop=True)
                last.then_inc(fin_ready, 1)

            def step(t, p, has_next):
                if has_next:
                    select_k(t + 1, 0)
                shifted_scores(t, p, 0)
                shifted_scores(t, p, 1)
                if has_next:
                    select_q(t + 1, 1 - p)
                    select_k(t + 1, 1)
                for u in range(XU):
                    if has_next:
                        scores(t + 1, 1 - p, u)
                    if u == 1 and not (isinstance(t, int) and t == 0):
                        if has_next:
                            pe.wait_ge(k_ready, 2 * (t + 2))
                        gather_output(t - 1)
                    if u + 2 < XU:
                        shifted_scores(t, p, u + 2)
                    values(t, p, u)
                if has_next:
                    add_maxima(t + 1)
            over_tiles(pe, head, step)
            gather_output(TILES - 1)
RMS_EPS = 1e-6
BR = 64


def bias_rows(m, jobs, tag):
    nc = m.nc
    with ExitStack() as ctx:
        n_all = sum(src.shape[1] for src, _ in jobs)
        stage = ctx.enter_context(nc.sbuf_tensor(f"bstage{tag}", [1, n_all], F32))
        sem = ctx.enter_context(Semaphores(nc, tag))
        loaded, zeroed, high_done = sem("b_loaded"), sem("b_zeroed"), sem("b_high")
        starts = [sum(src.shape[1] for src, _ in jobs[:i]) for i in range(len(jobs))]
        block = ctx.enter_context(nc.Block())

        @block.sync
        def _(sp):
            for (src, rows), s in zip(jobs, starts):
                sp.dma_start(stage[0:1, s:s + src.shape[1]], src).then_inc(loaded, 16)
            sp.wait_ge(loaded, 16 * len(jobs))

        @block.scalar
        def _(act):
            act.wait_ge(loaded, 16 * len(jobs))
            act.wait_ge(zeroed, len(jobs))
            for (src, rows), s in zip(jobs, starts):
                act.activation(rows[0:1, :], stage[0:1, s:s + src.shape[1]], ACT.Copy, scale=WS).then_inc(high_done, 1)

        @block.vector
        def _(dve):
            for _, rows in jobs:
                dve.memset(rows, 0.0).then_inc(zeroed, 1)
            for i, ((src, rows), s) in enumerate(zip(jobs, starts)):
                dve.wait_ge(high_done, i + 1)
                dve.scalar_tensor_tensor(rows[32:33, :], stage[0:1, s:s + src.shape[1]], WS, rows[0:1, :],
                                         ALU.mult, ALU.subtract)


def attention_cross(m, x1_w):
    nc, d = m.nc, m.d
    NI = HEADS * HD
    with ExitStack() as ctx:
        sb = lambda n, s, t=F32: ctx.enter_context(nc.sbuf_tensor("x1_" + n, s, t))
        sem = ctx.enter_context(Semaphores(nc, "x1_"))
        ps = ctx.enter_context(nc.psum_tensor("x1_ps", [P, 8, 512], F32))
        parts = [x1_w[:, i].rearrange("p t n -> p (t n)") for i in range(2)]
        wq, wk, wv = [[a[:, j * KC * NI:(j + 1) * KC * NI].rearrange("p (c n) -> p c n", c=KC) for a in parts]
                      for j in range(3)]
        wo = [a[:, 3 * KC * NI:] for a in parts]
        bq, bk = (sb(n, [BR, NI], F16) for n in ("bq", "bk"))
        bias_rows(m, [(d["x1_bq"], bq[:, :]), (d["x1_bk"], bk[:, :])], "x1")
        ln = LayerNorm(m, ctx, sem, "x1", ps[:, 0, :])
        at_ = Attend(m, ctx, sem, "x1", ps, wo, NI)
        cf = sb("cf", [P, 2, KC, P])
        chi = sb("chi", [P, 2, KC, P], F16)
        clo = sb("clo", [P, 2, KC, P], F16)
        qs = sb("qs", [P, 2, HEADS])
        qk_scale = sb("qk_scale", [P, HEADS])
        bv = sb("bv", [P, HEADS])
        bo = sb("bo", [P, DM])
        q = sb("q", [P, HEADS, P])
        k = sb("k", [P, HEADS, P])
        sq = sb("sq", [P, 4, 512])
        sum4 = sb("sum4", [P, 512])
        sum2 = sb("sum2", [P, 2, P])
        sums = sb("sums", [P, 2, P])
        var = sb("var", [P, 3])
        rms = sb("rms", [P, 3])
        rkd = sb("rkd", [P, P])
        rkb = sb("rkb", [P, P])
        bvh_ready, bvl_ready, bvo_ready, bo_set = (sem(n) for n in ("bvh_ready", "bvl_ready", "bvo_ready", "bo_set"))
        const_in, scale_set, ctx_in = sem("const_in"), sem("scale_set"), [sem(f"ctx_in{i}") for i in range(2)]
        chain = sem("chain")
        chi_ready, clo_ready, proj_ready = sem("chi_ready"), sem("clo_ready"), sem("proj_ready")
        act_left, dve_left = sem("act_left"), sem("dve_left")
        sum4_ready, sum2_ready, sums_ready = sem("sum4_ready"), sem("sum2_ready"), sem("sums_ready")
        ss_ready, var_ready, rms_ready, rkd_ready = sem("ss_ready"), sem("var_ready"), sem("rms_ready"), sem("rkd_ready")
        rkp_ready, rkb_ready = sem("rkp_ready"), sem("rkb_ready")
        at_.v_ready, at_.v_count = act_left, 12
        bv_high, bv_low = (a[:, :, :, :].rearrange("p r h s -> p (r h) s") for a in (at_.oh, at_.ol))
        bank = lambda e: (e + 1) % 4
        further = lambda t: not (isinstance(t, int) and t + 2 >= TILES)
        block = ctx.enter_context(nc.Block())


        @block.sync
        def _(sp):
            sp.dma_start(qs[:, :, :], d["x1_scales"]).then_inc(const_in, 16)
            sp.dma_start(bo[:, :], d["x1_bo"].to_broadcast([P, DM])).then_inc(const_in, 16)
            sp.dma_start(bv[:, :], d["x1_bv"]).then_inc(const_in, 16)

            def load_context(t, p):
                wait_used(sp, clo_ready, t, 2)
                sp.dma_start(cf[:, p].rearrange("p c s -> p (c s)"), dram_tile(d["ctx_t"], t)).then_inc(ctx_in[p], 16)

            load_context(0, 0)
            load_context(1, 1)
            if TILES > 2:
                with sp.Fori(1, TILES // 2) as i:
                    load_context(2 * i, 0)
                    load_context(2 * i + 1, 1)
            for p in range(2):
                sp.wait_ge(ctx_in[p], 16 * (TILES // 2))
            sp.wait_ge(const_in, 48)

        @block.gpsimd
        def _(pool):
            def split_context(t, p):
                pool.wait_ge(ctx_in[p], (t - p) * 8 + 16)
                wait_used(pool, proj_ready, t, 2, 12)
                pool.tensor_tensor(chi[:, p], cf[:, p], repeat(m.ones[:, :], KC), ALU.mult).then_inc(chi_ready, 1)
                pool.wait_ge(chi_ready, t + 1)
                pool.tensor_tensor(clo[:, p], cf[:, p], chi[:, p], ALU.subtract).then_inc(clo_ready, 1)

            def sum_squares(t, i):
                for g in range(1, 4):
                    pool.wait_ge(act_left, 12 * t + 4 * i + g + 1)
                    if g > 1:
                        pool.wait_ge(sum4_ready, 3 * (2 * t + i) + g - 1)
                    pool.tensor_tensor(sum4[:, :], sq[:, 0, :] if g == 1 else sum4[:, :], sq[:, g, :],
                                       ALU.add).then_inc(sum4_ready, 1)
                pool.wait_ge(sum4_ready, 3 * (2 * t + i) + 3)
                halves = sum4[:, :].rearrange("p (a n) -> p a n", a=2)
                pool.tensor_tensor(sum2[:, :, :].rearrange("p a n -> p (a n)"), halves[:, 0], halves[:, 1], ALU.add).then_inc(sum2_ready, 1)
                pool.wait_ge(sum2_ready, 2 * t + i + 1)
                wait_used(pool, ss_ready, t, 1)
                pool.tensor_tensor(sums[:, i, :], sum2[:, 0, :], sum2[:, 1, :], ALU.add).then_inc(sums_ready, 1)

            def factors(t):
                pool.wait_ge(var_ready, t + 1)
                wait_used(pool, at_.e_ready, t, 1)
                pool.tensor_tensor(rms[:, :], var[:, :], m.mhalf[:, 0:3], ALU.pow).then_inc(rms_ready, 1)
                pool.wait_ge(rms_ready, t + 1)
                wait_used(pool, rkp_ready, t, 1)
                pool.tensor_tensor(rkd[:, :], m.ident[:, :], rms[:, 2:3].to_broadcast([P, P]), ALU.mult).then_inc(rkd_ready, 1)

            def front(t):
                sum_squares(t, 0)
                sum_squares(t, 1)
                factors(t)

            def head():
                ln.pool(pool)
                split_context(0, 0)
                ln.pool_step(pool, 1, 1)
                split_context(1, 1)
                front(0)

            def step(t, p, has_next):
                at_.subtract_max(pool, t)
                at_.normalise(pool, t)
                if further(t):
                    split_context(t + 2, p)
                if has_next:
                    sum_squares(t + 1, 0)
                if further(t):
                    ln.pool_step(pool, t + 2, p)
                if has_next:
                    sum_squares(t + 1, 1)
                    factors(t + 1)
            over_tiles(pool, head, step)

        @block.scalar
        def _(act):
            def square(t, e):
                act.wait_ge(proj_ready, 12 * t + e + 1)
                summed = max(e % 4, 1)
                if e >= 4:
                    act.wait_ge(sum4_ready, 6 * t + summed)
                else:
                    wait_used(act, sum4_ready, t, 1, 6, 3 + summed)
                act.activation(sq[:, e % 4, :], ps[:, bank(e), :], ACT.Square).then_inc(act_left, 1)

            def value(t, p, g):
                act.wait_ge(proj_ready, 12 * t + 8 + g + 1)
                wait_used(act, at_.pv_ready, t, 2, 2)
                act.activation(at_.v[:, p, g * 512:(g + 1) * 512], ps[:, bank(8 + g), :], ACT.Copy,
                               scale=1.0 / WS).then_inc(act_left, 1)

            def head():
                act.wait_ge(const_in, 48)
                act.copy(bv_high, spread(bv[:, :], P)).then_inc(bvh_ready, 1)
                ln.high(act, 0, 0, proj_ready, 12)
                for e in range(8):
                    square(0, e)
                for g in range(4):
                    value(0, 0, g)

            def step(t, p, has_next):
                before = not (isinstance(t, int) and t == 0)
                act.wait_ge(rkp_ready, t + 1)
                wait_used(act, at_.sc_left, t, 1)
                act.copy(rkb[:, :], ps[:, 1, 0:P]).then_inc(rkb_ready, 1)
                if before:
                    at_.copy_transposed(act, t - 1)
                if has_next:
                    ln.high(act, t + 1, 1 - p, proj_ready, 12)
                    square(t + 1, 0)
                    square(t + 1, 1)
                if before:
                    at_.high(act, t - 1, 0)
                act.wait_ge(rms_ready, t + 1)
                at_.exponential(act, t, (rms[:, 0:1], rms[:, 1:2]))
                if has_next:
                    square(t + 1, 2)
                if before:
                    at_.high(act, t - 1, 1)
                if has_next:
                    for e in range(3, 8):
                        square(t + 1, e)
                    for g in range(4):
                        value(t + 1, 1 - p, g)
            over_tiles(act, head, step)
            at_.copy_transposed(act, TILES - 1)
            at_.high(act, TILES - 1, 0)
            at_.high(act, TILES - 1, 1)

        @block.vector
        def _(dve):
            ch = Chain(dve, chain, 2, 2, 1)

            def leave(t, e):
                dve.wait_ge(act_left, 12 * t + e + 1)
                wait_used(dve, at_.sc_ready, t, 1)
                g = e % 4
                src = ps[:, bank(e), :].rearrange("p (h s) -> p h s", s=P)
                if e >= 4:
                    ins = dve.tensor_tensor(q[:, 4 * g:4 * g + 4, :], src, spread(qk_scale[:, 4 * g:4 * g + 4], P), ALU.mult)
                else:
                    ins = dve.tensor_copy(k[:, 4 * g:4 * g + 4, :], src)
                ins.then_inc(dve_left, 1)

            def variances(t):
                dve.wait_ge(ss_ready, t + 1)
                wait_used(dve, rms_ready, t, 1)
                dve.tensor_scalar(var[:, 2:3], ps[:, 1, 2:3], 1.0 / NI, RMS_EPS * WS * WS, ALU.mult, ALU.add)
                dve.tensor_scalar(var[:, 0:2], ps[:, 1, 0:2], HD / NI, HD * RMS_EPS * WS * WS,
                                  ALU.mult, ALU.add).then_inc(var_ready, 1)

            def head():
                dve.wait_ge(const_in, 48)
                dve.tensor_tensor(qk_scale[:, :], qs[:, 0, :], qs[:, 1, :], ALU.mult).then_inc(scale_set, 1)
                ln.stats(dve, ch, 0, 0)
                ln.normalise(dve, 0, 0)
                ln.stats(dve, ch, 1, 1)
                ln.normalise(dve, 1, 1)
                ln.low(dve, 0, 0)
                dve.wait_ge(bvh_ready, 1)
                dve.tensor_tensor(bv_low, spread(bv[:, :], P), bv_high, ALU.subtract).then_inc(bvl_ready, 1)
                dve.wait_ge(scale_set, 1)
                for e in range(8):
                    leave(0, e)
                dve.wait_ge(bvo_ready, 1)
                dve.scalar_tensor_tensor(bo[:, :], at_.y, 1.0 / WS, bo[:, :], ALU.mult, ALU.add).then_inc(bo_set, 1)
                variances(0)

            def step(t, p, has_next):
                ch.tile(t)
                before = not (isinstance(t, int) and t == 0)
                if has_next:
                    ln.low(dve, t + 1, 1 - p)
                dve.wait_ge(at_.sc_ready, t + 1)
                dve.wait_ge(rkb_ready, t + 1)
                wait_used(dve, at_.e_ready, t, 1)
                by_k = lambda a: a.rearrange("p (k b) s -> p k (b s)", b=2)
                dve.tensor_tensor(by_k(at_.s[:, :, :]), by_k(at_.sc), repeat(rkb[:, :], PAIRS), ALU.mult).then_inc(at_.sc_left, 1)
                dve.wait_ge(at_.sc_left, t + 1)
                at_.take_max(dve)
                if has_next:
                    leave(t + 1, 0)
                if before:
                    at_.low(dve, t - 1, 0)
                at_.denominator(dve, ch, t)
                if has_next:
                    leave(t + 1, 1)
                    leave(t + 1, 2)
                if before:
                    at_.low(dve, t - 1, 1)
                if has_next:
                    leave(t + 1, 3)
                    leave(t + 1, 4)
                if further(t):
                    ln.stats(dve, ch, t + 2, p)
                if has_next:
                    leave(t + 1, 5)
                if before:
                    at_.add(dve, t - 1, bo[:, :])
                if has_next:
                    leave(t + 1, 6)
                    leave(t + 1, 7)
                if further(t):
                    ln.normalise(dve, t + 2, p)
                if has_next:
                    variances(t + 1)
            over_tiles(dve, head, step)
            at_.low(dve, TILES - 1, 0)
            at_.low(dve, TILES - 1, 1)
            at_.add(dve, TILES - 1, bo[:, :])

        @block.tensor
        def _(pe):
            def project_heads(t, p, e, w, bias, operand):
                g = e % 4
                for h in range(4):
                    cols = slice((4 * g + h) * HD, (4 * g + h + 1) * HD)
                    out = ps[:, bank(e), h * P:(h + 1) * P]
                    for c in range(KC):
                        mm3(pe, out, (w[0][:, c, cols], w[1][:, c, cols]), operand(p, c), c == 0, False)
                    last = pe.matmul(out, bias[:, cols], m.onesh[0:BR, :], start=False, stop=True)
                last.then_inc(proj_ready, 1)

            def context(p, c):
                return chi[:, p, c, :], clo[:, p, c, :]

            def front(t, p, groups):
                for e in groups:
                    if e == 0:
                        pe.wait_ge(clo_ready, t + 1)
                        wait_used(pe, rkb_ready, t, 1)
                    if e == 3:
                        pe.wait_ge(ln.xl_ready, t + 1)
                    if e >= 4:
                        pe.wait_ge(dve_left, 8 * t + e - 3)
                    else:
                        wait_used(pe, act_left, t, 1, 12, 9 + e)
                    if e < 4:
                        project_heads(t, p, e, wk, bk, context)
                    elif e < 8:
                        project_heads(t, p, e, wq, bq, ln.operand)
                    else:
                        cols = slice((e - 8) * 512, (e - 7) * 512)
                        out = ps[:, bank(e), :]
                        for c in range(KC):
                            last = mm3(pe, out, context(p, c), (wv[0][:, c, cols], wv[1][:, c, cols]), c == 0, c == KC - 1)
                        last.then_inc(proj_ready, 1)

            def sums_of_squares(t):
                pe.wait_ge(sums_ready, 2 * (t + 1))
                pe.wait_ge(act_left, 12 * t + 9)
                for half in range(2):
                    for b in range(2):
                        pe.matmul(ps[half * SEQ:(half + 1) * SEQ, 1, b:b + 1], sums[:, 1, b * SEQ:(b + 1) * SEQ],
                                  m.ones[:, 0:1], start=True, stop=True)
                pe.matmul(ps[:, 1, 2:3], sums[:, 0, :], m.ones[:, 0:1], start=True, stop=True).then_inc(ss_ready, 1)

            def key_factors(t):
                pe.wait_ge(rkd_ready, t + 1)
                pe.matmul(ps[:, 1, 0:P], m.ones[:, :], rkd[:, :], start=True, stop=True).then_inc(rkp_ready, 1)

            def scores(t):
                pe.wait_ge(dve_left, 8 * (t + 1))
                if not (isinstance(t, int) and t == 0):
                    pe.wait_ge(at_.pt_ready, t)
                for h in range(HEADS):
                    for b in range(2):
                        tok = slice(b * SEQ, (b + 1) * SEQ)
                        rows = slice(h % 2 * SEQ, (h % 2 + 1) * SEQ)
                        last = pe.matmul(at_.sc[rows, h // 2 * 2 + b, :], q[:, h, tok], k[:, h, tok], start=True, stop=True)
                last.then_inc(at_.sc_ready, 1)

            def head():
                ln.transpose(pe, 0, 0)
                front(0, 0, range(12))
                pe.wait_ge(bvl_ready, 1)
                for h in range(HEADS):
                    last = mm3(pe, at_.y, (bv_high[:, h, :], bv_low[:, h, :]),
                               (wo[0][:, h * DM:(h + 1) * DM], wo[1][:, h * DM:(h + 1) * DM]), h == 0, h == HEADS - 1)
                last.then_inc(bvo_ready, 1)
                sums_of_squares(0)

            def step(t, p, has_next):
                before = not (isinstance(t, int) and t == 0)
                if before:
                    at_.transpose(pe, t - 1, at_.x_done)
                else:
                    pe.wait_ge(bo_set, 1)
                if has_next:
                    pe.wait_ge(act_left, 12 * (t + 1))
                    ln.transpose(pe, t + 1, 1 - p)
                key_factors(t)
                if has_next:
                    front(t + 1, 1 - p, range(1))
                scores(t)
                if has_next:
                    front(t + 1, 1 - p, range(1, 2))
                if before:
                    at_.values(pe, t - 1, 1 - p, 0)
                if has_next:
                    front(t + 1, 1 - p, range(2, 4))
                if before:
                    at_.project(pe, t - 1, 0)
                    at_.values(pe, t - 1, 1 - p, 1)
                if has_next:
                    front(t + 1, 1 - p, range(4, 6))
                if before:
                    at_.project(pe, t - 1, 1)
                if has_next:
                    front(t + 1, 1 - p, range(6, 11))
                    sums_of_squares(t + 1)
                    front(t + 1, 1 - p, range(11, 12))
            over_tiles(pe, head, step)
            t, p = TILES - 1, 1
            at_.transpose(pe, t, at_.x_done)
            for r in range(2):
                at_.values(pe, t, p, r)
                at_.project(pe, t, r, True)
AH, AD = 16, 16
AG = P // AD


def attention_mqa(m, x1_w):
    nc, d = m.nc, m.d
    with ExitStack() as ctx:
        sb = lambda n, s, t=F32: ctx.enter_context(nc.sbuf_tensor("a1_" + n, s, t))
        sem = ctx.enter_context(Semaphores(nc, "a1_"))
        ps = ctx.enter_context(nc.psum_tensor("a1_ps", [P, 8, 512], F32))
        wqk = [sb(f"wqk{i}", [P, KC, 3 * P], F16) for i in range(2)]
        wv = [sb(f"wv{i}", [P, KC, AD], F16) for i in range(2)]
        wo = [sb(f"wo{i}", [P, KC, DM], F16) for i in range(2)]
        flat = lambda w: w[:, :, :].rearrange("p c n -> p (c n)")
        split_weights(m, [(d["a1_qk"], flat(wqk[0]), flat(wqk[1]), 0), (d["a1_v"], flat(wv[0]), flat(wv[1]), 0),
                          (d["a1_o"], flat(wo[0]), flat(wo[1]), 0)], "a1")
        ln = LayerNorm(m, ctx, sem, "a1", ps[:, 0, :])
        qk_bias = sb("qk_bias", [P, 3])
        v_bias = sb("v_bias", [P, AD])
        o_bias = sb("o_bias", [P, DM])
        mask = sb("mask", [P, SEQ])
        maskb = sb("maskb", [P, SEQ], BF16)
        own = sb("own", [P, AG])
        qk = sb("qk", [P, 2, 3, P])
        kd = sb("kd", [P, AG, P])
        v = sb("v", [P, 2, AD])
        s = sb("s", [P, AH, SEQ])
        e = sb("e", [P, AH, SEQ])
        mx = sb("mx", [P, AH])
        den = sb("den", [P, AH])
        rden = sb("rden", [P, AH])
        pt = sb("pt", [P, AG, P])
        o_sb = sb("o_sb", [P, 2, P])
        oh = sb("oh", [P, 2, P], F16)
        ol = sb("ol", [P, 2, P], F16)
        stage = sb("stage", [P, 2, X1_PIECE])
        piece_in = [sem(f"piece_in{i}") for i in range(2)]
        whigh_ready, wlow_ready = sem("whigh_ready"), sem("wlow_ready")
        const_in, mask_set, chain = sem("const_in"), sem("mask_set"), sem("chain")
        proj_ready, qk_ready, kd_ready, v_ready = sem("proj_ready"), sem("qk_ready"), sem("kd_ready"), sem("v_ready")
        sc_ready, mx_ready, s_ready, e_ready, den_ready, rden_ready = (
            sem(n) for n in ("sc_ready", "mx_ready", "s_ready", "e_ready", "den_ready", "rden_ready"))
        ptr_ready, pt_ready, pv_ready, o_ready, ot_ready, oh_ready, ol_ready = (
            sem(n) for n in ("ptr_ready", "pt_ready", "pv_ready", "o_ready", "ot_ready", "oh_ready", "ol_ready"))
        y_ready, y_added, x_done = sem("y_ready"), sem("y_added"), sem("x_done")
        proj = ps[:, 1, :]
        ot_ps = ps[:, 2, 0:2 * P].rearrange("p (b n) -> p b n", b=2)
        y = ps[:, 3, 0:DM]
        sc = ps[:, 4:6, :].rearrange("p a (h s) -> p (a h) s", s=SEQ)
        ptp = ps[:, 4:6, :].rearrange("p a (h s) -> p (a h) s", s=P)
        o_ps = ps[:, 6:8, 0:P]
        started = lambda t, lag: not (isinstance(t, int) and t < lag)
        further = lambda t: not (isinstance(t, int) and t + 2 >= TILES)
        block = ctx.enter_context(nc.Block())

        @block.sync
        def _(sp):
            sp.dma_start(qk_bias[:, :], d["a1_bqk"]).then_inc(const_in, 16)
            sp.dma_start(v_bias[:, :], d["a1_bv"].to_broadcast([P, AD])).then_inc(const_in, 16)
            sp.dma_start(o_bias[:, :], d["a1_bo"].to_broadcast([P, DM])).then_inc(const_in, 16)
            sp.dma_start(mask[:, :], d["causal"]).then_inc(const_in, 16)
            sp.dma_start(own[:, :], d["a1_own"]).then_inc(const_in, 16)
            sp.wait_ge(const_in, 80)

            def load_piece(t, p):
                wait_used(sp, wlow_ready, t, 2)
                sp.dma_start(stage[:, p, :], dram_tile(d["x1_w"], t)).then_inc(piece_in[p], 16)

            load_piece(0, 0)
            load_piece(1, 1)
            with sp.Fori(1, TILES // 2) as i:
                load_piece(2 * i, 0)
                load_piece(2 * i + 1, 1)
            for p in range(2):
                sp.wait_ge(piece_in[p], 8 * TILES)

        @block.gpsimd
        def _(pool):
            def diagonal_keys(t, p):
                pool.wait_ge(qk_ready, t + 1)
                wait_used(pool, sc_ready, t, 1)
                pool.tensor_tensor(kd[:, :, :], repeat(qk[:, p, 2, :], AG), spread(own[:, :], P), ALU.mult).then_inc(kd_ready, 1)

            def head():
                ln.pool(pool)
                ln.pool_step(pool, 1, 1)
                pool.wait_ge(const_in, 80)
                diagonal_keys(0, 0)

            def step(t, p, has_next):
                if further(t):
                    ln.pool_step(pool, t + 2, p)
                if has_next:
                    diagonal_keys(t + 1, 1 - p)
            over_tiles(pool, head, step)

        @block.scalar
        def _(act):
            def query_key(t, p):
                act.wait_ge(proj_ready, t + 1)
                wait_used(act, sc_ready, t, 2)
                for c in range(3):
                    last = act.activation(qk[:, p, c, :], proj[:, c * P:(c + 1) * P], ACT.Identity,
                                          scale=1.0 / WS, bias=qk_bias[:, c:c + 1])
                last.then_inc(qk_ready, 1)

            def copy_transposed(t):
                act.wait_ge(ptr_ready, t + 1)
                wait_used(act, pv_ready, t, 1)
                act.copy(pt[:, :, :], ptp).then_inc(pt_ready, 1)

            def exponential(t):
                act.wait_ge(s_ready, t + 1)
                wait_used(act, ptr_ready, t, 1)
                wait_used(act, den_ready, t, 1)
                act.activation(e[:, :, :], s[:, :, :], ACT.Exp, scale=AD ** -0.5).then_inc(e_ready, 1)

            def high(t):
                act.wait_ge(ot_ready, t + 1)
                wait_used(act, y_ready, t, 1)
                act.copy(oh[:, :, :].rearrange("p c (b s) -> p b c s", b=2),
                         ot_ps.rearrange("p b (c s) -> p b c s", c=2)).then_inc(oh_ready, 1)

            def head():
                act.wait_ge(const_in, 80)
                ln.high(act, 0, 0, proj_ready)
                query_key(0, 0)

            def step(t, p, has_next):
                if started(t, 1):
                    copy_transposed(t - 1)
                if has_next:
                    ln.high(act, t + 1, 1 - p, proj_ready)
                    query_key(t + 1, 1 - p)
                exponential(t)
                if started(t, 1):
                    high(t - 1)
                act.wait_ge(piece_in[p], (t - p) * 8 + 16)
                act.activation(x1_w[:, 0, at(t), :], stage[:, p, :], ACT.Copy, scale=WS).then_inc(whigh_ready, 1)
            over_tiles(act, head, step)
            copy_transposed(TILES - 1)
            high(TILES - 1)

        @block.vector
        def _(dve):
            ch = Chain(dve, chain, 2, 1, 1)

            def values(t, p):
                dve.wait_ge(qk_ready, t + 1)
                wait_used(dve, pv_ready, t, 2)
                dve.scalar_tensor_tensor(v[:, p, :], proj[:, 3 * P:3 * P + AD], 1.0 / WS, v_bias[:, :],
                                         ALU.mult, ALU.add).then_inc(v_ready, 1)

            def maximum(t):
                dve.wait_ge(sc_ready, t + 1)
                dve.reduce_max(mx[:, :], sc, AX).then_inc(mx_ready, 1)
                dve.wait_ge(mx_ready, t + 1)
                wait_used(dve, e_ready, t, 1)
                dve.tensor_tensor(s[:, :, :], sc, spread(mx[:, :], SEQ), ALU.subtract).then_inc(s_ready, 1)

            def denominator(t):
                dve.wait_ge(e_ready, t + 1)
                wait_used(dve, o_ready, t, 1)
                dve.reduce_sum(den[:, :], e[:, :, :], AX).then_inc(den_ready, 1)
                dve.wait_ge(den_ready, t + 1)
                dve.reciprocal(rden[:, :], den[:, :]).then_inc(rden_ready, 1)

            def divide(t):
                dve.wait_ge(pv_ready, t + 1)
                dve.wait_ge(rden_ready, t + 1)
                wait_used(dve, ot_ready, t, 1)
                dve.tensor_tensor(o_sb[:, :, :].rearrange("p b (k d) -> p b k d", d=AD),
                                  o_ps.rearrange("p b (k d) -> p b k d", d=AD),
                                  rden[:, :].rearrange("p (k b o) -> p b k o", b=2, o=1).to_broadcast([P, 2, AG, AD]),
                                  ALU.mult).then_inc(o_ready, 1)

            def low(t):
                dve.wait_ge(oh_ready, t + 1)
                by_b = lambda a: a[:, :, :].rearrange("p c (b s) -> p b c s", b=2)
                dve.tensor_tensor(by_b(ol), ot_ps.rearrange("p b (c s) -> p b c s", c=2), by_b(oh),
                                  ALU.subtract).then_inc(ol_ready, 1)

            def weights_low(t, p):
                dve.wait_ge(whigh_ready, t + 1)
                dve.scalar_tensor_tensor(x1_w[:, 1, at(t), :], stage[:, p, :], WS, x1_w[:, 0, at(t), :],
                                         ALU.mult, ALU.subtract).then_inc(wlow_ready, 1)

            def add(t):
                dve.wait_ge(y_ready, t + 1)
                x = m.x_all[:, at(t), :]
                dve.scalar_tensor_tensor(x, y, 1.0 / WS, x, ALU.mult, ALU.add).then_inc(y_added, 1)
                dve.wait_ge(y_added, t + 1)
                dve.tensor_tensor(x, x, o_bias[:, :], ALU.add).then_inc(x_done, 1)

            def head():
                ln.stats(dve, ch, 0, 0)
                ln.normalise(dve, 0, 0)
                ln.stats(dve, ch, 1, 1)
                ln.normalise(dve, 1, 1)
                dve.wait_ge(const_in, 80)
                dve.tensor_copy(maskb[:, :], mask[:, :]).then_inc(mask_set, 1)
                ln.low(dve, 0, 0)
                values(0, 0)

            def step(t, p, has_next):
                ch.tile(t)
                if has_next:
                    ln.low(dve, t + 1, 1 - p)
                if started(t, 2):
                    add(t - 2)
                if further(t):
                    ln.stats(dve, ch, t + 2, p)
                if further(t):
                    ln.normalise(dve, t + 2, p)
                maximum(t)
                if started(t, 1):
                    divide(t - 1)
                if has_next:
                    values(t + 1, 1 - p)
                denominator(t)
                if started(t, 1):
                    low(t - 1)
                if started(t, 1):
                    weights_low(t - 1, 1 - p)
            over_tiles(dve, head, step)
            weights_low(TILES - 1, 1)
            divide(TILES - 1)
            low(TILES - 1)
            add(TILES - 2)
            add(TILES - 1)

        @block.tensor
        def _(pe):
            def front(t, p):
                pe.wait_ge(ln.xl_ready, t + 1)
                wait_used(pe, v_ready, t, 1)
                for j in range(3):
                    cols = slice(j * P, (j + 1) * P)
                    for c in range(KC):
                        mm3(pe, proj[:, cols], (wqk[0][:, c, cols], wqk[1][:, c, cols]), ln.operand(p, c),
                            c == 0, c == KC - 1)
                for c in range(KC):
                    last = mm3(pe, proj[:, 3 * P:3 * P + AD], ln.operand(p, c), (wv[0][:, c, :], wv[1][:, c, :]),
                               c == 0, c == KC - 1)
                last.then_inc(proj_ready, 1)

            def scores(t, p):
                pe.wait_ge(kd_ready, t + 1)
                if started(t, 1):
                    pe.wait_ge(pt_ready, t)
                for a in range(2):
                    for c in range(2):
                        rows = slice(c * SEQ, (c + 1) * SEQ)
                        for b in range(2):
                            tok = slice(b * SEQ, (b + 1) * SEQ)
                            out = sc[rows, a * 8 + b:a * 8 + 8:2, :]
                            pe.matmul(out, m.identb[:, rows], repeat(maskb[:, :], 4), start=True, stop=False)
                            last = pe.matmul(out, qk[:, p, c, tok], kd[:, 4 * a:4 * a + 4, tok], start=False, stop=True)
                last.then_inc(sc_ready, 1)

            def transpose(t):
                pe.wait_ge(e_ready, t + 1)
                pe.wait_ge(s_ready, t + 1)
                for k in range(AG):
                    last = pe.transpose(ptp[:, k, :], e[:, 2 * k:2 * k + 2, :].rearrange("p b s -> p (b s)"), m.ident[:, :])
                last.then_inc(ptr_ready, 1)

            def products(t, p):
                pe.wait_ge(pt_ready, t + 1)
                pe.wait_ge(v_ready, t + 1)
                wait_used(pe, o_ready, t, 1)
                for b in range(2):
                    rows = slice(b * SEQ, (b + 1) * SEQ)
                    for k in range(AG):
                        last = pe.matmul(o_ps[:, b, k * AD:(k + 1) * AD], pt[rows, k, :], v[rows, p, :], start=True, stop=True)
                last.then_inc(pv_ready, 1)

            def transpose_o(t):
                pe.wait_ge(o_ready, t + 1)
                wait_used(pe, ol_ready, t, 1)
                for b in range(2):
                    last = pe.transpose(ot_ps[:, b, :], o_sb[:, b, :], m.ident[:, :])
                last.then_inc(ot_ready, 1)

            def output(t):
                pe.wait_ge(ol_ready, t + 1)
                wait_used(pe, x_done, t, 1)
                for c in range(2):
                    last = mm3(pe, y, (oh[:, c, :], ol[:, c, :]), (wo[0][:, c, :], wo[1][:, c, :]), c == 0, c == 1)
                last.then_inc(y_ready, 1)

            def head():
                ln.transpose(pe, 0, 0)
                front(0, 0)
                pe.wait_ge(mask_set, 1)

            def step(t, p, has_next):
                if started(t, 1):
                    transpose(t - 1)
                if has_next:
                    ln.transpose(pe, t + 1, 1 - p)
                if started(t, 2):
                    output(t - 2)
                if has_next:
                    front(t + 1, 1 - p)
                scores(t, p)
                if started(t, 1):
                    products(t - 1, 1 - p)
                    transpose_o(t - 1)
            over_tiles(pe, head, step)
            transpose(TILES - 1)
            output(TILES - 2)
            products(TILES - 1, 1)
            transpose_o(TILES - 1)
            output(TILES - 1)


FF = 704
QMAX, Q_EPS = 127.0, 1e-8
ROUND = 1.5 * 2.0 ** 23


def ffn_quantised(m):
    nc, d = m.nc, m.d
    G1, C2 = 2 * FF // P, -(-FF // P)
    tail = FF - (C2 - 1) * P
    with ExitStack() as ctx:
        sb = lambda n, s, t=F32: ctx.enter_context(nc.sbuf_tensor("f1_" + n, s, t))
        sem = ctx.enter_context(Semaphores(nc, "f1_"))
        ps = ctx.enter_context(nc.psum_tensor("f1_ps", [P, 8, 512], F32))
        w1 = sb("w1", [P, KC, 2 * FF], BF16)
        w2 = sb("w2", [P, C2, DM], BF16)
        s1 = sb("s1", [P, 2 * FF])
        s2 = sb("s2", [P, DM])
        with ExitStack() as c1:
            quantise_weights(m, c1, ps, w1, w2, s1, s2)
        ln = LayerNorm(m, ctx, sem, "f1", ps[:, 0, :])
        stat = sb("stat", [P, 2, 3])
        hstat = sb("hstat", [P, 2, 3])
        xr = sb("xr", [P, DM])
        xq = sb("xq", [P, 2, DM], BF16)
        xt = sb("xt", [P, 2, KC, P], BF16)
        gate = sb("gate", [P, FF])
        up = sb("up", [P, FF])
        sig = sb("sig", [P, FF])
        gate_up = sb("gate_up", [P, FF])
        h = sb("h", [P, FF])
        hr = sb("hr", [P, FF])
        rnd = sb("rnd", [P, 1])
        hq = sb("hq", [P, 2, C2 * P], BF16)
        ht = sb("ht", [P, C2, P], BF16)
        yt = sb("yt", [P, DM])
        chain, zeroed, gup = sem("chain"), sem("zeroed"), sem("gup_ready")
        xq_ready, xtp_ready, xt_ready, gu_ready, gate_ready, up_ready, sig_ready, hq_ready = (
            sem(n) for n in ("xq_ready", "xtp_ready", "xt_ready", "gu_ready", "gate_ready", "up_ready", "sig_ready", "hq_ready"))
        htp_ready, ht_ready, y_ready, yt_ready, x_done = (sem(n) for n in ("htp_ready", "ht_ready", "y_ready", "yt_ready", "x_done"))
        HF = FF // 2
        gate_ps, up_ps = ps[:, 1:3, 0:HF], ps[:, 3:5, 0:HF]
        xt_ps = ps[:, 0, 0:DM // 2].bitcast(BF16)
        ht_ps = ps[:, 5, 0:C2 * P // 2].bitcast(BF16)
        y_ps = lambda p: ps[:, 6 + p, 0:DM]
        halves = lambda a: a.rearrange("p (k n) -> p k n", k=2)
        started = lambda t: not (isinstance(t, int) and t < 1)
        further = lambda t: not (isinstance(t, int) and t + 2 >= TILES)
        rnd_set, xs_ready, xr_ready, hs_ready, hr_ready = (sem(n) for n in ("rnd_set", "xs_ready", "xr_ready", "hs_ready", "hr_ready"))
        x_out = [sem(f"x_out{i}") for i in range(2)]
        block = ctx.enter_context(nc.Block())

        @block.sync
        def _(sp):
            def store(pair, p):
                rows = m.d["out"][pair * 2 * P:(pair + 1) * 2 * P, :] if isinstance(pair, int) else \
                    m.d["out"][bass.ds(pair * 2 * P, 2 * P), :]
                tiles = slice(2 * pair, 2 * pair + 2) if isinstance(pair, int) else bass.ds(pair * 2, 2)
                sp.wait_ge(x_done, 2 * pair + 2)
                sp.dma_start(rows.rearrange("(t p) d -> p t d", p=P), m.x_all[:, tiles, :]).then_inc(x_out[p], 16)

            store(0, 0)
            store(1, 1)
            with sp.Fori(1, TILES // 4) as i:
                store(2 * i, 0)
                store(2 * i + 1, 1)
            for p in range(2):
                sp.wait_ge(x_out[p], 4 * TILES)

        @block.gpsimd
        def _(pool):
            def head():
                ln.pool(pool)
                ln.pool_step(pool, 1, 1)

            def step(t, p, has_next):
                if further(t):
                    ln.pool_step(pool, t + 2, p)
                pool.wait_ge(up_ready, t + 1)
                pool.tensor_tensor(gate_up[:, :], gate[:, :], up[:, :], ALU.mult).then_inc(gup, 1)
            over_tiles(pool, head, step)

        @block.scalar
        def _(act):
            def x_transposed(t, p):
                act.wait_ge(xtp_ready, t + 1)
                wait_used(act, gu_ready, t, 2)
                act.copy(xt[:, p].rearrange("p c s -> p (c s)"), xt_ps).then_inc(xt_ready, 1)

            def h_transposed(t):
                act.wait_ge(htp_ready, t + 1)
                wait_used(act, y_ready, t, 1)
                act.copy(ht[:, :, :].rearrange("p c s -> p (c s)"), ht_ps).then_inc(ht_ready, 1)

            def x_rounded(t, p):
                act.wait_ge(xs_ready, t + 1)
                act.activation(xr[:, :], ln.xn[:, p], ACT.Identity, scale=stat[:, p, 2:3], bias=rnd[:, :]).then_inc(xr_ready, 1)

            def h_rounded(t, p):
                act.wait_ge(hs_ready, t + 1)
                act.activation(hr[:, :], h[:, :], ACT.Identity, scale=hstat[:, p, 2:3], bias=rnd[:, :]).then_inc(hr_ready, 1)

            def head():
                act.wait_ge(rnd_set, 1)
                x_rounded(0, 0)
                x_transposed(0, 0)
                x_rounded(1, 1)
                x_transposed(1, 1)

            def step(t, p, has_next):
                act.wait_ge(gate_ready, t + 1)
                act.activation(sig[:, :], gate[:, :], ACT.Sigmoid).then_inc(sig_ready, 1)
                if further(t):
                    x_rounded(t + 2, p)
                if started(t):
                    h_transposed(t - 1)
                if further(t):
                    x_transposed(t + 2, p)
                h_rounded(t, p)
            over_tiles(act, head, step)
            h_transposed(TILES - 1)

        @block.vector
        def _(dve):
            ch = Chain(dve, chain, 6, 6, 3)

            def scale(v, st):
                ch.link(dve.tensor_reduce(st[:, 0:1], v, AX, ALU.max, apply_absolute_value=True))
                ch.link(dve.tensor_scalar(st[:, 1:2], st[:, 0:1], 1.0 / QMAX, Q_EPS, ALU.mult, ALU.max))
                return dve.reciprocal(st[:, 2:3], st[:, 1:2])

            def scale_x(t, p):
                ln.normalise(dve, t, p)
                dve.wait_ge(ln.xn_ready, t + 1)
                scale(ln.xn[:, p], stat[:, p]).then_inc(xs_ready, 1)

            def quantise_x(t, p):
                dve.wait_ge(xr_ready, t + 1)
                wait_used(dve, xtp_ready, t, 2)
                dve.tensor_scalar(xq[:, p], xr[:, :], -ROUND, None, ALU.add).then_inc(xq_ready, 1)

            def make_h(t, p):
                dve.wait_ge(sig_ready, t + 1)
                dve.wait_ge(gup, t + 1)
                ch.link(dve.tensor_tensor(h[:, :], gate_up[:, :], sig[:, :], ALU.mult))
                scale(h[:, :], hstat[:, p]).then_inc(hs_ready, 1)

            def quantise_h(t, p):
                dve.wait_ge(hr_ready, t + 1)
                wait_used(dve, htp_ready, t, 2)
                dve.tensor_scalar(hq[:, p, 0:FF], hr[:, :], -ROUND, None, ALU.add).then_inc(hq_ready, 1)

            def add(t, p):
                dve.wait_ge(y_ready, t + 1)
                dve.scalar_tensor_tensor(yt[:, :], y_ps(p), hstat[:, p, 1:2], s2[:, :], ALU.mult, ALU.mult).then_inc(yt_ready, 1)
                dve.wait_ge(yt_ready, t + 1)
                x = m.x_all[:, at(t), :]
                dve.tensor_tensor(x, x, yt[:, :], ALU.add).then_inc(x_done, 1)

            def head():
                dve.memset(rnd[:, :], ROUND).then_inc(rnd_set, 1)
                dve.memset(hq[:, :, :].rearrange("p a n -> p (a n)"), 0.0).then_inc(zeroed, 1)
                dve.wait_ge(zeroed, 1)
                for t in range(2):
                    ln.stats(dve, ch, t, t)
                    scale_x(t, t)
                    quantise_x(t, t)

            def step(t, p, has_next):
                ch.tile(t)
                if further(t):
                    ln.stats(dve, ch, t + 2, p)
                dve.wait_ge(gu_ready, t + 1)
                dve.scalar_tensor_tensor(halves(gate[:, :]), gate_ps, stat[:, p, 1:2], halves(s1[:, 0:FF]),
                                         ALU.mult, ALU.mult).then_inc(gate_ready, 1)
                dve.scalar_tensor_tensor(halves(up[:, :]), up_ps, stat[:, p, 1:2], halves(s1[:, FF:]),
                                         ALU.mult, ALU.mult).then_inc(up_ready, 1)
                if started(t):
                    quantise_h(t - 1, 1 - p)
                if further(t):
                    scale_x(t + 2, p)
                make_h(t, p)
                if further(t):
                    quantise_x(t + 2, p)
                if started(t):
                    add(t - 1, 1 - p)
            over_tiles(dve, head, step)
            quantise_h(TILES - 1, 1)
            add(TILES - 1, 1)

        @block.tensor
        def _(pe):
            def x_transpose(t, p):
                pe.wait_ge(xq_ready, t + 1)
                wait_used(pe, xt_ready, t, 1)
                for c in range(KC):
                    last = pe.transpose(xt_ps[:, c * P:(c + 1) * P], xq[:, p, c * P:(c + 1) * P], m.identb[:, :])
                last.then_inc(xtp_ready, 1)

            def gate_and_up(t, p):
                pe.wait_ge(xt_ready, t + 1)
                wait_used(pe, up_ready, t, 1)
                for c in range(KC):
                    for k in range(4):
                        last = pe.matmul(ps[:, 1 + k, 0:HF], xt[:, p, c, :], w1[:, c, k * HF:(k + 1) * HF],
                                         start=c == 0, stop=c == KC - 1)
                last.then_inc(gu_ready, 1)

            def transpose_h(t, p):
                pe.wait_ge(hq_ready, t + 1)
                wait_used(pe, ht_ready, t, 1)
                for c in range(C2):
                    last = pe.transpose(ht_ps[:, c * P:(c + 1) * P], hq[:, p, c * P:(c + 1) * P], m.identb[:, :])
                last.then_inc(htp_ready, 1)

            def down(t, p):
                pe.wait_ge(ht_ready, t + 1)
                wait_used(pe, x_done, t, 2)
                for c in range(C2):
                    k = P if c < C2 - 1 else tail
                    last = pe.matmul(y_ps(p), ht[0:k, c, :], w2[0:k, c, :], start=c == 0, stop=c == C2 - 1)
                last.then_inc(y_ready, 1)

            def head():
                x_transpose(0, 0)
                gate_and_up(0, 0)
                x_transpose(1, 1)

            def step(t, p, has_next):
                if started(t):
                    transpose_h(t - 1, 1 - p)
                if has_next:
                    gate_and_up(t + 1, 1 - p)
                if started(t):
                    down(t - 1, 1 - p)
                if further(t):
                    x_transpose(t + 2, p)
            over_tiles(pe, head, step)
            transpose_h(TILES - 1, 1)
            down(TILES - 1, 1)


def quantise_weights(m, ctx, ps, w1, w2, s1, s2):
    nc, d = m.nc, m.d
    G1, C2 = 2 * FF // P, -(-FF // P)
    sb = lambda n, s, t=F32: ctx.enter_context(nc.sbuf_tensor("fw_" + n, s, t))
    sem = ctx.enter_context(Semaphores(nc, "fw_"))
    wa = sb("wa", [P, G1, DM])
    wb = sb("wb", [P, KC, FF])
    qa = sb("qa", [P, G1, DM], BF16)
    qb = sb("qb", [P, KC, FF], BF16)
    NS = G1 + KC
    st = sb("st", [P, 3, NS])
    diag = sb("diag", [P, NS, P])
    loaded, chain, q_ready, diag_ready = sem("loaded"), sem("chain"), sem("q_ready"), sem("diag_ready")
    t_ready, t_left, r_ready, r_left = sem("t_ready"), sem("t_left"), sem("r_ready"), sem("r_left")
    jobs = [(qa[:, j, c * P:(c + 1) * P], P, w1[:, c, j * P:(j + 1) * P]) for j in range(G1) for c in range(KC)]
    jobs += [(qb[:, j, c * P:min(FF, (c + 1) * P)], min(FF, (c + 1) * P) - c * P, w2[0:min(FF, (c + 1) * P) - c * P, c, j * P:(j + 1) * P])
             for j in range(KC) for c in range(C2)]
    rows = [s1[:, j * P:(j + 1) * P] for j in range(G1)] + [s2[:, j * P:(j + 1) * P] for j in range(KC)]
    block = ctx.enter_context(nc.Block())

    @block.sync
    def _(sp):
        sp.dma_start(wa[:, :, :], d["f1_gu"].rearrange("p (j n) -> p j n", n=DM)).then_inc(loaded, 16)
        sp.dma_start(wb[:, :, :], d["f1_down"].rearrange("p (j n) -> p j n", n=FF)).then_inc(loaded, 16)
        sp.wait_ge(loaded, 32)

    @block.vector
    def _(dve):
        k = [0]

        def link(ins):
            k[0] += 1
            ins.then_inc(chain, 1)
            dve.wait_ge(chain, k[0])

        dve.wait_ge(loaded, 32)
        dve.tensor_reduce(st[:, 0, 0:G1], wa[:, :, :], AX, ALU.max, apply_absolute_value=True)
        link(dve.tensor_reduce(st[:, 0, G1:], wb[:, :, :], AX, ALU.max, apply_absolute_value=True))
        link(dve.tensor_scalar(st[:, 1, :], st[:, 0, :], 1.0 / QMAX, Q_EPS, ALU.mult, ALU.max))
        link(dve.reciprocal(st[:, 2, :], st[:, 1, :]))
        for j in range(G1):
            dve.tensor_scalar(wa[:, j, :], wa[:, j, :], st[:, 2, j:j + 1], ROUND, ALU.mult, ALU.add)
        for j in range(KC):
            last = dve.tensor_scalar(wb[:, j, :], wb[:, j, :], st[:, 2, G1 + j:G1 + j + 1], ROUND, ALU.mult, ALU.add)
        link(last)
        dve.tensor_scalar(qa[:, :, :], wa[:, :, :], -ROUND, None, ALU.add)
        dve.tensor_scalar(qb[:, :, :], wb[:, :, :], -ROUND, None, ALU.add).then_inc(q_ready, 1)
        dve.tensor_tensor(diag[:, :, :], repeat(m.ident[:, :], NS), spread(st[:, 1, :], P), ALU.mult).then_inc(diag_ready, 1)
        for i, (_, n, dst) in enumerate(jobs):
            dve.wait_ge(t_ready, i + 1)
            dve.tensor_copy(dst, ps[0:n, i % 4, 0:P // 2].bitcast(BF16)).then_inc(t_left, 1)

    @block.scalar
    def _(act):
        for i, dst in enumerate(rows):
            act.wait_ge(r_ready, i + 1)
            act.copy(dst, ps[:, 4 + i % 4, 0:P]).then_inc(r_left, 1)

    @block.tensor
    def _(pe):
        pe.wait_ge(q_ready, 1)
        for i, (src, n, _) in enumerate(jobs):
            if i >= 4:
                pe.wait_ge(t_left, i - 3)
            pe.transpose(ps[0:n, i % 4, 0:P // 2].bitcast(BF16), src, m.identb[:, :]).then_inc(t_ready, 1)
        pe.wait_ge(diag_ready, 1)
        for i in range(NS):
            if i >= 4:
                pe.wait_ge(r_left, i - 3)
            pe.matmul(ps[:, 4 + i % 4, 0:P], m.ones[:, :], diag[:, i, :], start=True, stop=True).then_inc(r_ready, 1)


def layer1_attentions(m):
    with m.nc.sbuf_tensor("x1_w", [P, 2, TILES, X1_PIECE], F16) as x1_w:
        attention_mqa(m, x1_w)
        attention_cross(m, x1_w)


BUILDERS = (attention_gqa, attention_features, ffn_lora, layer1_attentions, ffn_quantised)


def decoder_kernel(nc, d):
    with ExitStack() as ctx:
        m = Machine(nc, ctx, d)
        load_resident(m)
        for build in BUILDERS:
            build(m)


def host_layout(i):
    f = lambda a: np.ascontiguousarray(a)
    a = {k: np.asarray(v) for k, v in i.items()}
    kmajor = lambda w: f(w.reshape(KC, P, -1).transpose(1, 0, 2).reshape(P, -1))
    out = {"x": f(a["x"].reshape(-1, DM)), "ident": np.eye(P, dtype=np.float32)}
    out["ffn0_base"] = kmajor(a["L0_ffn_W_base"].T)
    out["ffn0_a"] = kmajor(np.concatenate([a["L0_ffn_A"].reshape(-1, DM).T, a["L0_ffn_router_W"].T], 1))
    out["ffn0_b"] = f(a["L0_ffn_Bw"].transpose(0, 2, 1).reshape(P, DM))
    out["ffn0_bias"] = f(a["L0_ffn_b_base"].reshape(1, DM))
    out["desc"] = np.broadcast_to(np.arange(EXPERTS, 0, -1, dtype=np.float32), (P, EXPERTS)).copy()
    qkv = a["L0_attn_w_qkv"]
    nq, nk = HEADS * HD, KV * HD
    swap = lambda v, axis=0: np.concatenate(np.split(v, 2, axis)[::-1], axis)
    wk = qkv[nq:nq + nk]
    out["a0_q"] = kmajor(qkv[:nq].T)
    out["a0_k"] = kmajor(wk.T)
    out["a0_v"] = kmajor(qkv[nq + nk:].T)
    out["a0_o"] = f(a["L0_attn_w_o"].T.reshape(HEADS, HD, DM).transpose(1, 0, 2).reshape(P, -1))
    qg, qb, kg, kb = (a["L0_attn_" + n] for n in ("qn_g", "qn_b", "kn_g", "kn_b"))
    out["a0_gb"] = f(np.stack([qg, qb, swap(qb), swap(qg), kg, kb, swap(kb), swap(kg)], 1))
    inv = (1.0 / np.float32(1e6) ** (np.arange(0, HD, 2, dtype=np.float32) / np.float32(HD))).astype(np.float32)
    ang = np.concatenate([inv, inv])[:, None] * np.arange(SEQ, dtype=np.float32)[None]
    sgn = np.where(np.arange(HD) < HD // 2, -1.0, 1.0)[:, None]
    out["rope"] = np.stack([np.cos(ang), sgn * np.sin(ang)], 1).astype(np.float32)
    out["causal"] = np.tile(np.triu(np.full((SEQ, SEQ), NEG), 1), (2, 1)).astype(np.float32)
    x1 = {n: a["L1_xattn_" + n] for n in ("q_w", "ki_w", "vi_w", "o_w", "q_b", "ki_b", "vi_b", "o_b", "nq_s", "nki_s")}
    wo = f(x1["o_w"].reshape(HEADS, HD, DM).transpose(1, 0, 2).reshape(P, -1))
    w = np.concatenate([kmajor(x1["q_w"]), kmajor(x1["ki_w"]), kmajor(x1["vi_w"]), wo], 1)
    out["x1_w"] = f(w.reshape(P, TILES, X1_PIECE).transpose(1, 0, 2))
    for n, k in (("bq", "q_b"), ("bk", "ki_b"), ("bo", "o_b")):
        out["x1_" + n] = f(x1[k].reshape(1, -1))
    out["x1_bv"] = f(x1["vi_b"].reshape(HEADS, HD).T)
    out["x1_scales"] = f(np.stack([x1["nq_s"].reshape(HEADS, HD).T, x1["nki_s"].reshape(HEADS, HD).T], 1))
    c = a["ctx_2048"].reshape(-1, P, DM)
    out["ctx_t"] = f(c.transpose(0, 2, 1).reshape(-1, KC, P, P).transpose(0, 2, 1, 3).reshape(-1, P, DM))
    out["ctx"] = f(c)
    v = c.transpose(0, 2, 1).reshape(-1, KC, P, XU, XT).transpose(0, 2, 1, 3, 4)
    out["ctx_v"] = f(np.concatenate([v, np.ones_like(v[..., :1])], -1).reshape(-1, P, KC * XU * VC))
    sel = np.zeros((P, 4, XG, 4, 32), np.float32)
    one = np.zeros((4, 32, 1), np.float32)
    one[:, 3 * XT] = 1.0
    for tok in range(P):
        g, jj, i = tok // 32, tok % 32 // XT, tok % XT
        for part, thirds in enumerate(((0, 1), (2,), (0, 2), (1,))):
            for r in thirds:
                sel[tok, part, g, jj, r * XT + i] = 1.0
    gather = np.zeros((4, 32, 2, 4, XT), np.float32)
    for jj in range(4):
        gather[jj, np.arange(XT), 0, jj, np.arange(XT)] = 1.0
        gather[jj, XT, 1, jj] = 1.0
    out["x0_gather"] = gather.reshape(P, 2, 32)
    out["x0_sel"] = sel.reshape(P, 4, XG * P)
    out["x0_one"] = one.reshape(P, 1)
    w1 = a["L1_attn_Wqkv_w"]
    bias = a["L1_attn_Wqkv_b"]
    wk = np.tile(w1[DM:DM + AD], (AG, 1))
    out["a1_qk"] = kmajor(np.concatenate([w1[:DM], wk], 0).T)
    out["a1_v"] = kmajor(w1[DM + AD:].T)
    out["a1_o"] = kmajor(a["L1_attn_out_w"].T)
    out["a1_bqk"] = f(np.concatenate([bias[:DM], np.tile(bias[DM:DM + AD], AG)]).reshape(3, P).T)
    out["a1_bv"] = f(bias[DM + AD:].reshape(1, AD))
    out["a1_bo"] = f(a["L1_attn_out_b"].reshape(1, DM))
    out["a1_own"] = np.kron(np.eye(AG), np.ones((AD, 1))).astype(np.float32)
    rows = lambda w: f(w.reshape(-1, P, w.shape[1]).transpose(1, 0, 2).reshape(P, -1))
    out["f1_gu"] = rows(a["L1_ffn_w_gate_up"])
    out["f1_down"] = rows(a["L1_ffn_w_down"])
    return out


def kernel(**inputs):
    import concourse.bacc as _bacc
    from concourse.bass_utils import run_bass_kernel_spmd as _run

    nc = _bacc.Bacc("TRN2", target_bir_lowering=False, num_devices=1)
    arrays, d = {}, {}
    for name, a in host_layout(inputs).items():
        arrays[f"in_{name}"] = a
        d[name] = nc.dram_tensor(f"in_{name}", a.shape, F32, kind="ExternalInput").ap()
    d["out"] = nc.dram_tensor("out_x", (64 * SEQ, DM), F32, kind="ExternalOutput").ap()
    decoder_kernel(nc, d)
    r = _run(nc, [arrays], core_ids=[0])
    return r.results[0]["out_x"].reshape(64, SEQ, DM)
```
